# Optimizing a Trainium2 kernel written in Bass

```python
import numpy as np
import jax
import jax.numpy as jnp

def _softmax(x, axis=-1):
    return jax.nn.softmax(x, axis=axis)

def _gelu(x):
    return jax.nn.gelu(x, approximate=True)

def _silu(x):
    return jax.nn.silu(x)

def _sigmoid(x):
    return jax.nn.sigmoid(x)

def _layernorm(x, axis=-1, eps=1e-05):
    m = jnp.mean(x, axis=axis, keepdims=True)
    v = jnp.var(x, axis=axis, keepdims=True)
    return (x - m) / jnp.sqrt(v + eps)

def _scatter_add(tgt, idx, src, axis=0):
    return tgt.at[idx].add(src)

def _segment_sum(src, seg, n):
    return jax.ops.segment_sum(src, seg, n)
kernel_name = 'mk_decoder_postln_d1_seqx_r4_a9bda2'

def setup_inputs(seed: int=0):
    np.random.seed(seed)
    _w = jnp.asarray

    def _rec_inputs():
        import jax
        import jax.numpy as jnp
        _rk = jax.random.key(seed)
        x = -0.0005207 + 1.001 * jax.random.normal(jax.random.fold_in(_rk, 1), (8, 256, 256), jnp.float32)
        _lenS = 256 - jax.random.randint(jax.random.fold_in(_rk, 7), (8,), 0, max(1, 256 // 4) + 1, jnp.int32)
        _lenS2 = 256 - jax.random.randint(jax.random.fold_in(_rk, 8), (8,), 0, max(1, 256 // 4) + 1, jnp.int32)
        _ctx_1024P = jax.random.normal(jax.random.fold_in(_rk, 11), (8, 16, 256), jnp.float32)
        _ctx_1024c = jax.random.dirichlet(jax.random.fold_in(_rk, 511), 0.3 * jnp.ones((16,), jnp.float32), (8, 256))
        _ctx_1024t = jnp.einsum('bsk,bkd->bsd', _ctx_1024c, _ctx_1024P)
        _ctx_1024t = _ctx_1024t * jax.lax.rsqrt(jnp.mean(jnp.square(_ctx_1024t)) + 1e-12) * 0.953939
        ctx_1024 = -0.000514642 + 1.00011 * (_ctx_1024t + 0.3 * jax.random.normal(jax.random.fold_in(_rk, 611), (8, 256, 256), jnp.float32))
        return (x, ctx_1024)
    x, ctx_1024 = _rec_inputs()

    def _L0_attn_setup():
        import jax, jax.numpy as jnp
        import numpy as np
        N_LAYERS = 2
        D_MODEL = 256
        D_INNER = 2 * D_MODEL
        D_STATE = 16
        D_CONV = 4
        DT_RANK = D_MODEL // 16
        B_SZ, L = (1, 512)
        EPS = 1e-05

        def layernorm(x, w, b):
            mu = jnp.mean(x, axis=-1, keepdims=True)
            var = jnp.mean(jnp.square(x - mu), axis=-1, keepdims=True)
            return (x - mu) * jax.lax.rsqrt(var + EPS) * w + b

        def mamba(x, in_w, cw, cb, xp_w, dtp_w, dtp_b, A_log, Dp, out_w):
            Bn, Ln, _ = x.shape
            xz = jnp.einsum('bld,ed->ble', x, in_w)
            xc, z = jnp.split(xz, 2, axis=-1)
            xp = jnp.pad(xc, ((0, 0), (D_CONV - 1, 0), (0, 0)))
            xc = sum((xp[:, k:k + Ln, :] * cw[:, k] for k in range(D_CONV))) + cb
            xc = jax.nn.silu(xc)
            dbl = jnp.einsum('ble,re->blr', xc, xp_w)
            dt, Bm, Cm = jnp.split(dbl, [DT_RANK, DT_RANK + D_STATE], axis=-1)
            dt = jax.nn.softplus(jnp.einsum('blr,er->ble', dt, dtp_w) + dtp_b)
            A = -jnp.exp(A_log)
            dA = jnp.exp(dt[..., None] * A)
            dBu = (dt * xc)[..., None] * Bm[:, :, None, :]

            def step(h, inp):
                dA_t, dBu_t, C_t = inp
                h = dA_t * h + dBu_t
                y = jnp.einsum('ben,bn->be', h, C_t)
                return (h, y)
            h0 = jnp.zeros((Bn, D_INNER, D_STATE), dA.dtype)
            _, ys = jax.lax.scan(step, h0, (dA.transpose(1, 0, 2, 3), dBu.transpose(1, 0, 2, 3), Cm.transpose(1, 0, 2)))
            y = ys.transpose(1, 0, 2) + xc * Dp
            y = y * jax.nn.silu(z)
            return jnp.einsum('ble,de->bld', y, out_w)
        key = jax.random.key(seed)
        ks = jax.random.split(key, 12)
        s = 0.02
        dt_init = np.log(np.expm1(0.01)).astype(np.float32)
        A_row = jnp.log(jnp.arange(1, D_STATE + 1, dtype=jnp.float32))
        return {'x': jax.random.normal(ks[0], (B_SZ, L, D_MODEL), jnp.float32), 'ln_w': jnp.ones((N_LAYERS, D_MODEL), jnp.float32), 'ln_b': jnp.zeros((N_LAYERS, D_MODEL), jnp.float32), 'in_proj_w': jax.random.normal(ks[1], (N_LAYERS, 2 * D_INNER, D_MODEL)) * s, 'conv_w': jax.random.normal(ks[2], (N_LAYERS, D_INNER, D_CONV)) * 0.2, 'conv_b': jnp.zeros((N_LAYERS, D_INNER), jnp.float32), 'x_proj_w': jax.random.normal(ks[3], (N_LAYERS, DT_RANK + 2 * D_STATE, D_INNER)) * s, 'dt_proj_w': jax.random.normal(ks[4], (N_LAYERS, D_INNER, DT_RANK)) * DT_RANK ** (-0.5), 'dt_proj_b': jnp.full((N_LAYERS, D_INNER), dt_init), 'A_log': jnp.broadcast_to(A_row, (N_LAYERS, D_INNER, D_STATE)).copy(), 'D_skip': jnp.ones((N_LAYERS, D_INNER), jnp.float32), 'out_proj_w': jax.random.normal(ks[5], (N_LAYERS, D_MODEL, D_INNER)) * s, 'norm_f_w': jnp.ones((D_MODEL,), jnp.float32), 'norm_f_b': jnp.zeros((D_MODEL,), jnp.float32)}
    _L0_attn_all = _L0_attn_setup()
    _L0_attn_in = {k: v for k, v in _L0_attn_all.items() if k in ('ln_w', 'ln_b', 'in_proj_w', 'conv_w', 'conv_b', 'x_proj_w', 'dt_proj_w', 'dt_proj_b', 'A_log', 'D_skip', 'out_proj_w', 'norm_f_w', 'norm_f_b')}
    del _L0_attn_all

    def _L0_xattn_setup():
        import jax, jax.numpy as jnp
        import numpy as np
        E = 256
        QH = 16
        KVH = 4
        HD = E // QH
        KVE = HD * KVH
        EPS = 1e-05
        ROPE_BASE = 10000.0

        def rope(x, d):
            b = x.shape[0]
            theta = 1.0 / ROPE_BASE ** (jnp.arange(0, d, 2, dtype=jnp.float32) / d)
            seq_idx = jnp.arange(b, dtype=jnp.float32)
            idx_theta = seq_idx[:, None] * theta[None, :]
            idx2 = jnp.concatenate([idx_theta, idx_theta], axis=-1)
            cos = jnp.cos(idx2)[:, None, :, None]
            sin = jnp.sin(idx2)[:, None, :, None]
            d2 = d // 2
            neg = jnp.concatenate([-x[..., d2:], x[..., :d2]], axis=-1)
            return x * cos + x * sin * neg
        key = jax.random.key(seed)
        ks = jax.random.split(key, 12)
        b, n = (1, 512)

        def xavier(k, shape):
            fan_out, fan_in = shape
            std = (2.0 / (fan_in + fan_out)) ** 0.5
            return jax.random.normal(k, shape, dtype=jnp.float32) * std
        return {'query': jax.random.normal(ks[0], (b, n, E), dtype=jnp.float32), 'key': jax.random.normal(ks[1], (b, n, E), dtype=jnp.float32), 'value': jax.random.normal(ks[2], (b, n, E), dtype=jnp.float32), 'Wq': xavier(ks[3], (E, E)), 'bq': jnp.zeros((E,), jnp.float32), 'Wk': xavier(ks[4], (KVE, E)), 'bk': jnp.zeros((KVE,), jnp.float32), 'Wv': xavier(ks[5], (KVE, E)), 'bv': jnp.zeros((KVE,), jnp.float32), 'gamma': jnp.ones((E,), jnp.float32), 'beta': jnp.zeros((E,), jnp.float32)}
    _L0_xattn_all = _L0_xattn_setup()
    _L0_xattn_in = {k: v for k, v in _L0_xattn_all.items() if k in ('Wq', 'bq', 'Wk', 'bk', 'Wv', 'bv', 'gamma', 'beta')}
    del _L0_xattn_all

    def _L0_ffn_setup():
        import jax, jax.numpy as jnp
        import numpy as np
        B, S, D, E, H, K = (4, 512, 256, 8, 256, 2)
        CAPACITY_FACTOR = 1.25
        MIN_CAPACITY = 4
        key = jax.random.key(seed)
        ks = jax.random.split(key, 5)
        return {'inputs': jax.random.normal(ks[0], (B, S, D), jnp.float32), 'router_w': jax.random.normal(ks[1], (D, E), jnp.float32) / np.sqrt(D), 'router_b': jnp.zeros((E,), jnp.float32), 'w1': jax.random.normal(ks[2], (E, D, H), jnp.float32) / np.sqrt(D), 'b1': jnp.zeros((E, H), jnp.float32), 'w2': jax.random.normal(ks[3], (E, H, D), jnp.float32) / np.sqrt(H), 'b2': jnp.zeros((E, D), jnp.float32)}
    _L0_ffn_all = _L0_ffn_setup()
    _L0_ffn_in = {k: v for k, v in _L0_ffn_all.items() if k in ('router_w', 'router_b', 'w1', 'b1', 'w2', 'b2')}
    del _L0_ffn_all
    return {'x': x, 'ctx_1024': ctx_1024, 'L0_attn_ln_w': _L0_attn_in['ln_w'], 'L0_attn_ln_b': _L0_attn_in['ln_b'], 'L0_attn_in_proj_w': _L0_attn_in['in_proj_w'], 'L0_attn_conv_w': _L0_attn_in['conv_w'], 'L0_attn_conv_b': _L0_attn_in['conv_b'], 'L0_attn_x_proj_w': _L0_attn_in['x_proj_w'], 'L0_attn_dt_proj_w': _L0_attn_in['dt_proj_w'], 'L0_attn_dt_proj_b': _L0_attn_in['dt_proj_b'], 'L0_attn_A_log': _L0_attn_in['A_log'], 'L0_attn_D_skip': _L0_attn_in['D_skip'], 'L0_attn_out_proj_w': _L0_attn_in['out_proj_w'], 'L0_attn_norm_f_w': _L0_attn_in['norm_f_w'], 'L0_attn_norm_f_b': _L0_attn_in['norm_f_b'], 'L0_xattn_Wq': _L0_xattn_in['Wq'], 'L0_xattn_bq': _L0_xattn_in['bq'], 'L0_xattn_Wk': _L0_xattn_in['Wk'], 'L0_xattn_bk': _L0_xattn_in['bk'], 'L0_xattn_Wv': _L0_xattn_in['Wv'], 'L0_xattn_bv': _L0_xattn_in['bv'], 'L0_xattn_gamma': _L0_xattn_in['gamma'], 'L0_xattn_beta': _L0_xattn_in['beta'], 'L0_ffn_router_w': _L0_ffn_in['router_w'], 'L0_ffn_router_b': _L0_ffn_in['router_b'], 'L0_ffn_w1': _L0_ffn_in['w1'], 'L0_ffn_b1': _L0_ffn_in['b1'], 'L0_ffn_w2': _L0_ffn_in['w2'], 'L0_ffn_b2': _L0_ffn_in['b2']}

def reference(x, ctx_1024, L0_attn_ln_w, L0_attn_ln_b, L0_attn_in_proj_w, L0_attn_conv_w, L0_attn_conv_b, L0_attn_x_proj_w, L0_attn_dt_proj_w, L0_attn_dt_proj_b, L0_attn_A_log, L0_attn_D_skip, L0_attn_out_proj_w, L0_attn_norm_f_w, L0_attn_norm_f_b, L0_xattn_Wq, L0_xattn_bq, L0_xattn_Wk, L0_xattn_bk, L0_xattn_Wv, L0_xattn_bv, L0_xattn_gamma, L0_xattn_beta, L0_ffn_router_w, L0_ffn_router_b, L0_ffn_w1, L0_ffn_b1, L0_ffn_w2, L0_ffn_b2):
    import jax
    import jax.numpy as jnp

    def _L0_attn_ref(x, ln_w, ln_b, in_proj_w, conv_w, conv_b, x_proj_w, dt_proj_w, dt_proj_b, A_log, D_skip, out_proj_w, norm_f_w, norm_f_b):
        import jax, jax.numpy as jnp
        import numpy as np
        N_LAYERS = 2
        D_MODEL = 256
        D_INNER = 2 * D_MODEL
        D_STATE = 16
        D_CONV = 4
        DT_RANK = D_MODEL // 16
        B_SZ, L = (1, 512)
        EPS = 1e-05

        def layernorm(x, w, b):
            mu = jnp.mean(x, axis=-1, keepdims=True)
            var = jnp.mean(jnp.square(x - mu), axis=-1, keepdims=True)
            return (x - mu) * jax.lax.rsqrt(var + EPS) * w + b

        def mamba(x, in_w, cw, cb, xp_w, dtp_w, dtp_b, A_log, Dp, out_w):
            Bn, Ln, _ = x.shape
            xz = jnp.einsum('bld,ed->ble', x, in_w)
            xc, z = jnp.split(xz, 2, axis=-1)
            xp = jnp.pad(xc, ((0, 0), (D_CONV - 1, 0), (0, 0)))
            xc = sum((xp[:, k:k + Ln, :] * cw[:, k] for k in range(D_CONV))) + cb
            xc = jax.nn.silu(xc)
            dbl = jnp.einsum('ble,re->blr', xc, xp_w)
            dt, Bm, Cm = jnp.split(dbl, [DT_RANK, DT_RANK + D_STATE], axis=-1)
            dt = jax.nn.softplus(jnp.einsum('blr,er->ble', dt, dtp_w) + dtp_b)
            A = -jnp.exp(A_log)
            dA = jnp.exp(dt[..., None] * A)
            dBu = (dt * xc)[..., None] * Bm[:, :, None, :]

            def step(h, inp):
                dA_t, dBu_t, C_t = inp
                h = dA_t * h + dBu_t
                y = jnp.einsum('ben,bn->be', h, C_t)
                return (h, y)
            h0 = jnp.zeros((Bn, D_INNER, D_STATE), dA.dtype)
            _, ys = jax.lax.scan(step, h0, (dA.transpose(1, 0, 2, 3), dBu.transpose(1, 0, 2, 3), Cm.transpose(1, 0, 2)))
            y = ys.transpose(1, 0, 2) + xc * Dp
            y = y * jax.nn.silu(z)
            return jnp.einsum('ble,de->bld', y, out_w)
        for i in range(N_LAYERS):
            h = layernorm(x, ln_w[i], ln_b[i])
            h = mamba(h, in_proj_w[i], conv_w[i], conv_b[i], x_proj_w[i], dt_proj_w[i], dt_proj_b[i], A_log[i], D_skip[i], out_proj_w[i])
            x = h + x
        return layernorm(x, norm_f_w, norm_f_b)

    def _L0_xattn_ref(query, key, value, Wq, bq, Wk, bk, Wv, bv, gamma, beta):
        import jax, jax.numpy as jnp
        import numpy as np
        E = 256
        QH = 16
        KVH = 4
        HD = E // QH
        KVE = HD * KVH
        EPS = 1e-05
        ROPE_BASE = 10000.0

        def rope(x, d):
            b = x.shape[0]
            theta = 1.0 / ROPE_BASE ** (jnp.arange(0, d, 2, dtype=jnp.float32) / d)
            seq_idx = jnp.arange(b, dtype=jnp.float32)
            idx_theta = seq_idx[:, None] * theta[None, :]
            idx2 = jnp.concatenate([idx_theta, idx_theta], axis=-1)
            cos = jnp.cos(idx2)[:, None, :, None]
            sin = jnp.sin(idx2)[:, None, :, None]
            d2 = d // 2
            neg = jnp.concatenate([-x[..., d2:], x[..., :d2]], axis=-1)
            return x * cos + x * sin * neg
        b, n, _ = query.shape
        q = query @ Wq.T + bq
        k = key @ Wk.T + bk
        v = value @ Wv.T + bv
        q = q.reshape(b, n, QH, HD)
        k = k.reshape(b, n, KVH, HD)
        v = v.reshape(b, n, KVH, HD)
        q = rope(q, QH)
        k = rope(k, KVH)
        q = jnp.transpose(q, (0, 2, 1, 3))
        k = jnp.transpose(k, (0, 2, 1, 3))
        v = jnp.transpose(v, (0, 2, 1, 3))
        scale = float(HD) ** 0.5
        q = q / scale
        g = QH // KVH
        q = q.reshape(b, KVH, g, n, HD)
        q = jnp.transpose(q, (0, 2, 1, 3, 4))
        sim = jnp.einsum('bghnd,bhsd->bghns', q, k)
        attn = jax.nn.softmax(sim, axis=-1)
        out = jnp.einsum('bghns,bhsd->bghnd', attn, v)
        out = jnp.transpose(out, (0, 3, 2, 1, 4))
        x = out.reshape(b, n, QH * HD)
        mu = jnp.mean(x, axis=-1, keepdims=True)
        var = jnp.mean((x - mu) ** 2, axis=-1, keepdims=True)
        x = (x - mu) * jax.lax.rsqrt(var + EPS) * gamma + beta
        return x

    def _L0_ffn_ref(inputs, router_w, router_b, w1, b1, w2, b2):
        import jax, jax.numpy as jnp
        import numpy as np
        B, S, D, E, H, K = (4, 512, 256, 8, 256, 2)
        CAPACITY_FACTOR = 1.25
        MIN_CAPACITY = 4
        b, s, d = inputs.shape
        n = b * s
        flat = inputs.reshape(n, d)
        logits = flat @ router_w + router_b
        probs = jax.nn.softmax(logits, axis=-1)
        top_p, top_i = jax.lax.top_k(probs, K)
        top_p = top_p / jnp.sum(top_p, axis=-1, keepdims=True)
        expert_capacity = max(int(n * CAPACITY_FACTOR / E), MIN_CAPACITY)
        rows = jnp.arange(n)[:, None]
        mask = jnp.zeros((n, E), inputs.dtype).at[rows, top_i].set(top_p)
        mask = mask.at[top_i, jnp.arange(K)[None, :]].add(top_p)
        mask = jnp.minimum(mask, expert_capacity)
        xin = mask[:, :, None] * flat[:, None, :]
        h = jax.nn.gelu(jnp.einsum('ned,edh->neh', xin, w1) + b1, approximate=False)
        out = jnp.einsum('neh,ehd->ned', h, w2) + b2
        final = jnp.einsum('ne,ned->nd', mask, out)
        return final.reshape(b, s, d)
    x = _layernorm(x + _L0_attn_ref(x, L0_attn_ln_w, L0_attn_ln_b, L0_attn_in_proj_w, L0_attn_conv_w, L0_attn_conv_b, L0_attn_x_proj_w, L0_attn_dt_proj_w, L0_attn_dt_proj_b, L0_attn_A_log, L0_attn_D_skip, L0_attn_out_proj_w, L0_attn_norm_f_w, L0_attn_norm_f_b), axis=-1)
    x = _layernorm(x + _L0_xattn_ref(x, ctx_1024, ctx_1024, L0_xattn_Wq, L0_xattn_bq, L0_xattn_Wk, L0_xattn_bk, L0_xattn_Wv, L0_xattn_bv, L0_xattn_gamma, L0_xattn_beta), axis=-1)
    x = _layernorm(x + _L0_ffn_ref(x, L0_ffn_router_w, L0_ffn_router_b, L0_ffn_w1, L0_ffn_b1, L0_ffn_w2, L0_ffn_b2), axis=-1)
    return x

_drawn_inputs = setup_inputs


def setup_inputs(seed=0):
    import zlib

    import numpy as np

    out = dict(_drawn_inputs(seed))
    spreads = {'L0_attn_ln_w': (1.0, 0.6),
     'L0_attn_ln_b': (0.0, 0.8),
     'L0_attn_conv_b': (0.0, 0.8),
     'L0_attn_dt_proj_b': (-4.600165843963623, 0.6),
     'L0_attn_D_skip': (1.0, 0.6),
     'L0_attn_norm_f_w': (1.0, 0.2),
     'L0_attn_norm_f_b': (0.0, 0.1),
     'L0_xattn_bq': (0.0, 0.1),
     'L0_xattn_bk': (0.0, 0.1),
     'L0_xattn_bv': (0.0, 0.1),
     'L0_xattn_gamma': (1.0, 0.2),
     'L0_xattn_beta': (0.0, 0.1),
     'L0_ffn_router_b': (0.0, 0.1),
     'L0_ffn_b1': (0.0, 0.1),
     'L0_ffn_b2': (0.0, 0.1)}
    factors = {'L0_attn_in_proj_w': 6.063,
     'L0_attn_conv_w': 6.559,
     'L0_attn_x_proj_w': 8.0,
     'L0_attn_dt_proj_w': 8.0,
     'L0_attn_A_log': 8.0,
     'L0_attn_out_proj_w': 5.564}
    for name, (base, spread) in spreads.items():
        noise = np.random.default_rng([zlib.crc32(name.encode()), seed]).standard_normal(out[name].shape)
        drawn = base * np.exp(spread * noise) if base else spread * noise
        out[name] = jnp.asarray(drawn.astype(out[name].dtype))
    for name, factor in factors.items():
        out[name] = (out[name] * factor).astype(out[name].dtype)
    return out
```

```python
import concourse.bass as bass
from concourse import mybir
from contextlib import ExitStack

P = 128
BATCH, SEQ, DM = 8, 256, 256
TOK = BATCH * SEQ
TILES = TOK // P
KD = DM // P
LAYERS, DI, DS, RANK, TAPS = 2, 512, 16, 16, 4
M = DI // P
SB = 2
SEG = SB * SEQ
SEGS = BATCH // SB
ST = SEG // P
PAD = TAPS - 1
XPR = 3 * 2 * DS + RANK
EPS = 1e-5


def build(nc, A):
    fp32, bf16 = mybir.dt.float32, mybir.dt.bfloat16
    ALU, ACT, AX = mybir.AluOpType, mybir.ActivationFunctionType, mybir.AxisListType
    outer = ExitStack()
    with outer:
        x = outer.enter_context(nc.sbuf_tensor("x", [P, TILES, DM], fp32))
        ident = outer.enter_context(nc.sbuf_tensor("ident", [P, P], fp32))
        mamba(nc, A, x, ident)
        blend(nc, A, x, "norm_f", "x", None)
        attention(nc, A, x, ident)
        moe(nc, A, x, ident)


def mamba(nc, A, x, ident):
    fp32, bf16 = mybir.dt.float32, mybir.dt.bfloat16
    ALU, ACT, AX = mybir.AluOpType, mybir.ActivationFunctionType, mybir.AxisListType
    ctx = ExitStack()
    with ctx:
        def sb(name, shape, dt=fp32):
            return ctx.enter_context(nc.sbuf_tensor(name, shape, dt))

        def pb(name, shape):
            return ctx.enter_context(nc.psum_tensor(name, shape, fp32))

        def sem(name):
            return ctx.enter_context(nc.semaphore(name))

        pick = sb("pick", [96, 2 * DS, P], bf16)
        inw = [sb(f"inw{l}", [P, KD, 2 * DI]) for l in range(LAYERS)]
        xpw = [sb(f"xpw{l}", [P, M, XPR]) for l in range(LAYERS)]
        dtw = [sb(f"dtw{l}", [P, DI]) for l in range(LAYERS)]
        outw = [sb(f"outw{l}", [P, M, DM]) for l in range(LAYERS)]
        lnw = sb("lnw", [P, LAYERS, 2, KD])
        chan = sb("chan", [P, LAYERS, 3 + TAPS, M])
        alog = sb("alog", [P, LAYERS, M, DS])
        nega = sb("nega", [P, LAYERS, M, DS])
        stats = sb("stats", [P, ST, 6])
        mv = sb("mv", [P, ST, 2])
        vare = sb("vare", [P, ST])
        rstd = sb("rstd", [P, ST])
        xn = sb("xn", [P, ST, DM])
        hT = sb("hT", [P, KD, SEG])
        xp = sb("xp", [P, M, SB, PAD + SEQ])
        cv = sb("cv", [P, M, SEG])
        zs = sb("zs", [P, M, SEG])
        xc = sb("xc", [P, M, SEG])
        bc = sb("bc", [96, SEG], bf16)
        bcr = sb("bcr", [64, SEG])
        dr = sb("dr", [P, SEG])
        dt = sb("dt", [P, M, SEG])
        du = sb("du", [P, M, SEG])
        soft = sb("soft", [P, M, SEG])
        brow = sb("brow", [P, 2, SEG])
        dA = sb("dA", [P, 2, M, SEG])
        dBu = sb("dBu", [P, 2, M, SEG])
        h = sb("h", [P, M, SEG])
        hC = sb("hC", [P, 2, M, SEG])
        yz = cv
        Y = pb("Y", [P, M, SEG])
        Bp = pb("Bp", [P, SEG])
        Cp = pb("Cp", [P, SEG])
        W = [pb(f"W{i}", [P, SEG]) for i in range(2)]

        S = {n: sem(n) for n in """x_in w_in dve pool act ve rstd xn tp hT ip ip_used conv xc dbl
            hi r1 mid lo dr dtp dtp_used expn one lnu dtd dud b_ready b_copied c_ready expd dbud scan_done
            hc_done y_done yzd op res out_d""".split()}

        LW, LB = 0, 1
        CB, DTB, DSK, CW = 0, 1, 2, 3
        block = ctx.enter_context(nc.Block())

        @block.sync
        def _(sp):
            def load(dst, src, s):
                sp.dma_start(dst, src).then_inc(S[s], 16)
            load(x[:], A["x"], "x_in")
            load(ident[:], A["ident"], "w_in")
            load(lnw[:], A["lnw"], "w_in")
            load(chan[:], A["chan"], "w_in")
            load(alog[:], A["alog"], "w_in")
            load(pick[:], A["pick"].bitcast(bf16), "w_in")
            for l in range(LAYERS):
                load(inw[l][:], A["inw"][l], "w_in")
                load(xpw[l][:], A["xpw"][l], "w_in")
                load(dtw[l][96:96 + RANK, :], A["dtw"][l], "w_in")
                load(outw[l][:], A["outw"][l], "w_in")
        WALL = 16 * (5 + 4 * LAYERS)

        @block.vector
        def _(dve):
            n_own = [0]
            KV = 5 + 4 * 4 - 1 + 1

            def own(ins):
                ins.then_inc(S["dve"], 1)
                n_own[0] += 1

            dve.memset(xp[:], 0.0).then_inc(S["dve"], 1)
            dve.memset(dA[:], 0.0).then_inc(S["dve"], 1)
            dve.wait_ge(S["x_in"], 16)
            dve.wait_ge(S["w_in"], WALL)
            dve.wait_ge(S["act"], 1)
            dve.tensor_scalar(nega[:], nega[:], -1.0, None, ALU.mult).then_inc(S["dve"], 1)
            dve.sem_inc(S["scan_done"], 2)
            dve.sem_inc(S["hc_done"], 1)
            dve.sem_inc(S["res"], 1)
            base0 = 3
            for l in range(LAYERS):
                with dve.Fori(0, SEGS) as s:
                    u = s + l * SEGS
                    K = 28
                    n_own[0] = 0
                    base = base0 + u * K

                    def held():
                        dve.wait_ge(S["dve"], base + n_own[0])
                    dve.wait_ge(S["dve"], base)
                    if l:
                        dve.wait_ge(S["res"], 1 + u * 2)
                    for j in range(ST):
                        own(dve.bn_stats(stats[:, j, :], x[:, s * ST + j, :]))
                    held()
                    own(dve.memset(vare[:], 0.0))
                    for j in range(ST):
                        own(dve.bn_aggr(mv[:, j, :], stats[:, j, :]))
                    held()
                    dve.tensor_scalar(vare[:], mv[:, :, 1], EPS, None, ALU.add).then_inc(S["ve"], 1)
                    dve.wait_ge(S["rstd"], u * 2 + 2)
                    for j in range(ST):
                        dve.tensor_scalar(xn[:, j, :], x[:, s * ST + j, :], mv[:, j, 0:1], rstd[:, j:j + 1],
                                          ALU.subtract, ALU.mult).then_inc(S["xn"], 1)
                    cv4 = cv[:].rearrange("p m (b t) -> p m b t", b=SB)
                    for t in range(TAPS):
                        for m in range(M):
                            w = chan[:, l, CW + t, m:m + 1]
                            src = xp[:, m, :, t:t + SEQ]
                            if t == 0:
                                dve.wait_ge(S["ip_used"], u * 8 + m + 1)
                                own(dve.tensor_scalar(cv4[:, m], src, w, chan[:, l, CB, m:m + 1], ALU.mult, ALU.add))
                            else:
                                dve.wait_ge(S["dve"], base + 2 * ST + 1 + M * (t - 1) + m + 1)
                                ins = dve.scalar_tensor_tensor(cv4[:, m], src, w, cv4[:, m], ALU.mult, ALU.add)
                                if t < TAPS - 1:
                                    own(ins)
                                else:
                                    ins.then_inc(S["conv"], 1)
                    dve.wait_ge(S["hi"], u + 1)
                    dve.tensor_tensor(bcr[:], W[0][0:64, :], bc[0:64, :], ALU.subtract).then_inc(S["r1"], 1)
                    dve.wait_ge(S["r1"], u + 1)
                    dve.tensor_copy(bc[0:64, :], bcr[:]).then_inc(S["mid"], 1)
                    dve.wait_ge(S["mid"], u + 1)
                    dve.tensor_tensor(bc[0:32, :], bcr[0:32, :], bc[0:32, :], ALU.subtract).then_inc(S["lo"], 1)
                    dve.wait_ge(S["expn"], u + 1)
                    dve.tensor_scalar(cv[:], soft[:], 1.0, None, ALU.add).then_inc(S["one"], 1)
                    dve.wait_ge(S["one"], u + 1)
                    own(dve.scalar_tensor_tensor(soft[:], cv[:], 1.0, soft[:], ALU.subtract, ALU.subtract))
                    held()
                    own(dve.tensor_tensor(dt[:], dt[:], soft[:], ALU.subtract))
                    held()
                    dve.wait_ge(S["lnu"], u + 1)
                    own(dve.scalar_tensor_tensor(h[:], cv[:], 1.0, h[:], ALU.is_gt, ALU.mult))
                    held()
                    dve.tensor_tensor(dt[:], dt[:], h[:], ALU.add).then_inc(S["dtd"], 1)
                    dve.wait_ge(S["dtd"], u + 1)
                    dve.tensor_tensor(du[:], dt[:], xc[:], ALU.mult).then_inc(S["dud"], 1)
                    hf = h[:].rearrange("p m t -> p (m t)")
                    with dve.Fori(0, DS // 2) as k:
                        for par in range(2):
                            g = u * DS + k * 2 + par
                            dve.wait_ge(S["expd"], g + 1)
                            dve.wait_ge(S["dbud"], g + 1)
                            dve.wait_ge(S["hc_done"], g + 1)
                            dve.tensor_tensor_scan(hf, dA[:, par].rearrange("p m t -> p (m t)"),
                                                   dBu[:, par].rearrange("p m t -> p (m t)"), 0.0,
                                                   ALU.mult, ALU.add).then_inc(S["scan_done"], 1)
                            dve.wait_ge(S["scan_done"], g + 3)
                            dve.wait_ge(S["c_ready"], g + 1)
                            dve.wait_ge(S["y_done"], g + 1)
                            dve.tensor_tensor(hC[:, par], h[:], Cp[:].unsqueeze(1).broadcast_to([P, M, SEG]),
                                              ALU.mult).then_inc(S["hc_done"], 1)
                    dve.wait_ge(S["y_done"], (u + 1) * DS + 2)
                    for m in range(M):
                        own(dve.scalar_tensor_tensor(yz[:, m], xc[:, m], chan[:, l, DSK, m:m + 1], Y[:, m],
                                                     ALU.mult, ALU.add))
                    held()
                    dve.tensor_tensor(yz[:], yz[:], zs[:], ALU.mult).then_inc(S["yzd"], 1)
                    for w in range(2):
                        dve.wait_ge(S["op"], u * 2 + w + 1)
                        xs = x[:, bass.ds(s * ST + 2 * w, 2), :]
                        dve.tensor_tensor(xs, xs, W[w][:].rearrange("p (j d) -> p j d", j=2),
                                          ALU.add).then_inc(S["res"], 1)
                    if n_own[0] != K:
                        print("K should be", n_own[0])

        @block.scalar
        def _(act):
            act.wait_ge(S["w_in"], WALL)
            act.activation(nega[:], alog[:], ACT.Exp).then_inc(S["act"], 1)
            act.wait_ge(S["dve"], 3)
            act.sem_inc(S["b_copied"], 1)
            for l in range(LAYERS):
                with act.Fori(0, SEGS) as s:
                    u = s + l * SEGS
                    act.wait_ge(S["ve"], u + 1)
                    act.activation(vare[:], vare[:], ACT.Ln).then_inc(S["rstd"], 1)
                    act.wait_ge(S["rstd"], u * 2 + 1)
                    act.activation(rstd[:], vare[:], ACT.Exp, scale=-0.5).then_inc(S["rstd"], 1)
                    for k in range(KD):
                        act.wait_ge(S["tp"], u * KD + k + 1)
                        act.activation(hT[:, k, :], W[k][:], ACT.Identity, scale=lnw[:, l, LW, k:k + 1],
                                       bias=lnw[:, l, LB, k:k + 1]).then_inc(S["hT"], 1)
                    for m in range(2 * M):
                        act.wait_ge(S["ip"], u * 8 + m + 1)
                        if m < M:
                            act.activation(xp[:, m, :, PAD:PAD + SEQ], W[m % 2][:].rearrange("p (b t) -> p b t", b=SB),
                                           ACT.Copy).then_inc(S["ip_used"], 1)
                        else:
                            act.activation(zs[:, m - M, :], W[m % 2][:], ACT.Silu).then_inc(S["ip_used"], 1)
                    for m in range(M):
                        act.wait_ge(S["conv"], u * M + m + 1)
                        act.activation(xc[:, m, :], cv[:, m, :], ACT.Silu).then_inc(S["xc"], 1)
                    act.wait_ge(S["dbl"], u + 1)
                    act.activation(bc[:], W[0][0:96, :], ACT.Copy).then_inc(S["hi"], 1)
                    act.activation(dr[96:96 + RANK, :], W[0][96:96 + RANK, :], ACT.Copy).then_inc(S["dr"], 1)
                    for m in range(M):
                        act.wait_ge(S["dtp"], u * M + m + 1)
                        act.activation(soft[:, m, :], W[(m + 1) % 2][:], ACT.Abs, bias=chan[:, l, DTB, m:m + 1])
                        act.activation(dt[:, m, :], W[(m + 1) % 2][:], ACT.Relu,
                                       bias=chan[:, l, DTB, m:m + 1]).then_inc(S["dtp_used"], 1)
                    act.wait_ge(S["dtp_used"], (u + 1) * M)
                    act.activation(soft[:], soft[:], ACT.Exp, scale=-1.0).then_inc(S["expn"], 1)
                    act.wait_ge(S["one"], u + 1)
                    act.activation(h[:], cv[:], ACT.Ln).then_inc(S["lnu"], 1)
                    act.wait_ge(S["dtd"], u + 1)
                    with act.Fori(0, DS // 2) as k:
                        for par in range(2):
                            g = u * DS + k * 2 + par
                            act.wait_ge(S["b_ready"], g + 1)
                            act.wait_ge(S["scan_done"], g + 1)
                            act.activation(brow[:, par, :], Bp[:], ACT.Copy).then_inc(S["b_copied"], 1)
                            for m in range(M):
                                ins = act.activation(
                                    dA[:, par, m, :].rearrange("p (b t) -> p b t", b=SB)[:, :, 1:],
                                    dt[:, m, :].rearrange("p (b t) -> p b t", b=SB)[:, :, 1:],
                                    ACT.Exp, scale=nega[:, l, m, bass.ds(k * 2 + par, 1)])
                            ins.then_inc(S["expd"], 1)

        @block.gpsimd
        def _(pool):
            for l in range(LAYERS):
                with pool.Fori(0, SEGS) as s:
                    u = s + l * SEGS
                    with pool.Fori(0, DS // 2) as k:
                        pool.wait_ge(S["dud"], u + 1)
                        for par in range(2):
                            g = u * DS + k * 2 + par
                            pool.wait_ge(S["b_copied"], g + 2)
                            pool.wait_ge(S["scan_done"], g + 1)
                            pool.tensor_tensor(dBu[:, par], du[:], brow[:, par].unsqueeze(1).broadcast_to([P, M, SEG]),
                                               ALU.mult).then_inc(S["dbud"], 1)

        @block.tensor
        def _(pe):
            pe.wait_ge(S["w_in"], WALL)
            pe.sem_inc(S["y_done"], 2)
            for l in range(LAYERS):
                with pe.Fori(0, SEGS) as s:
                    u = s + l * SEGS
                    pe.wait_ge(S["xn"], (u + 1) * ST)
                    pe.wait_ge(S["res"], 1 + u * 2)
                    for k in range(KD):
                        for j in range(ST):
                            ins = pe.transpose(W[k][:, j * P:(j + 1) * P], xn[:, j, k * P:(k + 1) * P], ident[:])
                        ins.then_inc(S["tp"], 1)
                    pe.wait_ge(S["hT"], (u + 1) * KD)
                    for m in range(2 * M):
                        if m >= 2:
                            pe.wait_ge(S["ip_used"], u * 8 + m - 1)
                        for k in range(KD):
                            ins = pe.matmul(W[m % 2][:], inw[l][:, k, m * P:(m + 1) * P], hT[:, k, :],
                                            start=(k == 0), stop=(k == KD - 1))
                        ins.then_inc(S["ip"], 1)
                    pe.wait_ge(S["ip_used"], u * 8 + 8)
                    for m in range(M):
                        pe.wait_ge(S["xc"], u * M + m + 1)
                        ins = pe.matmul(W[0][0:XPR, :], xpw[l][:, m, :], xc[:, m, :], start=(m == 0), stop=(m == M - 1))
                    ins.then_inc(S["dbl"], 1)
                    pe.wait_ge(S["dr"], u + 1)
                    for m in range(M):
                        if m == 1:
                            pe.wait_ge(S["r1"], u + 1)
                        if m >= 2:
                            pe.wait_ge(S["dtp_used"], u * M + m - 1)
                        pe.matmul(W[(m + 1) % 2][:], dtw[l][96:96 + RANK, m * P:(m + 1) * P], dr[96:96 + RANK, :],
                                  start=True, stop=True).then_inc(S["dtp"], 1)
                    pe.wait_ge(S["lo"], u + 1)

                    def rows(n, g):
                        pe.wait_ge(S["b_copied"], g + 1)
                        pe.matmul(Bp[:], pick[:, bass.ds(n, 1), :].rearrange("p a c -> p (a c)"), bc[:],
                                  start=True, stop=True).then_inc(S["b_ready"], 1)
                        pe.wait_ge(S["hc_done"], g + 1)
                        pe.matmul(Cp[:], pick[:, bass.ds(n + DS, 1), :].rearrange("p a c -> p (a c)"), bc[:],
                                  start=True, stop=True).then_inc(S["c_ready"], 1)

                    def add(par, g, start, stop):
                        pe.wait_ge(S["hc_done"], g + 2)
                        for m in range(M):
                            ins = pe.matmul(Y[:, m], ident[:], hC[:, par, m], start=start, stop=stop)
                        ins.then_inc(S["y_done"], 1)

                    g0 = u * DS
                    rows(0, g0)
                    rows(1, g0 + 1)
                    add(0, g0, True, False)
                    with pe.Fori(1, DS // 2) as k:
                        g = g0 + k * 2
                        rows(k * 2, g)
                        add(1, g - 1, False, False)
                        rows(k * 2 + 1, g + 1)
                        add(0, g, False, False)
                    add(1, g0 + DS - 1, False, True)
                    pe.wait_ge(S["yzd"], u + 1)
                    for j in range(ST):
                        for m in range(M):
                            ins = pe.matmul(W[j // 2][:, (j % 2) * DM:(j % 2 + 1) * DM], yz[:, m, j * P:(j + 1) * P],
                                            outw[l][:, m, :], start=(m == 0), stop=(m == M - 1))
                        if j % 2:
                            ins.then_inc(S["op"], 1)


HEADS, KV, HDIM = 16, 4, 16
GRP = HEADS // KV
SLOT = 32
EXP, TOP = 8, 2
CAPACITY = float(max(int(TOK * 1.25 / EXP), 4))


def wide(ap, shape):
    return ap.broadcast_to(shape)


def blend(nc, A, x, name, res, add):
    fp32 = mybir.dt.float32
    ALU, ACT = mybir.AluOpType, mybir.ActivationFunctionType
    with ExitStack() as ctx:
        sb = lambda n, shape: ctx.enter_context(nc.sbuf_tensor(name + n, shape, fp32))
        sem = lambda n: ctx.enter_context(nc.semaphore(name + "_" + n))
        wb = sb("wb", [P, 2, DM])
        if add is None:
            r = sb("r", [P, TILES, DM])
            v = x
        else:
            r = x
            v = add
        stats = sb("stats", [P, TILES, 6])
        mv = sb("mv", [P, TILES, 2])
        rstd = sb("rstd", [P, TILES])
        inp, var, rs, own = sem("inputs"), sem("variance"), sem("rstd"), sem("vector")
        block = ctx.enter_context(nc.Block())

        @block.sync
        def _(sp):
            src = A["nf"] if add is None else A["xn_wb"]
            sp.dma_start(wb[:].rearrange("p a d -> p (a d)"), src.broadcast_to([P, 2 * DM])).then_inc(inp, 16)
            if add is None:
                sp.dma_start(r[:], A["x"]).then_inc(inp, 16)
        N_IN = 32 if add is None else 16

        @block.scalar
        def _(act):
            for rnd in range(2):
                act.wait_ge(var, rnd + 1)
                act.activation(rstd[:], rstd[:], ACT.Ln).then_inc(rs, 1)
                act.wait_ge(rs, 2 * rnd + 1)
                act.activation(rstd[:], rstd[:], ACT.Exp, scale=-0.5).then_inc(rs, 1)

        @block.vector
        def _(dve):
            n = [0]

            def mark(ins):
                ins.then_inc(own, 1)
                n[0] += 1

            def held():
                dve.wait_ge(own, n[0])

            def norm(t, rnd):
                for j in range(TILES):
                    mark(dve.bn_stats(stats[:, j, :], t[:, j, :]))
                held()
                for j in range(TILES):
                    mark(dve.bn_aggr(mv[:, j, :], stats[:, j, :]))
                held()
                dve.tensor_scalar(rstd[:], mv[:, :, 1], EPS, None, ALU.add).then_inc(var, 1)
                dve.wait_ge(rs, 2 * rnd + 2)
                for j in range(TILES):
                    mark(dve.tensor_scalar(t[:, j, :], t[:, j, :], mv[:, j, 0:1], rstd[:, j:j + 1],
                                           ALU.subtract, ALU.mult))
                held()
            norm(v, 0)
            dve.wait_ge(inp, N_IN)
            mark(dve.tensor_tensor(v[:], v[:], wb[:, 0].unsqueeze(1).broadcast_to([P, TILES, DM]), ALU.mult))
            held()
            mark(dve.tensor_tensor(v[:], v[:], wb[:, 1].unsqueeze(1).broadcast_to([P, TILES, DM]), ALU.add))
            held()
            mark(dve.tensor_tensor(x[:], v[:], r[:], ALU.add))
            held()
            norm(x, 1)


def attention(nc, A, x, ident):
    fp32, bf16 = mybir.dt.float32, mybir.dt.bfloat16
    ALU, ACT, AX = mybir.AluOpType, mybir.ActivationFunctionType, mybir.AxisListType
    HW = HEADS * HDIM
    KW = KV * HDIM
    BT = SEQ // P
    UNITS = KV * GRP // 2
    with ExitStack() as outer:
        att = outer.enter_context(nc.sbuf_tensor("att", [P, TILES, DM], fp32))
        with ExitStack() as ctx:
            sb = lambda n, shape: ctx.enter_context(nc.sbuf_tensor("at_" + n, shape, fp32))
            pb = lambda n, shape: ctx.enter_context(nc.psum_tensor("ap_" + n, shape, fp32))
            sem = lambda n: ctx.enter_context(nc.semaphore("a_" + n))
            wq, wkv = sb("wq", [P, KD, HW]), sb("wkv", [P, KD, 2 * KW])
            bqkv = sb("bqkv", [P, HW + 2 * KW])
            rope = sb("rope", [P, BATCH, 2 * HW + 2 * KW])
            ctxT = sb("ctxT", [P, KD, SEQ])
            xb = sb("xb", [P, BT, DM])
            xT = sb("xT", [P, KD, SEQ])
            qk = sb("qk", [P, BT, HW + KW])
            rot = sb("rot", [P, BT, HW + KW])
            qp = sb("qp", [P, BT, KV, GRP, SLOT])
            kp = sb("kp", [P, BT, KV, GRP, SLOT])
            vb = sb("vb", [P, BT, KV, HDIM + 1])
            qT = sb("qT", [P, KV, SEQ])
            kT = sb("kT", [P, KV, SEQ])
            top = sb("top", [P, UNITS, GRP])
            prob = sb("prob", [P, 2, GRP, SEQ])
            probT = sb("probT", [P, BT, GRP, P])
            inv = sb("inv", [P, UNITS, GRP])
            SP_ = pb("S", [P, 2, GRP, SEQ])
            TP = pb("T", [P, BT, GRP, P])
            OP = pb("O", [P, GRP, HDIM + 1])
            QP = pb("Q", [P, BT, HW])
            KP_ = TP[:, 0].rearrange("p g t -> p (g t)")[:, 0:BT * 2 * KW].rearrange("p (b k) -> p b k", b=BT)
            S = {n: sem(n) for n in """w ctx xb xt xtc qkv own qkp qkt qktc s top prob pt ptc pv norm""".split()}
            block = ctx.enter_context(nc.Block())
            NW = 16 * 4

            @block.sync
            def _(sp):
                sp.dma_start(wq[:], A["wq"]).then_inc(S["w"], 16)
                sp.dma_start(wkv[:], A["wkv"]).then_inc(S["w"], 16)
                sp.dma_start(bqkv[:], A["bqkv"].broadcast_to([P, HW + 2 * KW])).then_inc(S["w"], 16)
                sp.dma_start(rope[:].rearrange("p a d -> p (a d)"),
                             A["rope"].broadcast_to([P, BATCH * 2 * (HW + KW)])).then_inc(S["w"], 16)
                with sp.Fori(0, BATCH) as b:
                    sp.wait_ge(S["qkv"], b + 1)
                    sp.dma_start(ctxT[:], A["ctxT"][bass.ds(b, 1)].rearrange("a p k t -> p (a k) t")).then_inc(S["ctx"], 16)

            @block.vector
            def _(dve):
                dve.sem_inc(S["ptc"], 1)
                dve.sem_inc(S["norm"], 1)
                dve.memset(qp[:], 0.0).then_inc(S["own"], 1)
                dve.memset(kp[:], 0.0).then_inc(S["own"], 1)
                dve.memset(vb[:], 1.0).then_inc(S["own"], 1)
                dve.wait_ge(S["w"], NW)
                with dve.Fori(0, BATCH) as b:
                    K = 11
                    n = [0]
                    base = b * K + 3

                    def mark(ins):
                        ins.then_inc(S["own"], 1)
                        n[0] += 1

                    def held():
                        dve.wait_ge(S["own"], base + n[0])
                    held()
                    mark(dve.tensor_copy(xb[:], x[:, bass.ds(b * BT, BT), :]))
                    held()
                    dve.tensor_scalar(xb[:], xb[:], 1.0, None, ALU.mult).then_inc(S["xb"], 1)
                    dve.wait_ge(S["qkv"], b + 2)
                    bias = bqkv[:].unsqueeze(1).broadcast_to([P, BT, HW + 2 * KW])
                    mark(dve.tensor_tensor(qk[:, :, 0:HW], QP[:], bias[:, :, 0:HW], ALU.add))
                    mark(dve.tensor_tensor(qk[:, :, HW:], KP_[:, :, 0:KW], bias[:, :, HW:HW + KW], ALU.add))
                    mark(dve.tensor_tensor(vb[:, :, :, 0:HDIM],
                                           KP_[:, :, KW:].rearrange("p b (h d) -> p b h d", h=KV),
                                           bias[:, :, HW + KW:].rearrange("p b (h d) -> p b h d", h=KV), ALU.add))
                    held()
                    rb = rope[:, bass.ds(b, 1), :]
                    for lo, heads, cut, c0 in ((0, HEADS, HEADS // 2, 0), (HW, KV, KV // 2, 2 * HW)):
                        w = heads * HDIM
                        v = lambda t, a, z: t.rearrange("p b (h d) -> p b h d", h=heads)[:, :, :, a:z]
                        for j in range(BT):
                            q1 = qk[:, j:j + 1, lo:lo + w]
                            r1 = rot[:, j:j + 1, lo:lo + w]
                            sn = rb[:, :, c0 + w:c0 + 2 * w]
                            first = HDIM - cut
                            last = dve.tensor_tensor(v(r1, 0, first), v(q1, cut, HDIM), v(sn, 0, first), ALU.mult)
                            last = dve.tensor_tensor(v(r1, first, HDIM), v(q1, 0, cut), v(sn, first, HDIM), ALU.mult)
                        mark(last)
                    held()
                    for lo, w, c0 in ((0, HW, 0), (HW, KW, 2 * HW)):
                        for j in range(BT):
                            last = dve.tensor_tensor(rot[:, j:j + 1, lo:lo + w], rot[:, j:j + 1, lo:lo + w],
                                                     rb[:, :, c0:c0 + w], ALU.add)
                        mark(last)
                    held()
                    for j in range(BT):
                        last = dve.tensor_tensor(
                            qp[:, j, :, :, 0:HDIM].rearrange("p k g d -> p (k g) d"),
                            rot[:, j, 0:HW].rearrange("p (h d) -> p h d", h=HEADS),
                            qk[:, j, 0:HW].rearrange("p (h d) -> p h d", h=HEADS), ALU.mult)
                    mark(last)
                    mark(dve.tensor_tensor(rot[:, :, HW:], rot[:, :, HW:], qk[:, :, HW:], ALU.mult))
                    held()
                    for j in range(BT):
                        for g in range(GRP):
                            last = dve.tensor_copy(kp[:, j, :, g, 0:HDIM],
                                                   rot[:, j, HW:].rearrange("p (h d) -> p h d", h=KV))
                    last.then_inc(S["qkp"], 1)
                    def tail(i):
                        ui = b * UNITS + i
                        dve.wait_ge(S["pt"], ui + 1)
                        dve.wait_ge(S["pv"], ui + 1)
                        dve.tensor_copy(probT[:], TP[:]).then_inc(S["ptc"], 1)

                    def norm(i):
                        ui = b * UNITS + i
                        dve.wait_ge(S["pv"], ui + 2)
                        dve.reciprocal(inv[:, i, :], OP[:, :, HDIM]).then_inc(S["norm"], 1)
                        dve.wait_ge(S["norm"], 2 * ui + 2)
                        out = att[:, bass.ds(b * BT, BT), i * 2 * HDIM:(i + 1) * 2 * HDIM]
                        dve.tensor_tensor(out.rearrange("p n (h d) -> p n h d", h=2),
                                          OP[:, :, 0:HDIM].rearrange("p (h n) d -> p n h d", h=2),
                                          inv[:, i, :].rearrange("p (h n) -> p n h", h=2).unsqueeze(3).broadcast_to([P, BT, 2, HDIM]),
                                          ALU.mult).then_inc(S["norm"], 1)
                    for i in range(UNITS + 1):
                        ui = b * UNITS + i
                        if i < UNITS:
                            dve.wait_ge(S["s"], ui + 1)
                            dve.tensor_reduce(top[:, i, :], SP_[:, i % 2], AX.X, ALU.max, negate=True).then_inc(S["top"], 1)
                        if i >= 1:
                            tail(i - 1)
                            norm(i - 1)
                    mark(dve.memset(inv[:, 0, 0:1], 0.0))
                    if n[0] != K:
                        print("att K", n[0])
                        assert 0

            @block.scalar
            def _(act):
                act.sem_inc(S["prob"], 1)
                with act.Fori(0, BATCH) as b:
                    for k in range(KD):
                        act.wait_ge(S["xt"], b * KD + k + 1)
                        act.activation(xT[:, k, :], SP_[:, k, 0, :], ACT.Copy).then_inc(S["xtc"], 1)
                    for r, dst in ((0, qT), (1, kT)):
                        act.wait_ge(S["qkt"], 2 * b + r + 1)
                        act.activation(dst[:].rearrange("p k t -> p (k t)"),
                                       SP_[:, r].rearrange("p g t -> p (g t)"), ACT.Copy).then_inc(S["qktc"], 1)
                    for i in range(UNITS):
                        ui = b * UNITS + i
                        act.wait_ge(S["top"], ui + 1)
                        if i >= 2:
                            act.wait_ge(S["pt"], ui - 1)
                        for g in range(GRP):
                            last = act.activation(prob[:, i % 2, g], SP_[:, i % 2, g], ACT.Exp, bias=top[:, i, g:g + 1])
                        last.then_inc(S["prob"], 1)

            @block.tensor
            def _(pe):
                pe.wait_ge(S["w"], NW)
                pe.sem_inc(S["qkv"], 1)
                pe.sem_inc(S["pv"], 1)
                with pe.Fori(0, BATCH) as b:
                    pe.wait_ge(S["xb"], b + 1)
                    pe.wait_ge(S["prob"], b * UNITS + 1)
                    for k in range(KD):
                        for j in range(BT):
                            last = pe.transpose(SP_[:, k, 0, j * P:(j + 1) * P], xb[:, j, k * P:(k + 1) * P], ident[:])
                        last.then_inc(S["xt"], 1)
                    pe.wait_ge(S["xtc"], (b + 1) * KD)
                    for j in range(BT):
                        for k in range(KD):
                            pe.matmul(QP[:, j], xT[:, k, j * P:(j + 1) * P], wq[:, k, :], start=(k == 0), stop=(k == KD - 1))
                    pe.wait_ge(S["ctx"], 16 * b + 16)
                    pe.wait_ge(S["ptc"], b * UNITS + 1)
                    for j in range(BT):
                        for k in range(KD):
                            last = pe.matmul(KP_[:, j], ctxT[:, k, j * P:(j + 1) * P], wkv[:, k, :],
                                             start=(k == 0), stop=(k == KD - 1))
                    last.then_inc(S["qkv"], 1)
                    pe.wait_ge(S["qkp"], b + 1)
                    for r, src in ((0, qp), (1, kp)):
                        for m in range(KV):
                            for j in range(BT):
                                last = pe.transpose(SP_[:, r].rearrange("p g t -> p (g t)")[:, (m * BT + j) * P:(m * BT + j + 1) * P],
                                                    src[:, j, m].rearrange("p g d -> p (g d)"), ident[:])
                        last.then_inc(S["qkt"], 1)
                    pe.wait_ge(S["qktc"], 2 * b + 2)

                    def scores(i):
                        m, pair = divmod(i, GRP // 2)
                        ui = b * UNITS + i
                        if i >= 2:
                            pe.wait_ge(S["prob"], ui)
                        for q in range(BT):
                            for hd in range(2):
                                g = 2 * pair + hd
                                rows = slice(g * SLOT, g * SLOT + HDIM)
                                last = pe.matmul(SP_[:, i % 2, hd * BT + q], qT[rows, m, q * P:(q + 1) * P], kT[rows, m, :],
                                                 start=True, stop=True)
                        last.then_inc(S["s"], 1)

                    def turn(i):
                        ui = b * UNITS + i
                        pe.wait_ge(S["prob"], ui + 2)
                        pe.wait_ge(S["ptc"], ui + 1)
                        for g in range(GRP):
                            for st in range(BT):
                                last = pe.transpose(TP[:, st, g], prob[:, i % 2, g, st * P:(st + 1) * P], ident[:])
                        last.then_inc(S["pt"], 1)

                    def values(i):
                        m = i // (GRP // 2)
                        ui = b * UNITS + i
                        pe.wait_ge(S["ptc"], ui + 2)
                        pe.wait_ge(S["norm"], 2 * ui + 1)
                        for g in range(GRP):
                            for st in range(BT):
                                last = pe.matmul(OP[:, g], probT[:, st, g], vb[:, st, m, :], start=(st == 0), stop=(st == BT - 1))
                        last.then_inc(S["pv"], 1)
                    scores(0)
                    for i in range(UNITS):
                        if i + 1 < UNITS:
                            scores(i + 1)
                        turn(i)
                        values(i)
        blend(nc, A, x, "xattn", "x", att)


def moe(nc, A, x, ident):
    fp32, bf16 = mybir.dt.float32, mybir.dt.bfloat16
    ALU, ACT, AX = mybir.AluOpType, mybir.ActivationFunctionType, mybir.AxisListType
    CH = 512
    CHUNKS = TOK // CH
    CT = CH // P
    with ExitStack() as ctx:
        sb = lambda n, shape, dt=fp32: ctx.enter_context(nc.sbuf_tensor("mo_" + n, shape, dt))
        sem = lambda n: ctx.enter_context(nc.semaphore("m_" + n))
        rw = sb("rw", [P, KD, EXP])
        rb = sb("rb", [P, EXP])
        iota = sb("iota", [P, EXP])
        identb = sb("identb", [P, P], bf16)
        picke = sb("picke", [96, EXP, P], bf16)
        b1 = sb("b1", [P, KD, EXP])
        b2 = sb("b2", [EXP, DM])
        b1e = sb("b1e", [P, 2, KD])
        w1 = sb("w1", [P, 2, KD, DM])
        w2 = sb("w2", [P, 2, KD, DM])
        xT = sb("xT", [P, KD, TOK])
        ones = sb("ones", [P, 1])
        lg = sb("lg", [P, TILES, EXP])
        tmp = sb("tmp", [P, TILES, EXP])
        one = [sb(f"hot{k}", [P, TILES, EXP]) for k in range(TOP)]
        mask = sb("mask", [P, TILES, EXP])
        rmax = sb("rmax", [P, TILES])
        best = sb("best", [P, TILES, 8])
        besti = sb("besti", [P, TILES, 8], mybir.dt.uint32)
        bestf = sb("bestf", [P, TILES, 8])
        norm2 = sb("norm2", [P, TILES])
        mres = sb("mres", [P, TILES, EXP])
        parts = sb("parts", [P, TILES, 96], bf16)
        maskT = sb("maskT", [EXP, TOK])
        partsT = sb("partsT", [96, TOK], bf16)
        mrow = sb("mrow", [P, 2, TOK])
        hid = sb("hid", [P, 2, KD, CH])
        act_ = sb("act", [P, 2, KD, CH])
        stats = sb("stats", [P, TILES, 6])
        mv = sb("mv", [P, TILES, 2])
        rstd = sb("rstd", [P, TILES])
        S = {n: sem(n) for n in """w xt xtc lg own rex mk mt mtc mr mrc wa wb2 w1u b1c st hp hm g o acc fin ve rs out""".split()}

        with ExitStack() as ps:
            TPs = [ps.enter_context(nc.psum_tensor(f"mo_t{i}", [P, CH], fp32)) for i in range(2)]
            LG = ps.enter_context(nc.psum_tensor("mo_logits", [P, TILES, EXP], fp32))
            CS = ps.enter_context(nc.psum_tensor("mo_cs", [EXP, TOP], fp32))
            MT = ps.enter_context(nc.psum_tensor("mo_mt", [EXP, CH], fp32))
            PT = ps.enter_context(nc.psum_tensor("mo_pt", [96, CH], bf16))
            IN = [ps.enter_context(nc.psum_tensor(f"mo_in{i}", [P, 2, DM], fp32)) for i in range(2)]
            block = ps.enter_context(nc.Block())
            NW = 16 * 7

            @block.sync
            def _(sp):
                sp.dma_start(rw[:], A["rw"]).then_inc(S["w"], 16)
                sp.dma_start(rb[:], A["rb"].broadcast_to([P, EXP])).then_inc(S["w"], 16)
                sp.dma_start(iota[:], A["iota"].broadcast_to([P, EXP])).then_inc(S["w"], 16)
                sp.dma_start(identb[:], A["identb"].bitcast(bf16)).then_inc(S["w"], 16)
                sp.dma_start(picke[:], A["picke"].bitcast(bf16)).then_inc(S["w"], 16)
                sp.dma_start(b1[:], A["b1"]).then_inc(S["w"], 16)
                sp.dma_start(b2[:], A["b2"]).then_inc(S["w"], 16)

            @block.tensor
            def _(pe):
                n = 0
                for c in range(CHUNKS):
                    for k in range(KD):
                        if n >= 2:
                            pe.wait_ge(S["xtc"], n - 1)
                        for j in range(CT):
                            last = pe.transpose(TPs[n % 2][:, j * P:(j + 1) * P], x[:, c * CT + j, k * P:(k + 1) * P], ident[:])
                        last.then_inc(S["xt"], 1)
                        n += 1
                pe.wait_ge(S["w"], NW)
                pe.wait_ge(S["xtc"], n)
                for t in range(TILES):
                    for k in range(KD):
                        last = pe.matmul(LG[:, t], xT[:, k, t * P:(t + 1) * P], rw[:, k, :], start=(k == 0), stop=(k == KD - 1))
                last.then_inc(S["lg"], 1)
                pe.wait_ge(S["mk"], 1)
                for k in range(TOP):
                    for t in range(TILES):
                        last = pe.matmul(CS[:, k:k + 1], one[k][:, t, :], ones[:], start=(t == 0), stop=(t == TILES - 1))
                last.then_inc(S["mt"], 1)
                pe.wait_ge(S["mk"], 2)
                for c in range(CHUNKS):
                    if c:
                        pe.wait_ge(S["mtc"], 2 * c)
                    for j in range(CT):
                        pe.transpose(MT[:, j * P:(j + 1) * P], mask[:, c * CT + j, :], ident[:])
                        last = pe.transpose(PT[:, j * P:(j + 1) * P], parts[:, c * CT + j, :], identb[:])
                    last.then_inc(S["mt"], 1)
                pe.wait_ge(S["mtc"], 2 * CHUNKS)
                for t in range(TILES):
                    w, half = divmod(t, 2)
                    if half == 0 and w >= 2:
                        pe.wait_ge(S["fin"], w - 1)
                    last = pe.matmul(IN[w % 2][:, half], maskT[:, t * P:(t + 1) * P], b2[:], start=True, stop=True)
                    if half:
                        last.then_inc(S["o"], 1)

            @block.scalar
            def _(act):
                n = 0
                for c in range(CHUNKS):
                    for k in range(KD):
                        act.wait_ge(S["xt"], n + 1)
                        act.activation(xT[:, k, c * CH:(c + 1) * CH], TPs[n % 2][:], ACT.Copy).then_inc(S["xtc"], 1)
                        n += 1
                act.wait_ge(S["rex"], 1)
                act.activation(tmp[:], tmp[:], ACT.Exp).then_inc(S["rex"], 1)
                for c in range(CHUNKS):
                    act.wait_ge(S["mt"], c + 2)
                    act.activation(maskT[:, c * CH:(c + 1) * CH], MT[:], ACT.Copy).then_inc(S["mtc"], 1)
                    act.activation(partsT[:, c * CH:(c + 1) * CH], PT[:], ACT.Copy).then_inc(S["mtc"], 1)

            @block.vector
            def _(dve):
                n = [0]

                def do(ins):
                    ins.then_inc(S["own"], 1)
                    n[0] += 1
                    dve.wait_ge(S["own"], n[0])
                per = lambda a: a.unsqueeze(2).broadcast_to([P, TILES, EXP])
                do(dve.memset(ones[:], 1.0))
                do(dve.memset(parts[:], 0.0))
                dve.wait_ge(S["w"], NW)
                dve.wait_ge(S["lg"], 1)
                do(dve.tensor_tensor(lg[:], LG[:], rb[:].unsqueeze(1).broadcast_to([P, TILES, EXP]), ALU.add))
                do(dve.tensor_reduce(rmax[:], lg[:], AX.X, ALU.max))
                dve.tensor_tensor(tmp[:], lg[:], per(rmax[:]), ALU.subtract).then_inc(S["rex"], 1)
                dve.wait_ge(S["rex"], 2)
                do(dve.tensor_reduce(norm2[:], tmp[:], AX.X, ALU.add))
                do(dve.reciprocal(norm2[:], norm2[:]))
                do(dve.tensor_tensor(lg[:], tmp[:], per(norm2[:]), ALU.mult))
                for t in range(TILES):
                    do(dve.max(best[:, t, :], lg[:, t, :]))
                    do(dve.max_index(besti[:, t, :], best[:, t, :], lg[:, t, :]))
                do(dve.tensor_copy(bestf[:], besti[:]))
                do(dve.tensor_tensor(norm2[:], best[:, :, 0], best[:, :, 1], ALU.add))
                do(dve.reciprocal(norm2[:], norm2[:]))
                do(dve.tensor_tensor(best[:], best[:], per(norm2[:]), ALU.mult))
                for k in range(TOP):
                    do(dve.tensor_tensor(one[k][:], iota[:].unsqueeze(1).broadcast_to([P, TILES, EXP]),
                                         per(bestf[:, :, k]), ALU.is_equal))
                    do(dve.tensor_tensor(one[k][:], one[k][:], per(best[:, :, k]), ALU.mult))
                dve.tensor_tensor(mask[:], one[0][:], one[1][:], ALU.add).then_inc(S["mk"], 1)
                dve.wait_ge(S["mk"], 1)
                dve.wait_ge(S["mt"], 1)
                do(dve.tensor_tensor(mask[0:EXP, 0, 0:TOP], mask[0:EXP, 0, 0:TOP], CS[:], ALU.add))
                do(dve.tensor_scalar(mask[:], mask[:], CAPACITY, None, ALU.min))
                do(dve.tensor_copy(parts[:, :, 0:EXP], mask[:]))
                do(dve.tensor_tensor(mres[:], mask[:], parts[:, :, 0:EXP], ALU.subtract))
                do(dve.tensor_copy(parts[:, :, 32:32 + EXP], mres[:]))
                dve.tensor_tensor(parts[:, :, 64:64 + EXP], mres[:], parts[:, :, 32:32 + EXP], ALU.subtract).then_inc(S["mk"], 1)
                for w in range(TILES // 2):
                    dve.wait_ge(S["o"], w + 1)
                    dve.tensor_tensor(x[:, 2 * w:2 * w + 2, :], x[:, 2 * w:2 * w + 2, :], IN[w % 2][:], ALU.add).then_inc(S["fin"], 1)

        with ExitStack() as ps:
            HP = [ps.enter_context(nc.psum_tensor(f"mo_h{i}", [P, CH], fp32)) for i in range(3)]
            MR = ps.enter_context(nc.psum_tensor("mo_mr", [P, CH], fp32))
            OP = [ps.enter_context(nc.psum_tensor(f"mo_o{i}", [P, 2, DM], fp32)) for i in range(4)]
            block = ps.enter_context(nc.Block())
            PAIRS = EXP // 2
            HPE = CHUNKS * KD
            OB = TILES // 2
            arrived = [S["wa"], S["wb2"]]

            @block.sync
            def _(sp):
                for par in range(2):
                    sp.dma_start(w1[:, par], A["w1"][par]).then_inc(arrived[par], 16)
                    sp.dma_start(w2[:, par], A["w2"][par]).then_inc(arrived[par], 16)
                with sp.Fori(1, PAIRS) as r:
                    for par in range(2):
                        sp.wait_ge(S["w1u"], 2 * r - 1 + par)
                        sp.dma_start(w1[:, par], A["w1"][bass.ds(2 * r + par, 1)].rearrange("a p k d -> p (a k) d")).then_inc(arrived[par], 16)
                        sp.dma_start(w2[:, par], A["w2"][bass.ds(2 * r + par, 1)].rearrange("a p k d -> p (a k) d")).then_inc(arrived[par], 16)
                sp.wait_ge(S["out"], TILES)
                sp.dma_start(A["out"], x[:]).then_inc(S["st"], 16)
                sp.wait_ge(S["st"], 16)

            @block.tensor
            def _(pe):
                with pe.Fori(0, PAIRS) as r:
                    for par in range(2):
                        e = r * 2 + par
                        pe.wait_ge(arrived[par], r * 32 + 32)
                        for c in range(CHUNKS):
                            pe.wait_ge(S["mrc"], e * CHUNKS + c + 1)
                            pe.matmul(MR[:], picke[:, bass.ds(e, 1), :].rearrange("p a c -> p (a c)"),
                                      partsT[:, c * CH:(c + 1) * CH], start=True, stop=True).then_inc(S["mr"], 1)

                        def up(c):
                            for m in range(KD):
                                i = c * KD + m
                                q = par * HPE + i
                                pe.wait_ge(S["hm"], e * HPE + i + 1)
                                for k in range(KD):
                                    last = pe.matmul(HP[i % 2][:], w1[:, par, k, m * P:(m + 1) * P],
                                                     xT[:, k, c * CH:(c + 1) * CH], start=(k == 0), stop=(k == KD - 1))
                                last.then_inc(S["hp"], 1)

                        def down(c):
                            pe.wait_ge(S["g"], e * HPE + (c + 1) * KD + 1)
                            for w in range(2):
                                o = c * 2 + w
                                pe.wait_ge(S["acc"], (e * CHUNKS + c) * 4 + 2 * w + 1)
                                for j in (2 * w, 2 * w + 1):
                                    for k in range(KD):
                                        last = pe.matmul(OP[o % 4][:, j % 2], act_[:, c % 2, k, j * P:(j + 1) * P],
                                                         w2[:, par, k, :], start=(k == 0), stop=(k == KD - 1))
                                last.then_inc(S["o"], 1)
                            if c == CHUNKS - 1:
                                last2 = None
                        up(0)
                        for c in range(CHUNKS):
                            if c + 1 < CHUNKS:
                                up(c + 1)
                            down(c)
                        pe.matmul(HP[2][:, 0:1], ident[:], ones[:], start=True, stop=True).then_inc(S["w1u"], 1)

            @block.scalar
            def _(act):
                act.sem_inc(S["mrc"], 1)
                act.sem_inc(S["g"], 1)
                with act.Fori(0, PAIRS) as r:
                    for par in range(2):
                        e = r * 2 + par
                        act.activation(b1e[:, par], b1[:, :, bass.ds(e, 1)].rearrange("p k a -> p (k a)"),
                                       ACT.Copy).then_inc(S["b1c"], 1)
                        act.wait_ge(S["b1c"], e + 1)
                        for c in range(CHUNKS):
                            act.wait_ge(S["mr"], e * CHUNKS + c + 1)
                            act.activation(mrow[:, par, c * CH:(c + 1) * CH], MR[:], ACT.Copy).then_inc(S["mrc"], 1)
                        for c in range(CHUNKS):
                            for m in range(KD):
                                i = c * KD + m
                                act.wait_ge(S["hm"], e * HPE + i + 3)
                                act.wait_ge(S["o"], OB + e * CHUNKS * 2 + 2 * (c - 2) + 2) if c >= 2 else act.wait_ge(S["o"], OB + e * CHUNKS * 2)
                                act.activation(act_[:, c % 2, m], hid[:, c % 2, m], ACT.Gelu,
                                               bias=b1e[:, par, m:m + 1]).then_inc(S["g"], 1)
                act.wait_ge(S["ve"], 1)
                act.activation(rstd[:], rstd[:], ACT.Ln).then_inc(S["rs"], 1)
                act.wait_ge(S["rs"], 1)
                act.activation(rstd[:], rstd[:], ACT.Exp, scale=-0.5).then_inc(S["rs"], 1)

            @block.vector
            def _(dve):
                dve.sem_inc(S["hm"], 2)
                dve.sem_inc(S["acc"], 8)
                with dve.Fori(0, PAIRS) as r:
                    for par in range(2):
                        e = r * 2 + par

                        def scale(c):
                            for m in range(KD):
                                i = c * KD + m
                                dve.wait_ge(S["hp"], e * HPE + i + 1)
                                if m == 0:
                                    dve.wait_ge(S["mrc"], e * CHUNKS + CHUNKS + 1)
                                if i >= 4:
                                    dve.wait_ge(S["g"], e * HPE + i - 2)
                                else:
                                    dve.wait_ge(S["g"], e * HPE + 1)
                                dve.tensor_tensor(hid[:, c % 2, m], HP[i % 2][:], mrow[:, par, c * CH:(c + 1) * CH],
                                                  ALU.mult).then_inc(S["hm"], 1)

                        def gather(c):
                            for w in range(2):
                                o = c * 2 + w
                                dve.wait_ge(S["o"], OB + (e * CHUNKS + c) * 2 + w + 1)
                                for j in (2 * w, 2 * w + 1):
                                    t = c * CT + j
                                    dve.wait_ge(S["acc"], e * TILES + 8)
                                    dve.scalar_tensor_tensor(x[:, t, :], OP[o % 4][:, j % 2], mask[:, t, bass.ds(e, 1)],
                                                             x[:, t, :], ALU.mult, ALU.add).then_inc(S["acc"], 1)
                        scale(0)
                        for c in range(CHUNKS):
                            if c + 1 < CHUNKS:
                                scale(c + 1)
                            gather(c)
                dve.wait_ge(S["acc"], EXP * TILES + 8)
                for j in range(TILES):
                    dve.bn_stats(stats[:, j, :], x[:, j, :]).then_inc(S["fin"], 1)
                dve.wait_ge(S["fin"], TILES // 2 + TILES)
                for j in range(TILES):
                    dve.bn_aggr(mv[:, j, :], stats[:, j, :]).then_inc(S["fin"], 1)
                dve.wait_ge(S["fin"], TILES // 2 + 2 * TILES)
                dve.tensor_scalar(rstd[:], mv[:, :, 1], EPS, None, ALU.add).then_inc(S["ve"], 1)
                dve.wait_ge(S["rs"], 2)
                for j in range(TILES):
                    dve.tensor_scalar(x[:, j, :], x[:, j, :], mv[:, j, 0:1], rstd[:, j:j + 1],
                                      ALU.subtract, ALU.mult).then_inc(S["out"], 1)


def layout(I, np):
    ONE = 0x3F80
    g = lambda n: np.asarray(I[n])
    parts = lambda a, k: np.ascontiguousarray(a.reshape(k, P, -1).transpose(1, 0, 2))
    out = {}
    out["x"] = g("x").reshape(TILES, P, DM).transpose(1, 0, 2)
    out["ident"] = np.eye(P, dtype=np.float32)
    pick = np.zeros((3, 2 * DS, 2 * DS, P), np.uint16)
    for r in range(2 * DS):
        pick[:, r, r, :] = ONE
    out["pick"] = pick.reshape(96, 2 * DS, P)
    out["lnw"] = np.stack([g("L0_attn_ln_w"), g("L0_attn_ln_b")], 1).reshape(LAYERS, 2, KD, P).transpose(3, 0, 1, 2)
    cw = g("L0_attn_conv_w").transpose(0, 2, 1)
    ch = np.concatenate([g("L0_attn_conv_b")[:, None], g("L0_attn_dt_proj_b")[:, None], g("L0_attn_D_skip")[:, None], cw], 1)
    out["chan"] = ch.reshape(LAYERS, 3 + TAPS, M, P).transpose(3, 0, 1, 2)
    out["alog"] = g("L0_attn_A_log").reshape(LAYERS, M, P, DS).transpose(2, 0, 1, 3)
    out["inw"] = np.stack([parts(g("L0_attn_in_proj_w")[l].T, KD) for l in range(LAYERS)])
    xw = g("L0_attn_x_proj_w")
    xw = np.concatenate([xw[:, RANK:]] * 3 + [xw[:, :RANK]], 1)
    out["xpw"] = np.stack([parts(xw[l].T, M) for l in range(LAYERS)])
    out["dtw"] = g("L0_attn_dt_proj_w").transpose(0, 2, 1)
    out["outw"] = np.stack([parts(g("L0_attn_out_proj_w")[l].T, M) for l in range(LAYERS)])
    QH, KVH, HD = HEADS, KV, HDIM
    out["nf"] = np.concatenate([g("L0_attn_norm_f_w"), g("L0_attn_norm_f_b")])[None]
    out["xn_wb"] = np.concatenate([g("L0_xattn_gamma"), g("L0_xattn_beta")])[None]
    out["ctxT"] = g("ctx_1024").reshape(BATCH, SEQ, KD, P).transpose(0, 3, 2, 1)
    out["wq"] = parts(g("L0_xattn_Wq").T, KD)
    out["wkv"] = parts(np.concatenate([g("L0_xattn_Wk"), g("L0_xattn_Wv")]).T, KD)
    out["bqkv"] = np.concatenate([g("L0_xattn_bq"), g("L0_xattn_bk"), g("L0_xattn_bv")])[None]

    def rope(d, scale):
        theta = (1.0 / 10000.0 ** (np.arange(0, d, 2, dtype=np.float32) / np.float32(d))).astype(np.float32)
        a = np.arange(BATCH, dtype=np.float32)[:, None] * theta[None]
        a = np.concatenate([a, a], -1)[:, :, None]
        sign = np.where(np.arange(HD) < HD - d // 2, -1.0, 1.0).astype(np.float32)
        c = np.broadcast_to(np.cos(a) * np.float32(scale), (BATCH, d, HD))
        return [c.reshape(BATCH, -1), (np.sin(a) * np.float32(scale) * sign).reshape(BATCH, -1)]
    out["rope"] = np.concatenate(rope(QH, HD ** -0.5) + rope(KVH, 1.0), 1).astype(np.float32).reshape(1, -1)
    out["rw"] = parts(g("L0_ffn_router_w"), KD)
    out["rb"] = g("L0_ffn_router_b")[None]
    out["w1"] = g("L0_ffn_w1").reshape(EXP, KD, P, DM).transpose(0, 2, 1, 3)
    out["w2"] = g("L0_ffn_w2").reshape(EXP, KD, P, DM).transpose(0, 2, 1, 3)
    out["b1"] = g("L0_ffn_b1").reshape(EXP, KD, P).transpose(2, 1, 0)
    out["b2"] = g("L0_ffn_b2")
    pe = np.zeros((96, EXP, P), np.uint16)
    for e in range(EXP):
        pe[[e, 32 + e, 64 + e], e, :] = ONE
    out["picke"] = pe
    out["identb"] = np.where(np.eye(P) > 0, ONE, 0).astype(np.uint16)
    out["iota"] = np.arange(EXP, dtype=np.float32)[None]
    return {k: np.ascontiguousarray(v) for k, v in out.items()}


def kernel(**inputs):
    import numpy as np
    import concourse.bacc as bacc
    from concourse.bass_utils import run_bass_kernel_spmd as run

    nc = bacc.Bacc("TRN2", target_bir_lowering=False, num_devices=1)
    arrays, A = {}, {}
    for name, a in layout(inputs, np).items():
        arrays["in_" + name] = a
        A[name] = nc.dram_tensor("in_" + name, a.shape, mybir.dt.from_np(a.dtype), kind="ExternalInput").ap()
    A["out"] = nc.dram_tensor("out", (P, TILES, DM), mybir.dt.float32, kind="ExternalOutput").ap()
    build(nc, A)
    got = run(nc, [arrays], core_ids=[0]).results[0]["out"]
    return np.ascontiguousarray(got.transpose(1, 0, 2)).reshape(BATCH, SEQ, DM)
```

```python
import concourse.bass as bass
from concourse import mybir
from contextlib import ExitStack

P = 128
BATCH, SEQ, DM = 8, 256, 256
TOK = BATCH * SEQ
TILES = TOK // P
KD = DM // P
LAYERS, DI, DS, RANK, TAPS = 2, 512, 16, 16, 4
M = DI // P
SB = 2
SEG = SB * SEQ
SEGS = BATCH // SB
ST = SEG // P
PAD = TAPS - 1
XPR = 3 * 2 * DS + RANK
EPS = 1e-5


AT = dict(statistics=0, rstd=2, normalise=1, residual=2, out_proj=0, transposes=2, norm_weights=5,
          in_proj=(3, 4, 5, 6), take=(6, 7, 8, 9), tap0=(7, 8), taps=(7, 8, 9), silus=11, x_proj=9, rows=12,
          split=11, dt_proj=(10, 11, 11, 12), dt_parts=(13, 14, 14, 15), small_exp=15, plus_one=14, logs=15,
          softplus=15, dt_x=15)


def build(nc, A):
    fp32 = mybir.dt.float32
    with ExitStack() as ctx:
        x = ctx.enter_context(nc.sbuf_tensor("x", [P, TILES, DM], fp32))
        ident = ctx.enter_context(nc.sbuf_tensor("ident", [P, P], fp32))
        mamba(nc, A, x, ident)
        if A.get("stop") is None:
            blend(nc, A, x, "norm_f", "x", None)
            attention(nc, A, x, ident)
            moe(nc, A, x, ident)
        else:
            with nc.semaphore("dbg") as d, nc.Block() as block:
                @block.sync
                def _(sp):
                    sp.dma_start(A["out"], x[:]).then_inc(d, 16)
                    sp.wait_ge(d, 16)


def mamba(nc, A, x, ident):
    fp32, bf16 = mybir.dt.float32, mybir.dt.bfloat16
    ALU, ACT = mybir.AluOpType, mybir.ActivationFunctionType
    with ExitStack() as ctx:
        def sb(name, shape, dt=fp32):
            return ctx.enter_context(nc.sbuf_tensor(name, shape, dt))

        def pb(name, shape):
            return ctx.enter_context(nc.psum_tensor(name, shape, fp32))

        pick = sb("pick", [96, 2 * DS, P], bf16)
        inw = [sb(f"inw{l}", [P, KD, 2 * DI]) for l in range(LAYERS)]
        xpw = [sb(f"xpw{l}", [P, M, XPR]) for l in range(LAYERS)]
        dtw = [sb(f"dtw{l}", [P, DI]) for l in range(LAYERS)]
        outw = [sb(f"outw{l}", [P, M, DM]) for l in range(LAYERS)]
        lnw = sb("lnw", [P, LAYERS, 2, KD])
        chan = sb("chan", [P, LAYERS, 3 + TAPS, M])
        nega = sb("nega", [P, LAYERS, M, DS])
        skip = sb("skip", [P, LAYERS, M, P])
        stats = sb("stats", [P, ST, 6])
        mv = sb("mv", [P, ST, 2])
        vare = sb("vare", [P, ST])
        rstd = sb("rstd", [P, ST])
        xp = sb("xp", [P, M, SB, PAD + SEQ])
        cv = sb("cv", [P, M, SEG])
        zs = sb("zs", [P, 2, M, SEG])
        xc = sb("xc", [P, M, SEG])
        bc = sb("bc", [96, 2, SEG], bf16)
        low = sb("low", [P, SEG])
        bcr, dr = low[0:64, :], low[96:96 + RANK, :]
        dt = sb("dt", [P, 2, M, SEG])
        du = sb("du", [P, 2, M, SEG])
        soft = sb("soft", [P, M, SEG])
        xn = soft[:, 0:2].rearrange("p m (j d) -> p (m j) d", d=DM)
        hT = soft[:, 2:4]
        brow = sb("brow", [P, 2, SEG])
        dA = sb("dA", [P, 2, M, SEG])
        dBu = sb("dBu", [P, 2, M, SEG])
        h = sb("h", [P, M, SEG])
        hC = sb("hC", [P, 2, M, SEG])
        yz = cv
        lnu = xp[:, :, :, PAD:].rearrange("p m b t -> p (m b) t")
        pairs = lambda t: t.rearrange("p m (b t) -> p (m b) t", b=SB)
        Y = pb("Y", [P, M, SEG])
        Bp, Cp = pb("Bp", [P, SEG]), pb("Cp", [P, SEG])
        W = [pb(f"W{i}", [P, SEG]) for i in range(2)]

        S = {n: ctx.enter_context(nc.semaphore(n)) for n in """x_in w_in start own_v diag ve rstd_ready xn_ready tp
            hT_ready ip ip_used tap0 conv xc_ready zs_ready dbl hi r1 mid lo dr_ready dtp dtp_used expn one lnu_ready
            dtd dud b_ready b_copied c_ready expd dbud scan_done hc_done y_done y_init yzd op res gate""".split()}
        LW, LB = 0, 1
        CB, DTB, DSK, CW = 0, 1, 2, 3
        WEIGHTS = 16 * (4 + 4 * LAYERS)
        UNITS = LAYERS * SEGS

        def after(eng, name, value):
            if not isinstance(value, int) or value > 0:
                eng.wait_ge(S[name], value)

        def gate(eng):
            eng.sem_inc(S["gate"], 1)

        def units(eng, prologue, scan, epilogue):
            prologue(0, 0, 0)
            for l in range(LAYERS):
                scan(l, 0, l * SEGS, (l, 1, l * SEGS + 1))
                with eng.Fori(1, SEGS - 1) as s:
                    scan(l, s, s + l * SEGS, (l, s + 1, s + (l * SEGS + 1)))
                scan(l, SEGS - 1, (l + 1) * SEGS - 1, (l + 1, 0, (l + 1) * SEGS) if l + 1 < LAYERS else None)
            epilogue(LAYERS - 1, SEGS - 1, UNITS)

        block = ctx.enter_context(nc.Block())

        @block.sync
        def _(sp):
            def load(dst, src, s="w_in"):
                sp.dma_start(dst, src).then_inc(S[s], 16)
            load(x[:], A["x"], "x_in")
            load(ident[:], A["ident"], "x_in")
            load(lnw[:], A["lnw"])
            load(chan[:], A["chan"])
            load(nega[:], A["alog"])
            load(pick[:], A["pick"].bitcast(bf16))
            for l in range(LAYERS):
                load(inw[l][:], A["inw"][l])
                load(xpw[l][:], A["xpw"][l])
                load(dtw[l][96:96 + RANK, :], A["dtw"][l])
                load(outw[l][:], A["outw"][l])

        @block.vector
        def _(dve):
            K = 2 * ST + 1 + M * (TAPS - 2) + 3
            START = 1
            dve.memset(xp[:], 0.0).then_inc(S["start"], 1)
            dve.memset(dA[:], 0.0).then_inc(S["start"], 1)
            dve.wait_ge(S["w_in"], WEIGHTS)
            dve.wait_ge(S["start"], 3)
            dve.tensor_scalar(nega[:], nega[:], -1.0, None, ALU.mult).then_inc(S["start"], 1)
            dve.memset(vare[:], 0.0).then_inc(S["own_v"], 1)
            dve.wait_ge(S["x_in"], 32)
            for l in range(LAYERS):
                for m in range(M):
                    dve.tensor_scalar(skip[:, l, m], ident[:], chan[:, l, DSK, m:m + 1], None, ALU.mult).then_inc(S["diag"], 1)

            def held(v, n):
                dve.wait_ge(S["own_v"], v * K + START + n)

            def statistics(l, s, v):
                held(v, 0)
                after(dve, "res", (v - SEGS + 1) * 2 if l else 0)
                dve.memset(vare[:], 0.0).then_inc(S["own_v"], 1)
                for j in range(ST):
                    dve.bn_stats(stats[:, j, :], x[:, s * ST + j, :]).then_inc(S["own_v"], 1)
                held(v, 1 + ST)
                dve.memset(rstd[:], 0.0).then_inc(S["gate"], 1)
                for j in range(ST):
                    dve.bn_aggr(mv[:, j, :], stats[:, j, :]).then_inc(S["own_v"], 1)
                held(v, 1 + 2 * ST)
                dve.tensor_scalar(vare[:], mv[:, :, 1], EPS, None, ALU.add).then_inc(S["ve"], 1)

            def normalise(l, s, v):
                dve.wait_ge(S["rstd_ready"], v * 2 + 2)
                after(dve, "tp", v * KD)
                for j in range(ST):
                    dve.tensor_scalar(xn[:, j, :], x[:, s * ST + j, :], mv[:, j, 0:1], rstd[:, j:j + 1],
                                      ALU.subtract, ALU.mult).then_inc(S["xn_ready"], 1)

            def tap(l, v, t):
                for m in range(M):
                    cvm = cv[:, m].rearrange("p (b t) -> p b t", b=SB)
                    if t == 1:
                        dve.wait_ge(S["tap0"], v * M + m + 1)
                    else:
                        held(v, 1 + 2 * ST + M * (t - 2) + m + 1)
                    ins = dve.scalar_tensor_tensor(cvm, xp[:, m, :, t:t + SEQ], chan[:, l, CW + t, m:m + 1], cvm,
                                                   ALU.mult, ALU.add)
                    ins.then_inc(S["own_v" if t < TAPS - 1 else "conv"], 1)

            def split(v, par):
                dve.wait_ge(S["hi"], v + 1)
                dve.tensor_tensor(bcr, W[0][0:64, :], bc[0:64, par, :], ALU.subtract).then_inc(S["r1"], 1)
                dve.wait_ge(S["r1"], v + 1)
                dve.tensor_scalar(bc[0:64, par, :], bcr, 1.0, None, ALU.mult).then_inc(S["mid"], 1)
                dve.wait_ge(S["mid"], v + 1)
                dve.tensor_tensor(bc[0:32, par, :], low[0:32, :], bc[0:32, par, :], ALU.subtract).then_inc(S["lo"], 1)

            def plus_one(v):
                dve.wait_ge(S["expn"], v + 1)
                dve.tensor_scalar(cv[:], soft[:], 1.0, None, ALU.add).then_inc(S["one"], 1)

            def softplus(v, par):
                n = 1 + 2 * ST + M * (TAPS - 2)
                dve.wait_ge(S["one"], v + 1)
                dve.scalar_tensor_tensor(soft[:], cv[:], 1.0, soft[:], ALU.subtract, ALU.subtract).then_inc(S["own_v"], 1)
                held(v, n + 1)
                dve.tensor_tensor(dt[:, par], dt[:, par], soft[:], ALU.subtract).then_inc(S["own_v"], 1)
                held(v, n + 2)
                dve.wait_ge(S["lnu_ready"], v + 1)
                dve.scalar_tensor_tensor(pairs(soft[:]), pairs(cv[:]), 1.0, lnu, ALU.is_gt, ALU.mult).then_inc(S["own_v"], 1)
                held(v, n + 3)
                dve.tensor_tensor(dt[:, par], dt[:, par], soft[:], ALU.add).then_inc(S["dtd"], 1)

            def residual(l, s, u):
                for w in range(2):
                    dve.wait_ge(S["op"], (u - 1) * 2 + w + 1)
                    xs = x[:, bass.ds(s * ST + 2 * w, 2), :]
                    dve.tensor_tensor(xs, xs, W[w][:].rearrange("p (j d) -> p j d", j=2), ALU.add).then_inc(S["res"], 1)

            def step(u, n):
                g = u * DS + n
                b = n % 2
                flat = lambda t: t.rearrange("p m t -> p (m t)")
                dve.wait_ge(S["expd"], g + 1)
                dve.wait_ge(S["dbud"], g + 1)
                after(dve, "hc_done", g)
                dve.tensor_tensor_scan(flat(h[:]), flat(dA[:, b]), flat(dBu[:, b]), 0.0,
                                       ALU.mult, ALU.add).then_inc(S["scan_done"], 1)
                dve.wait_ge(S["scan_done"], g + 1)
                dve.wait_ge(S["c_ready"], g + 1)
                after(dve, "y_done", g - 1)
                dve.tensor_tensor(hC[:, b], h[:], Cp[:].unsqueeze(1).broadcast_to([P, M, SEG]),
                                  ALU.mult).then_inc(S["hc_done"], 1)

            def prologue(l, s, v):
                statistics(l, s, v)
                normalise(l, s, v)
                for t in range(1, TAPS):
                    tap(l, v, t)
                split(v, v % 2)
                plus_one(v)
                softplus(v, v % 2)

            def scan(l, s, u, nxt):
                for n in range(DS):
                    step(u, n)
                    if n == AT["residual"] and not isinstance(u, int) or n == AT["residual"] and u > 0:
                        residual(l, (s + SEGS - 1) % SEGS, u)
                    if nxt is None:
                        continue
                    nl, ns, v = nxt
                    if n == AT["statistics"]:
                        statistics(nl, ns, v)
                    if n == AT["normalise"]:
                        normalise(nl, ns, v)
                    if n in AT["taps"]:
                        tap(nl, v, 1 + AT["taps"].index(n))
                    if n == AT["split"]:
                        split(v, ns % 2)
                    if n == AT["plus_one"]:
                        plus_one(v)
                    if n == AT["softplus"]:
                        softplus(v, ns % 2)
                dve.wait_ge(S["y_done"], (u + 1) * DS)
                dve.tensor_tensor(yz[:], Y[:], zs[:, s % 2], ALU.mult).then_inc(S["yzd"], 1)

            units(dve, prologue, scan, residual)

        @block.scalar
        def _(act):
            act.wait_ge(S["w_in"], WEIGHTS)
            act.activation(nega[:], nega[:], ACT.Exp).then_inc(S["start"], 1)
            act.wait_ge(S["start"], 4)

            def rstd_of(v):
                act.wait_ge(S["ve"], v + 1)
                act.activation(vare[:], vare[:], ACT.Ln).then_inc(S["rstd_ready"], 1)
                act.wait_ge(S["rstd_ready"], v * 2 + 1)
                act.activation(rstd[:], vare[:], ACT.Exp, scale=-0.5).then_inc(S["rstd_ready"], 1)

            def norm_weights(l, v):
                after(act, "ip", v * 2 * M)
                for k in range(KD):
                    act.wait_ge(S["tp"], v * KD + k + 1)
                    act.activation(hT[:, k, :], W[k][:], ACT.Identity, scale=lnw[:, l, LW, k:k + 1],
                                   bias=lnw[:, l, LB, k:k + 1]).then_inc(S["hT_ready"], 1)

            def take(v, m, par):
                act.wait_ge(S["ip"], v * 2 * M + m + 1)
                if m < M:
                    after(act, "dtd", v)
                    act.activation(xp[:, m, :, PAD:], W[m % 2][:].rearrange("p (b t) -> p b t", b=SB),
                                   ACT.Copy).then_inc(S["ip_used"], 1)
                else:
                    after(act, "yzd", v - 1)
                    gate(act)
                    act.activation(zs[:, par, m - M, :], W[m % 2][:], ACT.Copy).then_inc(S["ip_used"], 1)

            def silus(v, par):
                after(act, "y_init", v)
                after(act, "dud", v)
                for m in range(M):
                    act.wait_ge(S["conv"], v * M + m + 1)
                    act.activation(xc[:, m, :], cv[:, m, :], ACT.Silu).then_inc(S["xc_ready"], 1)
                act.wait_ge(S["ip_used"], (v + 1) * 2 * M)
                gate(act)
                act.activation(zs[:, par], zs[:, par], ACT.Silu).then_inc(S["zs_ready"], 1)

            def rows(v, par):
                act.wait_ge(S["dbl"], v + 1)
                after(act, "c_ready", (v - 1) * DS)
                gate(act)
                act.activation(bc[:, par, :], W[0][0:96, :], ACT.Copy).then_inc(S["hi"], 1)
                act.activation(dr, W[0][96:96 + RANK, :], ACT.Copy).then_inc(S["dr_ready"], 1)

            def dt_parts(l, v, m, par):
                act.wait_ge(S["dtp"], v * M + m + 1)
                bias = chan[:, l, DTB, m:m + 1]
                gate(act)
                act.activation(soft[:, m, :], W[(m + 1) % 2][:], ACT.Abs, bias=bias)
                act.activation(dt[:, par, m, :], W[(m + 1) % 2][:], ACT.Relu, bias=bias).then_inc(S["dtp_used"], 1)

            def small_exp(v):
                act.wait_ge(S["dtp_used"], (v + 1) * M)
                act.activation(soft[:], soft[:], ACT.Exp, scale=-1.0).then_inc(S["expn"], 1)

            def logs(v):
                act.wait_ge(S["one"], v + 1)
                act.activation(lnu, pairs(cv[:]), ACT.Ln).then_inc(S["lnu_ready"], 1)

            def step(l, u, n, par):
                g = u * DS + n
                act.wait_ge(S["b_ready"], g + 1)
                after(act, "scan_done", g - 1)
                act.activation(brow[:, n % 2, :], Bp[:], ACT.Copy).then_inc(S["b_copied"], 1)
                for m in range(M):
                    first = lambda t: t.rearrange("p (b t) -> p b t", b=SB)[:, :, 1:]
                    ins = act.activation(first(dA[:, n % 2, m, :]), first(dt[:, par, m, :]), ACT.Exp,
                                         scale=nega[:, l, m, n:n + 1])
                ins.then_inc(S["expd"], 1)

            def prologue(l, s, v):
                rstd_of(v)
                norm_weights(l, v)
                for m in range(2 * M):
                    take(v, m, v % 2)
                silus(v, v % 2)
                rows(v, v % 2)
                for m in range(M):
                    dt_parts(l, v, m, v % 2)
                small_exp(v)
                logs(v)

            def scan(l, s, u, nxt):
                act.wait_ge(S["dtd"], u + 1)
                for n in range(DS):
                    step(l, u, n, s % 2)
                    if nxt is None:
                        continue
                    nl, ns, v = nxt
                    par = ns % 2
                    if n == AT["rstd"]:
                        rstd_of(v)
                    if n == AT["norm_weights"]:
                        norm_weights(nl, v)
                    if n in AT["take"]:
                        for m in range(2):
                            take(v, 2 * AT["take"].index(n) + m, par)
                    if n == AT["silus"]:
                        silus(v, par)
                    if n == AT["rows"]:
                        rows(v, par)
                    for m in range(M):
                        if n == AT["dt_parts"][m]:
                            dt_parts(nl, v, m, par)
                    if n == AT["small_exp"]:
                        small_exp(v)
                    if n == AT["logs"]:
                        logs(v)

            units(act, prologue, scan, lambda *a: None)

        @block.gpsimd
        def _(pool):
            def tap0(l, v, ms):
                after(pool, "op", (v - 1) * 2)
                for m in ms:
                    pool.wait_ge(S["ip_used"], v * 2 * M + m + 1)
                    gate(pool)
                    pool.tensor_scalar(cv[:, m].rearrange("p (b t) -> p b t", b=SB), xp[:, m, :, 0:SEQ],
                                       chan[:, l, CW, m:m + 1], chan[:, l, CB, m:m + 1],
                                       ALU.mult, ALU.add).then_inc(S["tap0"], 1)

            def dt_x(v, par):
                pool.wait_ge(S["dtd"], v + 1)
                pool.wait_ge(S["xc_ready"], (v + 1) * M)
                gate(pool)
                pool.tensor_tensor(du[:, par], dt[:, par], xc[:], ALU.mult).then_inc(S["dud"], 1)

            def step(u, n, par):
                g = u * DS + n
                pool.wait_ge(S["b_copied"], g + 1)
                pool.wait_ge(S["dud"], u + 1)
                after(pool, "scan_done", g - 1)
                gate(pool)
                pool.tensor_tensor(dBu[:, n % 2], du[:, par], brow[:, n % 2].unsqueeze(1).broadcast_to([P, M, SEG]),
                                   ALU.mult).then_inc(S["dbud"], 1)

            def prologue(l, s, v):
                tap0(l, v, range(M))
                dt_x(v, v % 2)

            def scan(l, s, u, nxt):
                for n in range(DS):
                    step(u, n, s % 2)
                    if nxt is None:
                        continue
                    nl, ns, v = nxt
                    if n in AT["tap0"]:
                        i = AT["tap0"].index(n)
                        tap0(nl, v, (2 * i, 2 * i + 1))
                    if n == AT["dt_x"]:
                        dt_x(v, ns % 2)

            pool.wait_ge(S["w_in"], WEIGHTS)
            pool.wait_ge(S["start"], 1)
            units(pool, prologue, scan, lambda *a: None)

        @block.tensor
        def _(pe):
            pe.wait_ge(S["w_in"], WEIGHTS)
            pe.wait_ge(S["x_in"], 32)
            pe.wait_ge(S["diag"], LAYERS * M)

            def transposes(v):
                pe.wait_ge(S["xn_ready"], (v + 1) * ST)
                after(pe, "res", (v - 1) * 2)
                for k in range(KD):
                    for j in range(ST):
                        ins = pe.transpose(W[k][:, j * P:(j + 1) * P], xn[:, j, k * P:(k + 1) * P], ident[:])
                    ins.then_inc(S["tp"], 1)

            def in_proj(l, v, m):
                if m < 2:
                    pe.wait_ge(S["hT_ready"], (v + 1) * KD)
                else:
                    pe.wait_ge(S["ip_used"], v * 2 * M + m - 1)
                for k in range(KD):
                    ins = pe.matmul(W[m % 2][:], inw[l][:, k, m * P:(m + 1) * P], hT[:, k, :],
                                    start=(k == 0), stop=(k == KD - 1))
                ins.then_inc(S["ip"], 1)

            def x_proj(l, v):
                pe.wait_ge(S["ip_used"], (v + 1) * 2 * M)
                for m in range(M):
                    pe.wait_ge(S["xc_ready"], v * M + m + 1)
                    ins = pe.matmul(W[0][0:XPR, :], xpw[l][:, m, :], xc[:, m, :], start=(m == 0), stop=(m == M - 1))
                ins.then_inc(S["dbl"], 1)

            def dt_proj(l, v, m):
                if m == 0:
                    pe.wait_ge(S["dr_ready"], v + 1)
                elif m == 1:
                    pe.wait_ge(S["r1"], v + 1)
                else:
                    pe.wait_ge(S["dtp_used"], v * M + m - 1)
                pe.matmul(W[(m + 1) % 2][:], dtw[l][96:96 + RANK, m * P:(m + 1) * P], dr,
                          start=True, stop=True).then_inc(S["dtp"], 1)

            def out_proj(l, u):
                pe.wait_ge(S["yzd"], u)
                after(pe, "dtp_used", (u + 1) * M if not isinstance(u, int) or u < UNITS else UNITS * M)
                for j in range(ST):
                    for m in range(M):
                        ins = pe.matmul(W[j // 2][:, (j % 2) * DM:(j % 2 + 1) * DM], yz[:, m, j * P:(j + 1) * P],
                                        outw[l][:, m, :], start=(m == 0), stop=(m == M - 1))
                    if j % 2:
                        ins.then_inc(S["op"], 1)

            def row_b(u, n, par):
                g = u * DS + n
                pe.wait_ge(S["lo"], u + 1)
                after(pe, "b_copied", g)
                pe.matmul(Bp[:], pick[:, n, :], bc[:, par, :], start=True, stop=True).then_inc(S["b_ready"], 1)

            def row_c(u, n, par):
                g = u * DS + n
                after(pe, "hc_done", g)
                pe.matmul(Cp[:], pick[:, DS + n, :], bc[:, par, :], start=True, stop=True).then_inc(S["c_ready"], 1)

            def skips(l, u):
                after(pe, "yzd", u)
                pe.wait_ge(S["xc_ready"], (u + 1) * M)
                for m in range(M):
                    ins = pe.matmul(Y[:, m], skip[:, l, m, :], xc[:, m, :], start=True, stop=False)
                ins.then_inc(S["y_init"], 1)

            def add(u, n):
                pe.wait_ge(S["hc_done"], u * DS + n + 1)
                for m in range(M):
                    ins = pe.matmul(Y[:, m], ident[:], hC[:, n % 2, m], start=False, stop=(n == DS - 1))
                ins.then_inc(S["y_done"], 1)

            def prologue(l, s, v):
                transposes(v)
                for m in range(2 * M):
                    in_proj(l, v, m)
                x_proj(l, v)
                for m in range(M):
                    dt_proj(l, v, m)

            def scan(l, s, u, nxt):
                row_b(u, 0, s % 2)
                row_c(u, 0, s % 2)
                row_b(u, 1, s % 2)
                skips(l, u)
                for n in range(DS):
                    if n + 2 < DS:
                        row_b(u, n + 2, s % 2)
                    if n + 1 < DS:
                        row_c(u, n + 1, s % 2)
                    add(u, n)
                    if n == AT["out_proj"] and (not isinstance(u, int) or u > 0):
                        out_proj(l if not isinstance(s, int) or s > 0 else l - 1, u)
                    if nxt is None:
                        continue
                    nl, ns, v = nxt
                    if n == AT["transposes"]:
                        transposes(v)
                    if n in AT["in_proj"]:
                        for m in range(2):
                            in_proj(nl, v, 2 * AT["in_proj"].index(n) + m)
                    if n == AT["x_proj"]:
                        x_proj(nl, v)
                    for m in range(M):
                        if n == AT["dt_proj"][m]:
                            dt_proj(nl, v, m)

            units(pe, prologue, scan, lambda l, s, u: out_proj(l, u))


HEADS, KV, HDIM = 16, 4, 16
GRP = HEADS // KV
SLOT = 32
EXP, TOP = 8, 2
CAPACITY = float(max(int(TOK * 1.25 / EXP), 4))


def wide(ap, shape):
    return ap.broadcast_to(shape)


def blend(nc, A, x, name, res, add):
    fp32 = mybir.dt.float32
    ALU, ACT = mybir.AluOpType, mybir.ActivationFunctionType
    with ExitStack() as ctx:
        sb = lambda n, shape: ctx.enter_context(nc.sbuf_tensor(name + n, shape, fp32))
        sem = lambda n: ctx.enter_context(nc.semaphore(name + "_" + n))
        wb = sb("wb", [P, 2, DM])
        if add is None:
            r = sb("r", [P, TILES, DM])
            v = x
        else:
            r = x
            v = add
        stats = sb("stats", [P, TILES, 6])
        mv = sb("mv", [P, TILES, 2])
        rstd = sb("rstd", [P, TILES])
        inp, var, rs, own = sem("inputs"), sem("variance"), sem("rstd"), sem("vector")
        block = ctx.enter_context(nc.Block())

        @block.sync
        def _(sp):
            src = A["nf"] if add is None else A["xn_wb"]
            sp.dma_start(wb[:].rearrange("p a d -> p (a d)"), src.broadcast_to([P, 2 * DM])).then_inc(inp, 16)
            if add is None:
                sp.dma_start(r[:], A["x"]).then_inc(inp, 16)
        N_IN = 32 if add is None else 16

        @block.scalar
        def _(act):
            for rnd in range(2):
                act.wait_ge(var, rnd + 1)
                act.activation(rstd[:], rstd[:], ACT.Ln).then_inc(rs, 1)
                act.wait_ge(rs, 2 * rnd + 1)
                act.activation(rstd[:], rstd[:], ACT.Exp, scale=-0.5).then_inc(rs, 1)

        @block.vector
        def _(dve):
            n = [0]

            def mark(ins):
                ins.then_inc(own, 1)
                n[0] += 1

            def held():
                dve.wait_ge(own, n[0])

            def norm(t, rnd):
                for j in range(TILES):
                    mark(dve.bn_stats(stats[:, j, :], t[:, j, :]))
                held()
                for j in range(TILES):
                    mark(dve.bn_aggr(mv[:, j, :], stats[:, j, :]))
                held()
                dve.tensor_scalar(rstd[:], mv[:, :, 1], EPS, None, ALU.add).then_inc(var, 1)
                dve.wait_ge(rs, 2 * rnd + 2)
                for j in range(TILES):
                    mark(dve.tensor_scalar(t[:, j, :], t[:, j, :], mv[:, j, 0:1], rstd[:, j:j + 1],
                                           ALU.subtract, ALU.mult))
                held()
            norm(v, 0)
            dve.wait_ge(inp, N_IN)
            mark(dve.tensor_tensor(v[:], v[:], wb[:, 0].unsqueeze(1).broadcast_to([P, TILES, DM]), ALU.mult))
            held()
            mark(dve.tensor_tensor(v[:], v[:], wb[:, 1].unsqueeze(1).broadcast_to([P, TILES, DM]), ALU.add))
            held()
            mark(dve.tensor_tensor(x[:], v[:], r[:], ALU.add))
            held()
            norm(x, 1)


def attention(nc, A, x, ident):
    fp32, bf16 = mybir.dt.float32, mybir.dt.bfloat16
    ALU, ACT, AX = mybir.AluOpType, mybir.ActivationFunctionType, mybir.AxisListType
    HW = HEADS * HDIM
    KW = KV * HDIM
    BT = SEQ // P
    UNITS = KV * GRP // 2
    with ExitStack() as outer:
        att = outer.enter_context(nc.sbuf_tensor("att", [P, TILES, DM], fp32))
        with ExitStack() as ctx:
            sb = lambda n, shape: ctx.enter_context(nc.sbuf_tensor("at_" + n, shape, fp32))
            pb = lambda n, shape: ctx.enter_context(nc.psum_tensor("ap_" + n, shape, fp32))
            sem = lambda n: ctx.enter_context(nc.semaphore("a_" + n))
            wq, wkv = sb("wq", [P, KD, HW]), sb("wkv", [P, KD, 2 * KW])
            bqkv = sb("bqkv", [P, HW + 2 * KW])
            rope = sb("rope", [P, BATCH, 2 * HW + 2 * KW])
            ctxT = sb("ctxT", [P, KD, SEQ])
            xb = sb("xb", [P, BT, DM])
            xT = sb("xT", [P, KD, SEQ])
            qk = sb("qk", [P, BT, HW + KW])
            rot = sb("rot", [P, BT, HW + KW])
            qp = sb("qp", [P, BT, KV, GRP, SLOT])
            kp = sb("kp", [P, BT, KV, GRP, SLOT])
            vb = sb("vb", [P, BT, KV, HDIM + 1])
            qT = sb("qT", [P, KV, SEQ])
            kT = sb("kT", [P, KV, SEQ])
            top = sb("top", [P, UNITS, GRP])
            prob = sb("prob", [P, 2, GRP, SEQ])
            probT = sb("probT", [P, BT, GRP, P])
            inv = sb("inv", [P, UNITS, GRP])
            SP_ = pb("S", [P, 2, GRP, SEQ])
            TP = pb("T", [P, BT, GRP, P])
            OP = pb("O", [P, GRP, HDIM + 1])
            QP = pb("Q", [P, BT, HW])
            KP_ = TP[:, 0].rearrange("p g t -> p (g t)")[:, 0:BT * 2 * KW].rearrange("p (b k) -> p b k", b=BT)
            S = {n: sem(n) for n in """w ctx xb xt xtc qkv own qkp qkt qktc s top prob pt ptc pv norm""".split()}
            block = ctx.enter_context(nc.Block())
            NW = 16 * 4

            @block.sync
            def _(sp):
                sp.dma_start(wq[:], A["wq"]).then_inc(S["w"], 16)
                sp.dma_start(wkv[:], A["wkv"]).then_inc(S["w"], 16)
                sp.dma_start(bqkv[:], A["bqkv"].broadcast_to([P, HW + 2 * KW])).then_inc(S["w"], 16)
                sp.dma_start(rope[:].rearrange("p a d -> p (a d)"),
                             A["rope"].broadcast_to([P, BATCH * 2 * (HW + KW)])).then_inc(S["w"], 16)
                with sp.Fori(0, BATCH) as b:
                    sp.wait_ge(S["qkv"], b + 1)
                    sp.dma_start(ctxT[:], A["ctxT"][bass.ds(b, 1)].rearrange("a p k t -> p (a k) t")).then_inc(S["ctx"], 16)

            @block.vector
            def _(dve):
                dve.sem_inc(S["ptc"], 1)
                dve.sem_inc(S["norm"], 1)
                dve.memset(qp[:], 0.0).then_inc(S["own"], 1)
                dve.memset(kp[:], 0.0).then_inc(S["own"], 1)
                dve.memset(vb[:], 1.0).then_inc(S["own"], 1)
                dve.wait_ge(S["w"], NW)
                with dve.Fori(0, BATCH) as b:
                    K = 11
                    n = [0]
                    base = b * K + 3

                    def mark(ins):
                        ins.then_inc(S["own"], 1)
                        n[0] += 1

                    def held():
                        dve.wait_ge(S["own"], base + n[0])
                    held()
                    mark(dve.tensor_copy(xb[:], x[:, bass.ds(b * BT, BT), :]))
                    held()
                    dve.tensor_scalar(xb[:], xb[:], 1.0, None, ALU.mult).then_inc(S["xb"], 1)
                    dve.wait_ge(S["qkv"], b + 2)
                    bias = bqkv[:].unsqueeze(1).broadcast_to([P, BT, HW + 2 * KW])
                    mark(dve.tensor_tensor(qk[:, :, 0:HW], QP[:], bias[:, :, 0:HW], ALU.add))
                    mark(dve.tensor_tensor(qk[:, :, HW:], KP_[:, :, 0:KW], bias[:, :, HW:HW + KW], ALU.add))
                    mark(dve.tensor_tensor(vb[:, :, :, 0:HDIM],
                                           KP_[:, :, KW:].rearrange("p b (h d) -> p b h d", h=KV),
                                           bias[:, :, HW + KW:].rearrange("p b (h d) -> p b h d", h=KV), ALU.add))
                    held()
                    rb = rope[:, bass.ds(b, 1), :]
                    for lo, heads, cut, c0 in ((0, HEADS, HEADS // 2, 0), (HW, KV, KV // 2, 2 * HW)):
                        w = heads * HDIM
                        v = lambda t, a, z: t.rearrange("p b (h d) -> p b h d", h=heads)[:, :, :, a:z]
                        for j in range(BT):
                            q1 = qk[:, j:j + 1, lo:lo + w]
                            r1 = rot[:, j:j + 1, lo:lo + w]
                            sn = rb[:, :, c0 + w:c0 + 2 * w]
                            first = HDIM - cut
                            last = dve.tensor_tensor(v(r1, 0, first), v(q1, cut, HDIM), v(sn, 0, first), ALU.mult)
                            last = dve.tensor_tensor(v(r1, first, HDIM), v(q1, 0, cut), v(sn, first, HDIM), ALU.mult)
                        mark(last)
                    held()
                    for lo, w, c0 in ((0, HW, 0), (HW, KW, 2 * HW)):
                        for j in range(BT):
                            last = dve.tensor_tensor(rot[:, j:j + 1, lo:lo + w], rot[:, j:j + 1, lo:lo + w],
                                                     rb[:, :, c0:c0 + w], ALU.add)
                        mark(last)
                    held()
                    for j in range(BT):
                        last = dve.tensor_tensor(
                            qp[:, j, :, :, 0:HDIM].rearrange("p k g d -> p (k g) d"),
                            rot[:, j, 0:HW].rearrange("p (h d) -> p h d", h=HEADS),
                            qk[:, j, 0:HW].rearrange("p (h d) -> p h d", h=HEADS), ALU.mult)
                    mark(last)
                    mark(dve.tensor_tensor(rot[:, :, HW:], rot[:, :, HW:], qk[:, :, HW:], ALU.mult))
                    held()
                    for j in range(BT):
                        for g in range(GRP):
                            last = dve.tensor_copy(kp[:, j, :, g, 0:HDIM],
                                                   rot[:, j, HW:].rearrange("p (h d) -> p h d", h=KV))
                    last.then_inc(S["qkp"], 1)
                    def tail(i):
                        ui = b * UNITS + i
                        dve.wait_ge(S["pt"], ui + 1)
                        dve.wait_ge(S["pv"], ui + 1)
                        dve.tensor_copy(probT[:], TP[:]).then_inc(S["ptc"], 1)

                    def norm(i):
                        ui = b * UNITS + i
                        dve.wait_ge(S["pv"], ui + 2)
                        dve.reciprocal(inv[:, i, :], OP[:, :, HDIM]).then_inc(S["norm"], 1)
                        dve.wait_ge(S["norm"], 2 * ui + 2)
                        out = att[:, bass.ds(b * BT, BT), i * 2 * HDIM:(i + 1) * 2 * HDIM]
                        dve.tensor_tensor(out.rearrange("p n (h d) -> p n h d", h=2),
                                          OP[:, :, 0:HDIM].rearrange("p (h n) d -> p n h d", h=2),
                                          inv[:, i, :].rearrange("p (h n) -> p n h", h=2).unsqueeze(3).broadcast_to([P, BT, 2, HDIM]),
                                          ALU.mult).then_inc(S["norm"], 1)
                    for i in range(UNITS + 1):
                        ui = b * UNITS + i
                        if i < UNITS:
                            dve.wait_ge(S["s"], ui + 1)
                            dve.tensor_reduce(top[:, i, :], SP_[:, i % 2], AX.X, ALU.max, negate=True).then_inc(S["top"], 1)
                        if i >= 1:
                            tail(i - 1)
                            norm(i - 1)
                    mark(dve.memset(inv[:, 0, 0:1], 0.0))
                    if n[0] != K:
                        print("att K", n[0])
                        assert 0

            @block.scalar
            def _(act):
                act.sem_inc(S["prob"], 1)
                with act.Fori(0, BATCH) as b:
                    for k in range(KD):
                        act.wait_ge(S["xt"], b * KD + k + 1)
                        act.activation(xT[:, k, :], SP_[:, k, 0, :], ACT.Copy).then_inc(S["xtc"], 1)
                    for r, dst in ((0, qT), (1, kT)):
                        act.wait_ge(S["qkt"], 2 * b + r + 1)
                        act.activation(dst[:].rearrange("p k t -> p (k t)"),
                                       SP_[:, r].rearrange("p g t -> p (g t)"), ACT.Copy).then_inc(S["qktc"], 1)
                    for i in range(UNITS):
                        ui = b * UNITS + i
                        act.wait_ge(S["top"], ui + 1)
                        if i >= 2:
                            act.wait_ge(S["pt"], ui - 1)
                        for g in range(GRP):
                            last = act.activation(prob[:, i % 2, g], SP_[:, i % 2, g], ACT.Exp, bias=top[:, i, g:g + 1])
                        last.then_inc(S["prob"], 1)

            @block.tensor
            def _(pe):
                pe.wait_ge(S["w"], NW)
                pe.sem_inc(S["qkv"], 1)
                pe.sem_inc(S["pv"], 1)
                with pe.Fori(0, BATCH) as b:
                    pe.wait_ge(S["xb"], b + 1)
                    pe.wait_ge(S["prob"], b * UNITS + 1)
                    for k in range(KD):
                        for j in range(BT):
                            last = pe.transpose(SP_[:, k, 0, j * P:(j + 1) * P], xb[:, j, k * P:(k + 1) * P], ident[:])
                        last.then_inc(S["xt"], 1)
                    pe.wait_ge(S["xtc"], (b + 1) * KD)
                    for j in range(BT):
                        for k in range(KD):
                            pe.matmul(QP[:, j], xT[:, k, j * P:(j + 1) * P], wq[:, k, :], start=(k == 0), stop=(k == KD - 1))
                    pe.wait_ge(S["ctx"], 16 * b + 16)
                    pe.wait_ge(S["ptc"], b * UNITS + 1)
                    for j in range(BT):
                        for k in range(KD):
                            last = pe.matmul(KP_[:, j], ctxT[:, k, j * P:(j + 1) * P], wkv[:, k, :],
                                             start=(k == 0), stop=(k == KD - 1))
                    last.then_inc(S["qkv"], 1)
                    pe.wait_ge(S["qkp"], b + 1)
                    for r, src in ((0, qp), (1, kp)):
                        for m in range(KV):
                            for j in range(BT):
                                last = pe.transpose(SP_[:, r].rearrange("p g t -> p (g t)")[:, (m * BT + j) * P:(m * BT + j + 1) * P],
                                                    src[:, j, m].rearrange("p g d -> p (g d)"), ident[:])
                        last.then_inc(S["qkt"], 1)
                    pe.wait_ge(S["qktc"], 2 * b + 2)

                    def scores(i):
                        m, pair = divmod(i, GRP // 2)
                        ui = b * UNITS + i
                        if i >= 2:
                            pe.wait_ge(S["prob"], ui)
                        for q in range(BT):
                            for hd in range(2):
                                g = 2 * pair + hd
                                rows = slice(g * SLOT, g * SLOT + HDIM)
                                last = pe.matmul(SP_[:, i % 2, hd * BT + q], qT[rows, m, q * P:(q + 1) * P], kT[rows, m, :],
                                                 start=True, stop=True)
                        last.then_inc(S["s"], 1)

                    def turn(i):
                        ui = b * UNITS + i
                        pe.wait_ge(S["prob"], ui + 2)
                        pe.wait_ge(S["ptc"], ui + 1)
                        for g in range(GRP):
                            for st in range(BT):
                                last = pe.transpose(TP[:, st, g], prob[:, i % 2, g, st * P:(st + 1) * P], ident[:])
                        last.then_inc(S["pt"], 1)

                    def values(i):
                        m = i // (GRP // 2)
                        ui = b * UNITS + i
                        pe.wait_ge(S["ptc"], ui + 2)
                        pe.wait_ge(S["norm"], 2 * ui + 1)
                        for g in range(GRP):
                            for st in range(BT):
                                last = pe.matmul(OP[:, g], probT[:, st, g], vb[:, st, m, :], start=(st == 0), stop=(st == BT - 1))
                        last.then_inc(S["pv"], 1)
                    scores(0)
                    for i in range(UNITS):
                        if i + 1 < UNITS:
                            scores(i + 1)
                        turn(i)
                        values(i)
        blend(nc, A, x, "xattn", "x", att)


def moe(nc, A, x, ident):
    fp32, bf16 = mybir.dt.float32, mybir.dt.bfloat16
    ALU, ACT, AX = mybir.AluOpType, mybir.ActivationFunctionType, mybir.AxisListType
    CH = 512
    CHUNKS = TOK // CH
    CT = CH // P
    with ExitStack() as ctx:
        sb = lambda n, shape, dt=fp32: ctx.enter_context(nc.sbuf_tensor("mo_" + n, shape, dt))
        sem = lambda n: ctx.enter_context(nc.semaphore("m_" + n))
        rw = sb("rw", [P, KD, EXP])
        rb = sb("rb", [P, EXP])
        iota = sb("iota", [P, EXP])
        identb = sb("identb", [P, P], bf16)
        picke = sb("picke", [96, EXP, P], bf16)
        b1 = sb("b1", [P, KD, EXP])
        b2 = sb("b2", [EXP, DM])
        b1e = sb("b1e", [P, 2, KD])
        w1 = sb("w1", [P, 2, KD, DM])
        w2 = sb("w2", [P, 2, KD, DM])
        xT = sb("xT", [P, KD, TOK])
        ones = sb("ones", [P, 1])
        lg = sb("lg", [P, TILES, EXP])
        tmp = sb("tmp", [P, TILES, EXP])
        one = [sb(f"hot{k}", [P, TILES, EXP]) for k in range(TOP)]
        mask = sb("mask", [P, TILES, EXP])
        rmax = sb("rmax", [P, TILES])
        best = sb("best", [P, TILES, 8])
        besti = sb("besti", [P, TILES, 8], mybir.dt.uint32)
        bestf = sb("bestf", [P, TILES, 8])
        norm2 = sb("norm2", [P, TILES])
        mres = sb("mres", [P, TILES, EXP])
        parts = sb("parts", [P, TILES, 96], bf16)
        maskT = sb("maskT", [EXP, TOK])
        partsT = sb("partsT", [96, TOK], bf16)
        mrow = sb("mrow", [P, 2, TOK])
        hid = sb("hid", [P, 2, KD, CH])
        act_ = sb("act", [P, 2, KD, CH])
        stats = sb("stats", [P, TILES, 6])
        mv = sb("mv", [P, TILES, 2])
        rstd = sb("rstd", [P, TILES])
        S = {n: sem(n) for n in """w xt xtc lg own rex mk mt mtc mr mrc wa wb2 w1u b1c st hp hm g o acc fin ve rs out""".split()}

        with ExitStack() as ps:
            TPs = [ps.enter_context(nc.psum_tensor(f"mo_t{i}", [P, CH], fp32)) for i in range(2)]
            LG = ps.enter_context(nc.psum_tensor("mo_logits", [P, TILES, EXP], fp32))
            CS = ps.enter_context(nc.psum_tensor("mo_cs", [EXP, TOP], fp32))
            MT = ps.enter_context(nc.psum_tensor("mo_mt", [EXP, CH], fp32))
            PT = ps.enter_context(nc.psum_tensor("mo_pt", [96, CH], bf16))
            IN = [ps.enter_context(nc.psum_tensor(f"mo_in{i}", [P, 2, DM], fp32)) for i in range(2)]
            block = ps.enter_context(nc.Block())
            NW = 16 * 7

            @block.sync
            def _(sp):
                sp.dma_start(rw[:], A["rw"]).then_inc(S["w"], 16)
                sp.dma_start(rb[:], A["rb"].broadcast_to([P, EXP])).then_inc(S["w"], 16)
                sp.dma_start(iota[:], A["iota"].broadcast_to([P, EXP])).then_inc(S["w"], 16)
                sp.dma_start(identb[:], A["identb"].bitcast(bf16)).then_inc(S["w"], 16)
                sp.dma_start(picke[:], A["picke"].bitcast(bf16)).then_inc(S["w"], 16)
                sp.dma_start(b1[:], A["b1"]).then_inc(S["w"], 16)
                sp.dma_start(b2[:], A["b2"]).then_inc(S["w"], 16)

            @block.tensor
            def _(pe):
                n = 0
                for c in range(CHUNKS):
                    for k in range(KD):
                        if n >= 2:
                            pe.wait_ge(S["xtc"], n - 1)
                        for j in range(CT):
                            last = pe.transpose(TPs[n % 2][:, j * P:(j + 1) * P], x[:, c * CT + j, k * P:(k + 1) * P], ident[:])
                        last.then_inc(S["xt"], 1)
                        n += 1
                pe.wait_ge(S["w"], NW)
                pe.wait_ge(S["xtc"], n)
                for t in range(TILES):
                    for k in range(KD):
                        last = pe.matmul(LG[:, t], xT[:, k, t * P:(t + 1) * P], rw[:, k, :], start=(k == 0), stop=(k == KD - 1))
                last.then_inc(S["lg"], 1)
                pe.wait_ge(S["mk"], 1)
                for k in range(TOP):
                    for t in range(TILES):
                        last = pe.matmul(CS[:, k:k + 1], one[k][:, t, :], ones[:], start=(t == 0), stop=(t == TILES - 1))
                last.then_inc(S["mt"], 1)
                pe.wait_ge(S["mk"], 2)
                for c in range(CHUNKS):
                    if c:
                        pe.wait_ge(S["mtc"], 2 * c)
                    for j in range(CT):
                        pe.transpose(MT[:, j * P:(j + 1) * P], mask[:, c * CT + j, :], ident[:])
                        last = pe.transpose(PT[:, j * P:(j + 1) * P], parts[:, c * CT + j, :], identb[:])
                    last.then_inc(S["mt"], 1)
                pe.wait_ge(S["mtc"], 2 * CHUNKS)
                for t in range(TILES):
                    w, half = divmod(t, 2)
                    if half == 0 and w >= 2:
                        pe.wait_ge(S["fin"], w - 1)
                    last = pe.matmul(IN[w % 2][:, half], maskT[:, t * P:(t + 1) * P], b2[:], start=True, stop=True)
                    if half:
                        last.then_inc(S["o"], 1)

            @block.scalar
            def _(act):
                n = 0
                for c in range(CHUNKS):
                    for k in range(KD):
                        act.wait_ge(S["xt"], n + 1)
                        act.activation(xT[:, k, c * CH:(c + 1) * CH], TPs[n % 2][:], ACT.Copy).then_inc(S["xtc"], 1)
                        n += 1
                act.wait_ge(S["rex"], 1)
                act.activation(tmp[:], tmp[:], ACT.Exp).then_inc(S["rex"], 1)
                for c in range(CHUNKS):
                    act.wait_ge(S["mt"], c + 2)
                    act.activation(maskT[:, c * CH:(c + 1) * CH], MT[:], ACT.Copy).then_inc(S["mtc"], 1)
                    act.activation(partsT[:, c * CH:(c + 1) * CH], PT[:], ACT.Copy).then_inc(S["mtc"], 1)

            @block.vector
            def _(dve):
                n = [0]

                def do(ins):
                    ins.then_inc(S["own"], 1)
                    n[0] += 1
                    dve.wait_ge(S["own"], n[0])
                per = lambda a: a.unsqueeze(2).broadcast_to([P, TILES, EXP])
                do(dve.memset(ones[:], 1.0))
                do(dve.memset(parts[:], 0.0))
                dve.wait_ge(S["w"], NW)
                dve.wait_ge(S["lg"], 1)
                do(dve.tensor_tensor(lg[:], LG[:], rb[:].unsqueeze(1).broadcast_to([P, TILES, EXP]), ALU.add))
                do(dve.tensor_reduce(rmax[:], lg[:], AX.X, ALU.max))
                dve.tensor_tensor(tmp[:], lg[:], per(rmax[:]), ALU.subtract).then_inc(S["rex"], 1)
                dve.wait_ge(S["rex"], 2)
                do(dve.tensor_reduce(norm2[:], tmp[:], AX.X, ALU.add))
                do(dve.reciprocal(norm2[:], norm2[:]))
                do(dve.tensor_tensor(lg[:], tmp[:], per(norm2[:]), ALU.mult))
                for t in range(TILES):
                    do(dve.max(best[:, t, :], lg[:, t, :]))
                    do(dve.max_index(besti[:, t, :], best[:, t, :], lg[:, t, :]))
                do(dve.tensor_copy(bestf[:], besti[:]))
                do(dve.tensor_tensor(norm2[:], best[:, :, 0], best[:, :, 1], ALU.add))
                do(dve.reciprocal(norm2[:], norm2[:]))
                do(dve.tensor_tensor(best[:], best[:], per(norm2[:]), ALU.mult))
                for k in range(TOP):
                    do(dve.tensor_tensor(one[k][:], iota[:].unsqueeze(1).broadcast_to([P, TILES, EXP]),
                                         per(bestf[:, :, k]), ALU.is_equal))
                    do(dve.tensor_tensor(one[k][:], one[k][:], per(best[:, :, k]), ALU.mult))
                dve.tensor_tensor(mask[:], one[0][:], one[1][:], ALU.add).then_inc(S["mk"], 1)
                dve.wait_ge(S["mk"], 1)
                dve.wait_ge(S["mt"], 1)
                do(dve.tensor_tensor(mask[0:EXP, 0, 0:TOP], mask[0:EXP, 0, 0:TOP], CS[:], ALU.add))
                do(dve.tensor_scalar(mask[:], mask[:], CAPACITY, None, ALU.min))
                do(dve.tensor_copy(parts[:, :, 0:EXP], mask[:]))
                do(dve.tensor_tensor(mres[:], mask[:], parts[:, :, 0:EXP], ALU.subtract))
                do(dve.tensor_copy(parts[:, :, 32:32 + EXP], mres[:]))
                dve.tensor_tensor(parts[:, :, 64:64 + EXP], mres[:], parts[:, :, 32:32 + EXP], ALU.subtract).then_inc(S["mk"], 1)
                for w in range(TILES // 2):
                    dve.wait_ge(S["o"], w + 1)
                    dve.tensor_tensor(x[:, 2 * w:2 * w + 2, :], x[:, 2 * w:2 * w + 2, :], IN[w % 2][:], ALU.add).then_inc(S["fin"], 1)

        with ExitStack() as ps:
            HP = [ps.enter_context(nc.psum_tensor(f"mo_h{i}", [P, CH], fp32)) for i in range(3)]
            MR = ps.enter_context(nc.psum_tensor("mo_mr", [P, CH], fp32))
            OP = [ps.enter_context(nc.psum_tensor(f"mo_o{i}", [P, 2, DM], fp32)) for i in range(4)]
            block = ps.enter_context(nc.Block())
            PAIRS = EXP // 2
            HPE = CHUNKS * KD
            OB = TILES // 2
            arrived = [S["wa"], S["wb2"]]

            @block.sync
            def _(sp):
                for par in range(2):
                    sp.dma_start(w1[:, par], A["w1"][par]).then_inc(arrived[par], 16)
                    sp.dma_start(w2[:, par], A["w2"][par]).then_inc(arrived[par], 16)
                with sp.Fori(1, PAIRS) as r:
                    for par in range(2):
                        sp.wait_ge(S["w1u"], 2 * r - 1 + par)
                        sp.dma_start(w1[:, par], A["w1"][bass.ds(2 * r + par, 1)].rearrange("a p k d -> p (a k) d")).then_inc(arrived[par], 16)
                        sp.dma_start(w2[:, par], A["w2"][bass.ds(2 * r + par, 1)].rearrange("a p k d -> p (a k) d")).then_inc(arrived[par], 16)
                sp.wait_ge(S["out"], TILES)
                sp.dma_start(A["out"], x[:]).then_inc(S["st"], 16)
                sp.wait_ge(S["st"], 16)

            @block.tensor
            def _(pe):
                with pe.Fori(0, PAIRS) as r:
                    for par in range(2):
                        e = r * 2 + par
                        pe.wait_ge(arrived[par], r * 32 + 32)
                        for c in range(CHUNKS):
                            pe.wait_ge(S["mrc"], e * CHUNKS + c + 1)
                            pe.matmul(MR[:], picke[:, bass.ds(e, 1), :].rearrange("p a c -> p (a c)"),
                                      partsT[:, c * CH:(c + 1) * CH], start=True, stop=True).then_inc(S["mr"], 1)

                        def up(c):
                            for m in range(KD):
                                i = c * KD + m
                                q = par * HPE + i
                                pe.wait_ge(S["hm"], e * HPE + i + 1)
                                for k in range(KD):
                                    last = pe.matmul(HP[i % 2][:], w1[:, par, k, m * P:(m + 1) * P],
                                                     xT[:, k, c * CH:(c + 1) * CH], start=(k == 0), stop=(k == KD - 1))
                                last.then_inc(S["hp"], 1)

                        def down(c):
                            pe.wait_ge(S["g"], e * HPE + (c + 1) * KD + 1)
                            for w in range(2):
                                o = c * 2 + w
                                pe.wait_ge(S["acc"], (e * CHUNKS + c) * 4 + 2 * w + 1)
                                for j in (2 * w, 2 * w + 1):
                                    for k in range(KD):
                                        last = pe.matmul(OP[o % 4][:, j % 2], act_[:, c % 2, k, j * P:(j + 1) * P],
                                                         w2[:, par, k, :], start=(k == 0), stop=(k == KD - 1))
                                last.then_inc(S["o"], 1)
                            if c == CHUNKS - 1:
                                last2 = None
                        up(0)
                        for c in range(CHUNKS):
                            if c + 1 < CHUNKS:
                                up(c + 1)
                            down(c)
                        pe.matmul(HP[2][:, 0:1], ident[:], ones[:], start=True, stop=True).then_inc(S["w1u"], 1)

            @block.scalar
            def _(act):
                act.sem_inc(S["mrc"], 1)
                act.sem_inc(S["g"], 1)
                with act.Fori(0, PAIRS) as r:
                    for par in range(2):
                        e = r * 2 + par
                        act.activation(b1e[:, par], b1[:, :, bass.ds(e, 1)].rearrange("p k a -> p (k a)"),
                                       ACT.Copy).then_inc(S["b1c"], 1)
                        act.wait_ge(S["b1c"], e + 1)
                        for c in range(CHUNKS):
                            act.wait_ge(S["mr"], e * CHUNKS + c + 1)
                            act.activation(mrow[:, par, c * CH:(c + 1) * CH], MR[:], ACT.Copy).then_inc(S["mrc"], 1)
                        for c in range(CHUNKS):
                            for m in range(KD):
                                i = c * KD + m
                                act.wait_ge(S["hm"], e * HPE + i + 3)
                                act.wait_ge(S["o"], OB + e * CHUNKS * 2 + 2 * (c - 2) + 2) if c >= 2 else act.wait_ge(S["o"], OB + e * CHUNKS * 2)
                                act.activation(act_[:, c % 2, m], hid[:, c % 2, m], ACT.Gelu,
                                               bias=b1e[:, par, m:m + 1]).then_inc(S["g"], 1)
                act.wait_ge(S["ve"], 1)
                act.activation(rstd[:], rstd[:], ACT.Ln).then_inc(S["rs"], 1)
                act.wait_ge(S["rs"], 1)
                act.activation(rstd[:], rstd[:], ACT.Exp, scale=-0.5).then_inc(S["rs"], 1)

            @block.vector
            def _(dve):
                dve.sem_inc(S["hm"], 2)
                dve.sem_inc(S["acc"], 8)
                with dve.Fori(0, PAIRS) as r:
                    for par in range(2):
                        e = r * 2 + par

                        def scale(c):
                            for m in range(KD):
                                i = c * KD + m
                                dve.wait_ge(S["hp"], e * HPE + i + 1)
                                if m == 0:
                                    dve.wait_ge(S["mrc"], e * CHUNKS + CHUNKS + 1)
                                if i >= 4:
                                    dve.wait_ge(S["g"], e * HPE + i - 2)
                                else:
                                    dve.wait_ge(S["g"], e * HPE + 1)
                                dve.tensor_tensor(hid[:, c % 2, m], HP[i % 2][:], mrow[:, par, c * CH:(c + 1) * CH],
                                                  ALU.mult).then_inc(S["hm"], 1)

                        def gather(c):
                            for w in range(2):
                                o = c * 2 + w
                                dve.wait_ge(S["o"], OB + (e * CHUNKS + c) * 2 + w + 1)
                                for j in (2 * w, 2 * w + 1):
                                    t = c * CT + j
                                    dve.wait_ge(S["acc"], e * TILES + 8)
                                    dve.scalar_tensor_tensor(x[:, t, :], OP[o % 4][:, j % 2], mask[:, t, bass.ds(e, 1)],
                                                             x[:, t, :], ALU.mult, ALU.add).then_inc(S["acc"], 1)
                        scale(0)
                        for c in range(CHUNKS):
                            if c + 1 < CHUNKS:
                                scale(c + 1)
                            gather(c)
                dve.wait_ge(S["acc"], EXP * TILES + 8)
                for j in range(TILES):
                    dve.bn_stats(stats[:, j, :], x[:, j, :]).then_inc(S["fin"], 1)
                dve.wait_ge(S["fin"], TILES // 2 + TILES)
                for j in range(TILES):
                    dve.bn_aggr(mv[:, j, :], stats[:, j, :]).then_inc(S["fin"], 1)
                dve.wait_ge(S["fin"], TILES // 2 + 2 * TILES)
                dve.tensor_scalar(rstd[:], mv[:, :, 1], EPS, None, ALU.add).then_inc(S["ve"], 1)
                dve.wait_ge(S["rs"], 2)
                for j in range(TILES):
                    dve.tensor_scalar(x[:, j, :], x[:, j, :], mv[:, j, 0:1], rstd[:, j:j + 1],
                                      ALU.subtract, ALU.mult).then_inc(S["out"], 1)


def layout(I, np):
    ONE = 0x3F80
    g = lambda n: np.asarray(I[n])
    parts = lambda a, k: np.ascontiguousarray(a.reshape(k, P, -1).transpose(1, 0, 2))
    out = {}
    out["x"] = g("x").reshape(TILES, P, DM).transpose(1, 0, 2)
    out["ident"] = np.eye(P, dtype=np.float32)
    pick = np.zeros((3, 2 * DS, 2 * DS, P), np.uint16)
    for r in range(2 * DS):
        pick[:, r, r, :] = ONE
    out["pick"] = pick.reshape(96, 2 * DS, P)
    out["lnw"] = np.stack([g("L0_attn_ln_w"), g("L0_attn_ln_b")], 1).reshape(LAYERS, 2, KD, P).transpose(3, 0, 1, 2)
    cw = g("L0_attn_conv_w").transpose(0, 2, 1)
    ch = np.concatenate([g("L0_attn_conv_b")[:, None], g("L0_attn_dt_proj_b")[:, None], g("L0_attn_D_skip")[:, None], cw], 1)
    out["chan"] = ch.reshape(LAYERS, 3 + TAPS, M, P).transpose(3, 0, 1, 2)
    out["alog"] = g("L0_attn_A_log").reshape(LAYERS, M, P, DS).transpose(2, 0, 1, 3)
    out["inw"] = np.stack([parts(g("L0_attn_in_proj_w")[l].T, KD) for l in range(LAYERS)])
    xw = g("L0_attn_x_proj_w")
    xw = np.concatenate([xw[:, RANK:]] * 3 + [xw[:, :RANK]], 1)
    out["xpw"] = np.stack([parts(xw[l].T, M) for l in range(LAYERS)])
    out["dtw"] = g("L0_attn_dt_proj_w").transpose(0, 2, 1)
    out["outw"] = np.stack([parts(g("L0_attn_out_proj_w")[l].T, M) for l in range(LAYERS)])
    QH, KVH, HD = HEADS, KV, HDIM
    out["nf"] = np.concatenate([g("L0_attn_norm_f_w"), g("L0_attn_norm_f_b")])[None]
    out["xn_wb"] = np.concatenate([g("L0_xattn_gamma"), g("L0_xattn_beta")])[None]
    out["ctxT"] = g("ctx_1024").reshape(BATCH, SEQ, KD, P).transpose(0, 3, 2, 1)
    out["wq"] = parts(g("L0_xattn_Wq").T, KD)
    out["wkv"] = parts(np.concatenate([g("L0_xattn_Wk"), g("L0_xattn_Wv")]).T, KD)
    out["bqkv"] = np.concatenate([g("L0_xattn_bq"), g("L0_xattn_bk"), g("L0_xattn_bv")])[None]

    def rope(d, scale):
        theta = (1.0 / 10000.0 ** (np.arange(0, d, 2, dtype=np.float32) / np.float32(d))).astype(np.float32)
        a = np.arange(BATCH, dtype=np.float32)[:, None] * theta[None]
        a = np.concatenate([a, a], -1)[:, :, None]
        sign = np.where(np.arange(HD) < HD - d // 2, -1.0, 1.0).astype(np.float32)
        c = np.broadcast_to(np.cos(a) * np.float32(scale), (BATCH, d, HD))
        return [c.reshape(BATCH, -1), (np.sin(a) * np.float32(scale) * sign).reshape(BATCH, -1)]
    out["rope"] = np.concatenate(rope(QH, HD ** -0.5) + rope(KVH, 1.0), 1).astype(np.float32).reshape(1, -1)
    out["rw"] = parts(g("L0_ffn_router_w"), KD)
    out["rb"] = g("L0_ffn_router_b")[None]
    out["w1"] = g("L0_ffn_w1").reshape(EXP, KD, P, DM).transpose(0, 2, 1, 3)
    out["w2"] = g("L0_ffn_w2").reshape(EXP, KD, P, DM).transpose(0, 2, 1, 3)
    out["b1"] = g("L0_ffn_b1").reshape(EXP, KD, P).transpose(2, 1, 0)
    out["b2"] = g("L0_ffn_b2")
    pe = np.zeros((96, EXP, P), np.uint16)
    for e in range(EXP):
        pe[[e, 32 + e, 64 + e], e, :] = ONE
    out["picke"] = pe
    out["identb"] = np.where(np.eye(P) > 0, ONE, 0).astype(np.uint16)
    out["iota"] = np.arange(EXP, dtype=np.float32)[None]
    return {k: np.ascontiguousarray(v) for k, v in out.items()}


def kernel(**inputs):
    import numpy as np
    import concourse.bacc as bacc
    from concourse.bass_utils import run_bass_kernel_spmd as run

    nc = bacc.Bacc("TRN2", target_bir_lowering=False, num_devices=1)
    arrays, A = {}, {}
    for name, a in layout(inputs, np).items():
        arrays["in_" + name] = a
        A[name] = nc.dram_tensor("in_" + name, a.shape, mybir.dt.from_np(a.dtype), kind="ExternalInput").ap()
    A["out"] = nc.dram_tensor("out", (P, TILES, DM), mybir.dt.float32, kind="ExternalOutput").ap()
    build(nc, A)
    got = run(nc, [arrays], core_ids=[0]).results[0]["out"]
    return np.ascontiguousarray(got.transpose(1, 0, 2)).reshape(BATCH, SEQ, DM)
```

```python
import concourse.bass as bass
from concourse import mybir
from contextlib import ExitStack

P = 128
BATCH, SEQ, DM = 8, 256, 256
TOK = BATCH * SEQ
TILES = TOK // P
KD = DM // P
LAYERS, DI, DS, RANK, TAPS = 2, 512, 16, 16, 4
M = DI // P
SB = 2
SEG = SB * SEQ
SEGS = BATCH // SB
ST = SEG // P
PAD = TAPS - 1
XPR = 3 * 2 * DS + RANK
EPS = 1e-5


AT = dict(rstd=0, normalise=0, transposes=0, norm_weights=2, in_proj=(1, 1, 2, 3, 4, 6, 7, 7),
          take=(4, 4, 5, 7, 7, 9, 9, 10), tap0=(4, 5, 7, 8),
          taps=((4, 5, 5), (5, 6, 6), (7, 7, 7), (8, 8, 9)), silus=10, x_proj=9, rows=11, split=10,
          dt_proj=(10, 10, 10, 11), dt_parts=(12, 13), plus_one=(11, 13), logs=(13, 14), softplus=(13, 14),
          out_proj=(13, 14), residual=(14, 15))


def build(nc, A):
    fp32 = mybir.dt.float32
    with ExitStack() as ctx:
        x = ctx.enter_context(nc.sbuf_tensor("x", [P, TILES, DM], fp32))
        ident = ctx.enter_context(nc.sbuf_tensor("ident", [P, P], fp32))
        mamba(nc, A, x, ident)
        with ExitStack() as late:
            att = late.enter_context(nc.sbuf_tensor("att", [P, TILES, DM], fp32))
            with ExitStack() as its:
                weights = attention_inputs(nc, its, A)
                blend(nc, A, x, "norm_f", A["nf"], None, weights[-1])
                attention(nc, A, x, ident, att, weights)
            weights = moe_inputs(nc, late, A)
            blend(nc, A, x, "xattn", A["xn_wb"], att, weights[-1])
            moe(nc, A, x, ident, weights)


def mamba(nc, A, x, ident):
    fp32, bf16 = mybir.dt.float32, mybir.dt.bfloat16
    ALU, ACT = mybir.AluOpType, mybir.ActivationFunctionType
    with ExitStack() as ctx:
        def sb(name, shape, dt=fp32):
            return ctx.enter_context(nc.sbuf_tensor(name, shape, dt))

        def pb(name, shape):
            return ctx.enter_context(nc.psum_tensor(name, shape, fp32))

        pick = sb("pick", [96, 2 * DS, P], bf16)
        inw = sb("inw", [P, KD, 2 * DI])
        xpw = [sb(f"xpw{l}", [P, M, XPR]) for l in range(LAYERS)]
        dtw = [sb(f"dtw{l}", [P, DI]) for l in range(LAYERS)]
        outw = [sb(f"outw{l}", [P, M, DM]) for l in range(LAYERS)]
        lnw = sb("lnw", [P, LAYERS, 2, KD])
        chan = sb("chan", [P, LAYERS, 3 + TAPS, M])
        nega = sb("nega", [P, LAYERS, M, DS])
        skip = sb("skip", [P, LAYERS, M, P])
        stats = sb("stats", [P, ST, 6])
        mv = sb("mv", [P, ST, 2])
        vare = sb("vare", [P, ST])
        rstd = sb("rstd", [P, ST])
        power = sb("power", [P, ST])
        xp = sb("xp", [P, M, SB, PAD + SEQ])
        cv = sb("cv", [P, M, SEG])
        zs = sb("zs", [P, 2, M, SEG])
        xc = sb("xc", [P, M, SEG])
        bc = sb("bc", [96, 2, SEG], bf16)
        low = sb("low", [P, SEG])
        bcr, dr = low[0:64, :], low[96:96 + RANK, :]
        dt = sb("dt", [P, 2, M, SEG])
        du = sb("du", [P, 2, M, SEG])
        soft = sb("soft", [P, M, SEG])
        xn = soft[:, 0:2].rearrange("p m (j d) -> p (m j) d", d=DM)
        hT = soft[:, 2:4]
        brow = sb("brow", [P, 2, SEG])
        dA = sb("dA", [P, 2, M, SEG])
        dBu = sb("dBu", [P, 2, M, SEG])
        h = sb("h", [P, M, SEG])
        hC = sb("hC", [P, 2, M, SEG])
        yz = sb("yz", [P, M, SEG])
        half = lambda q: slice(q * M // 2, (q + 1) * M // 2)
        lnu = lambda q: xp[:, half(q), :, PAD:].rearrange("p m b t -> p (m b) t")
        pairs = lambda t: t.rearrange("p m (b t) -> p (m b) t", b=SB)
        Y = pb("Y", [P, M, SEG])
        Bp, Cp = pb("Bp", [P, SEG]), pb("Cp", [P, SEG])
        W = [pb(f"W{i}", [P, SEG]) for i in range(2)]

        S = {n: ctx.enter_context(nc.semaphore(n)) for n in """pow x_in x_rest small_in w_in start own_v diag ve rstd_ready xn_ready tp
            hT_ready ip ip_used tap0 conv xc_ready zs_ready dbl hi r1 mid lo dr_ready dtp dtp_used expn one lnu_ready
            dtd dud b_ready b_copied c_ready expd dbud scan_done hc_done y_done inw_in y_init yzd op res gate""".split()}
        LW, LB = 0, 1
        CB, DTB, DSK, CW = 0, 1, 2, 3
        WEIGHTS = 16 * (1 + 3 * LAYERS)
        SMALL = 16 * 4
        UNITS = LAYERS * SEGS

        def after(eng, name, value):
            if not isinstance(value, int) or value > 0:
                eng.wait_ge(S[name], value)

        def gate(eng):
            eng.sem_inc(S["gate"], 1)

        def units(eng, prologue, scan, epilogue):
            prologue(0, 0, 0)
            for l in range(LAYERS):
                scan(l, 0, l * SEGS, (l, 1, l * SEGS + 1))
                with eng.Fori(1, SEGS - 1) as s:
                    scan(l, s, s + l * SEGS, (l, s + 1, s + (l * SEGS + 1)))
                scan(l, SEGS - 1, (l + 1) * SEGS - 1, (l + 1, 0, (l + 1) * SEGS) if l + 1 < LAYERS else None)
            epilogue(LAYERS - 1, SEGS - 1, UNITS)

        block = ctx.enter_context(nc.Block())

        @block.sync
        def _(sp):
            def load(dst, src, s="w_in"):
                sp.dma_start(dst, src).then_inc(S[s], 16)
            load(x[:, 0:ST, :], A["x"][:, 0:ST, :], "x_in")
            load(ident[:], A["ident"], "small_in")
            load(lnw[:], A["lnw"], "small_in")
            load(chan[:], A["chan"], "small_in")
            load(nega[:], A["alog"], "small_in")
            load(inw[:], A["inw"][0], "inw_in")
            load(pick[:], A["pick"].bitcast(bf16))
            for l in range(LAYERS):
                load(xpw[l][:], A["xpw"][l])
                load(dtw[l][96:96 + RANK, :], A["dtw"][l])
            load(x[:, ST:, :], A["x"][:, ST:, :], "x_rest")
            for l in range(LAYERS):
                load(outw[l][:], A["outw"][l])
            for l in range(1, LAYERS):
                sp.wait_ge(S["ip"], l * SEGS * 2 * M)
                load(inw[:], A["inw"][l], "inw_in")

        @block.vector
        def _(dve):
            K = 2 * ST + 1 + M * (TAPS - 2) + 6
            START = 1
            dve.sem_inc(S["res"], 1)
            dve.memset(xp[:], 0.0).then_inc(S["start"], 1)
            dve.memset(dA[:], 0.0).then_inc(S["start"], 1)
            dve.memset(vare[:], 0.0).then_inc(S["own_v"], 1)

            def constants():
                dve.wait_ge(S["small_in"], SMALL)
                dve.wait_ge(S["start"], 3)
                dve.tensor_scalar(nega[:], nega[:], -1.0, None, ALU.mult).then_inc(S["start"], 1)
                for l in range(LAYERS):
                    for m in range(M):
                        dve.tensor_scalar(skip[:, l, m], ident[:], chan[:, l, DSK, m:m + 1], None, ALU.mult).then_inc(S["diag"], 1)

            def held(v, n):
                dve.wait_ge(S["own_v"], v * K + START + n)

            def statistics(l, s, v):
                held(v, 0)
                after(dve, "res", (v - SEGS + 1) * 2 + 1 if l else 0)
                dve.memset(vare[:], 0.0).then_inc(S["own_v"], 1)
                for j in range(ST):
                    dve.bn_stats(stats[:, j, :], x[:, s * ST + j, :]).then_inc(S["own_v"], 1)
                held(v, 1 + ST)
                dve.memset(rstd[:], 0.0).then_inc(S["gate"], 1)
                for j in range(ST):
                    dve.bn_aggr(mv[:, j, :], stats[:, j, :]).then_inc(S["own_v"], 1)
                held(v, 1 + 2 * ST)
                dve.tensor_scalar(vare[:], mv[:, :, 1], EPS, None, ALU.add).then_inc(S["ve"], 1)

            def normalise(l, s, v):
                dve.wait_ge(S["rstd_ready"], v + 1)
                after(dve, "tp", v * KD)
                for j in range(ST):
                    dve.tensor_scalar(xn[:, j, :], x[:, s * ST + j, :], mv[:, j, 0:1], rstd[:, j:j + 1],
                                      ALU.subtract, ALU.mult).then_inc(S["xn_ready"], 1)

            def tap(l, v, m, t):
                cvm = cv[:, m].rearrange("p (b t) -> p b t", b=SB)
                if t == 1:
                    dve.wait_ge(S["tap0"], v * M + m + 1)
                else:
                    held(v, 1 + 2 * ST + (TAPS - 2) * m + t - 1)
                dve.scalar_tensor_tensor(cvm, xp[:, m, :, t:t + SEQ], chan[:, l, CW + t, m:m + 1], cvm,
                                         ALU.mult, ALU.add).then_inc(S["own_v" if t < TAPS - 1 else "conv"], 1)

            def split(v, par):
                dve.wait_ge(S["hi"], v + 1)
                dve.tensor_tensor(bcr, W[0][0:64, :], bc[0:64, par, :], ALU.subtract).then_inc(S["r1"], 1)
                dve.wait_ge(S["r1"], v + 1)
                dve.tensor_scalar(bc[0:64, par, :], bcr, 1.0, None, ALU.mult).then_inc(S["mid"], 1)
                dve.wait_ge(S["mid"], v + 1)
                dve.tensor_tensor(bc[0:32, par, :], low[0:32, :], bc[0:32, par, :], ALU.subtract).then_inc(S["lo"], 1)

            def plus_one(v, q):
                dve.wait_ge(S["expn"], v * 2 + q + 1)
                dve.tensor_scalar(cv[:, half(q)], soft[:, half(q)], 1.0, None, ALU.add).then_inc(S["one"], 1)

            def softplus(v, par, q):
                n = 1 + 2 * ST + M * (TAPS - 2) + 3 * q
                e, one, d = soft[:, half(q)], cv[:, half(q)], dt[:, par, half(q)]
                dve.wait_ge(S["one"], v * 2 + q + 1)
                dve.scalar_tensor_tensor(e, one, 1.0, e, ALU.subtract, ALU.subtract).then_inc(S["own_v"], 1)
                held(v, n + 1)
                dve.tensor_tensor(d, d, e, ALU.subtract).then_inc(S["own_v"], 1)
                held(v, n + 2)
                dve.wait_ge(S["lnu_ready"], v * 2 + q + 1)
                dve.scalar_tensor_tensor(pairs(e), pairs(one), 1.0, lnu(q), ALU.is_gt, ALU.mult).then_inc(S["own_v"], 1)
                held(v, n + 3)
                dve.tensor_tensor(d, d, e, ALU.add).then_inc(S["dtd"], 1)

            def residual(s, u, w):
                dve.wait_ge(S["op"], (u - 1) * 2 + w + 2)
                xs = x[:, bass.ds(s * ST + 2 * w, 2), :]
                dve.tensor_tensor(xs, xs, W[w][:].rearrange("p (j d) -> p j d", j=2), ALU.add).then_inc(S["res"], 1)

            def gate_outputs(u, par):
                dve.wait_ge(S["y_done"], (u + 1) * DS)
                dve.wait_ge(S["op"], u * 2 + 1)
                dve.wait_ge(S["zs_ready"], u + 1)
                dve.tensor_tensor(yz[:], Y[:], zs[:, par], ALU.mult).then_inc(S["yzd"], 1)

            def step(l, s, u, n, nxt):
                g = u * DS + n
                b = n % 2
                flat = lambda t: t.rearrange("p m t -> p (m t)")
                dve.wait_ge(S["expd"], g + 1)
                dve.wait_ge(S["dbud"], g + 1)
                after(dve, "hc_done", g)
                dve.tensor_tensor_scan(flat(h[:]), flat(dA[:, b]), flat(dBu[:, b]), 0.0,
                                       ALU.mult, ALU.add).then_inc(S["scan_done"], 1)
                if n == 0:
                    if nxt is not None:
                        statistics(*nxt)
                    if not isinstance(u, int) or u > 0:
                        gate_outputs(u - 1, 1 - s % 2)
                dve.wait_ge(S["scan_done"], g + 1)
                dve.wait_ge(S["c_ready"], g + 1)
                after(dve, "y_done", g - 1)
                dve.tensor_tensor(hC[:, b], h[:], Cp[:].unsqueeze(1).broadcast_to([P, M, SEG]),
                                  ALU.mult).then_inc(S["hc_done"], 1)

            def prologue(l, s, v):
                dve.wait_ge(S["x_in"], 16)
                statistics(l, s, v)
                normalise(l, s, v)
                constants()
                dve.wait_ge(S["x_rest"], 16)
                for m in range(M):
                    for t in range(1, TAPS):
                        tap(l, v, m, t)
                split(v, v % 2)
                for q in range(2):
                    plus_one(v, q)
                    softplus(v, v % 2, q)

            def scan(l, s, u, nxt):
                for n in range(DS):
                    step(l, s, u, n, nxt)
                    if n in AT["residual"] and (not isinstance(u, int) or u > 0):
                        residual((s + SEGS - 1) % SEGS, u, AT["residual"].index(n))
                    if nxt is None:
                        continue
                    nl, ns, v = nxt
                    if n == AT["normalise"]:
                        normalise(nl, ns, v)
                    for m in range(M):
                        for t in range(1, TAPS):
                            if n == AT["taps"][m][t - 1]:
                                tap(nl, v, m, t)
                    if n == AT["split"]:
                        split(v, ns % 2)
                    for q in range(2):
                        if n == AT["plus_one"][q]:
                            plus_one(v, q)
                    for q in range(2):
                        if n == AT["softplus"][q]:
                            softplus(v, ns % 2, q)

            def epilogue(l, s, u):
                gate_outputs(u - 1, s % 2)
                for w in range(2):
                    residual(s, u, w)

            units(dve, prologue, scan, epilogue)

        @block.scalar
        def _(act):
            def norm_weights(l, v):
                after(act, "ip", v * 2 * M)
                for k in range(KD):
                    act.wait_ge(S["tp"], v * KD + k + 1)
                    act.activation(hT[:, k, :], W[k][:], ACT.Identity, scale=lnw[:, l, LW, k:k + 1],
                                   bias=lnw[:, l, LB, k:k + 1]).then_inc(S["hT_ready"], 1)

            def take(v, m, par):
                act.wait_ge(S["ip"], v * 2 * M + m + 1)
                if m < M:
                    after(act, "dtd", 2 * v)
                    act.activation(xp[:, m, :, PAD:], W[m % 2][:].rearrange("p (b t) -> p b t", b=SB),
                                   ACT.Copy).then_inc(S["ip_used"], 1)
                else:
                    after(act, "yzd", v - 1)
                    gate(act)
                    act.activation(zs[:, par, m - M, :], W[m % 2][:], ACT.Copy).then_inc(S["ip_used"], 1)

            def silus(v, par):
                after(act, "y_init", v)
                after(act, "dud", 2 * v)
                for m in range(M):
                    act.wait_ge(S["conv"], v * M + m + 1)
                    act.activation(xc[:, m, :], cv[:, m, :], ACT.Silu).then_inc(S["xc_ready"], 1)
                act.wait_ge(S["ip_used"], (v + 1) * 2 * M)
                gate(act)
                act.activation(zs[:, par], zs[:, par], ACT.Silu).then_inc(S["zs_ready"], 1)

            def rows(v, par):
                act.wait_ge(S["dbl"], v + 1)
                after(act, "c_ready", (v - 1) * DS)
                gate(act)
                act.activation(bc[:, par, :], W[0][0:96, :], ACT.Copy).then_inc(S["hi"], 1)
                act.activation(dr, W[0][96:96 + RANK, :], ACT.Copy).then_inc(S["dr_ready"], 1)

            def dt_parts(l, v, m, par):
                act.wait_ge(S["dtp"], v * M + m + 1)
                bias = chan[:, l, DTB, m:m + 1]
                gate(act)
                act.activation(soft[:, m, :], W[(m + 1) % 2][:], ACT.Abs, bias=bias)
                act.activation(dt[:, par, m, :], W[(m + 1) % 2][:], ACT.Relu, bias=bias).then_inc(S["dtp_used"], 1)

            def small_exp(v, q):
                act.wait_ge(S["dtp_used"], v * M + (q + 1) * M // 2)
                act.activation(soft[:, half(q)], soft[:, half(q)], ACT.Exp, scale=-1.0).then_inc(S["expn"], 1)

            def logs(v, q):
                act.wait_ge(S["one"], v * 2 + q + 1)
                act.activation(lnu(q), pairs(cv[:, half(q)]), ACT.Ln).then_inc(S["lnu_ready"], 1)

            def step(l, u, n, par):
                g = u * DS + n
                act.wait_ge(S["b_ready"], g + 1)
                after(act, "scan_done", g - 1)
                act.activation(brow[:, n % 2, :], Bp[:], ACT.Copy).then_inc(S["b_copied"], 1)
                if n == 0:
                    act.wait_ge(S["dtd"], 2 * u + 2)
                for m in range(M):
                    first = lambda t: t.rearrange("p (b t) -> p b t", b=SB)[:, :, 1:]
                    ins = act.activation(first(dA[:, n % 2, m, :]), first(dt[:, par, m, :]), ACT.Exp,
                                         scale=nega[:, l, m, n:n + 1])
                ins.then_inc(S["expd"], 1)

            def prologue(l, s, v):
                act.wait_ge(S["small_in"], SMALL)
                act.activation(nega[:], nega[:], ACT.Exp).then_inc(S["start"], 1)
                norm_weights(l, v)
                for m in range(2 * M):
                    take(v, m, v % 2)
                silus(v, v % 2)
                rows(v, v % 2)
                for q in range(2):
                    for m in range(M)[half(q)]:
                        dt_parts(l, v, m, v % 2)
                    small_exp(v, q)
                for q in range(2):
                    logs(v, q)

            def scan(l, s, u, nxt):
                if isinstance(u, int) and u == 0:
                    act.wait_ge(S["start"], 4)
                for n in range(DS):
                    step(l, u, n, s % 2)
                    if nxt is None:
                        continue
                    nl, ns, v = nxt
                    par = ns % 2
                    if n == AT["norm_weights"]:
                        norm_weights(nl, v)
                    for m in range(2 * M):
                        if n == AT["take"][m]:
                            take(v, m, par)
                    if n == AT["silus"]:
                        silus(v, par)
                    if n == AT["rows"]:
                        rows(v, par)
                    for q in range(2):
                        if n == AT["dt_parts"][q]:
                            for m in range(M)[half(q)]:
                                dt_parts(nl, v, m, par)
                            small_exp(v, q)
                    for q in range(2):
                        if n == AT["logs"][q]:
                            logs(v, q)

            units(act, prologue, scan, lambda *a: None)

        @block.gpsimd
        def _(pool):
            def rstd_of(v):
                pool.wait_ge(S["ve"], v + 1)
                pool.tensor_tensor(rstd[:], vare[:], power[:], ALU.pow).then_inc(S["rstd_ready"], 1)

            def tap0(l, v, ms):
                for m in ms:
                    pool.wait_ge(S["ip_used"], v * 2 * M + m + 1)
                    gate(pool)
                    pool.tensor_scalar(cv[:, m].rearrange("p (b t) -> p b t", b=SB), xp[:, m, :, 0:SEQ],
                                       chan[:, l, CW, m:m + 1], chan[:, l, CB, m:m + 1],
                                       ALU.mult, ALU.add).then_inc(S["tap0"], 1)

            def dt_x(v, par, q):
                pool.wait_ge(S["dtd"], 2 * v + q + 1)
                pool.wait_ge(S["xc_ready"], (v + 1) * M)
                gate(pool)
                pool.tensor_tensor(du[:, par, half(q)], dt[:, par, half(q)], xc[:, half(q)], ALU.mult).then_inc(S["dud"], 1)

            def inputs(u, n, par, channels, dtx):
                g = u * DS + n
                pool.wait_ge(S["b_copied"], g + 1)
                pool.wait_ge(S["dud"], dtx)
                after(pool, "scan_done", g - 1)
                gate(pool)
                b = brow[:, n % 2].unsqueeze(1)
                shape = [P, channels.stop - channels.start, SEG]
                return pool.tensor_tensor(dBu[:, n % 2, channels], du[:, par, channels], b.broadcast_to(shape), ALU.mult)

            def ready(v, par):
                dt_x(v, par, 0)
                inputs(v, 0, par, half(0), 2 * v + 1)
                dt_x(v, par, 1)

            def prologue(l, s, v):
                rstd_of(v)
                pool.wait_ge(S["small_in"], SMALL)
                tap0(l, v, range(M))
                ready(v, v % 2)

            def scan(l, s, u, nxt):
                for n in range(DS):
                    inputs(u, n, s % 2, slice(0, M) if n else half(1), 2 * u + 2).then_inc(S["dbud"], 1)
                    if nxt is None:
                        continue
                    nl, ns, v = nxt
                    if n == AT["rstd"]:
                        rstd_of(v)
                    for m in range(M):
                        if n == AT["tap0"][m]:
                            tap0(nl, v, (m,))
                    if n == DS - 1:
                        ready(v, ns % 2)

            pool.memset(power[:], -0.5).then_inc(S["pow"], 1)
            pool.wait_ge(S["pow"], 1)
            pool.wait_ge(S["start"], 1)
            units(pool, prologue, scan, lambda *a: None)

        @block.tensor
        def _(pe):
            pe.sem_inc(S["op"], 1)
            pe.wait_ge(S["small_in"], SMALL)

            def transposes(v):
                pe.wait_ge(S["xn_ready"], (v + 1) * ST)
                pe.wait_ge(S["res"], (v - 2) * 2 + 1 if not isinstance(v, int) or v > 2 else 1)
                for k in range(KD):
                    for j in range(ST):
                        ins = pe.transpose(W[k][:, j * P:(j + 1) * P], xn[:, j, k * P:(k + 1) * P], ident[:])
                    ins.then_inc(S["tp"], 1)

            def in_proj(l, v, m):
                if m == 0:
                    pe.wait_ge(S["inw_in"], 16 * (l + 1))
                if m < 2:
                    pe.wait_ge(S["hT_ready"], (v + 1) * KD)
                else:
                    pe.wait_ge(S["ip_used"], v * 2 * M + m - 1)
                for k in range(KD):
                    ins = pe.matmul(W[m % 2][:], inw[:, k, m * P:(m + 1) * P], hT[:, k, :],
                                    start=(k == 0), stop=(k == KD - 1))
                ins.then_inc(S["ip"], 1)

            def x_proj(l, v):
                pe.wait_ge(S["ip_used"], (v + 1) * 2 * M)
                for m in range(M):
                    pe.wait_ge(S["xc_ready"], v * M + m + 1)
                    ins = pe.matmul(W[0][0:XPR, :], xpw[l][:, m, :], xc[:, m, :], start=(m == 0), stop=(m == M - 1))
                ins.then_inc(S["dbl"], 1)

            def dt_proj(l, v, m):
                if m == 0:
                    pe.wait_ge(S["dr_ready"], v + 1)
                elif m == 1:
                    pe.wait_ge(S["r1"], v + 1)
                else:
                    pe.wait_ge(S["dtp_used"], v * M + m - 1)
                pe.matmul(W[(m + 1) % 2][:], dtw[l][96:96 + RANK, m * P:(m + 1) * P], dr,
                          start=True, stop=True).then_inc(S["dtp"], 1)

            def out_proj(l, u, w, nxt=None):
                pe.wait_ge(S["yzd"], u)
                pe.wait_ge(S["dtp_used"], (nxt + 1) * M if nxt is not None else UNITS * M)
                for j in range(2 * w, 2 * w + 2):
                    for m in range(M):
                        ins = pe.matmul(W[j // 2][:, (j % 2) * DM:(j % 2 + 1) * DM], yz[:, m, j * P:(j + 1) * P],
                                        outw[l][:, m, :], start=(m == 0), stop=(m == M - 1))
                    if j % 2:
                        ins.then_inc(S["op"], 1)

            def row_b(u, n, par):
                g = u * DS + n
                pe.wait_ge(S["lo"], u + 1)
                after(pe, "b_copied", g)
                pe.matmul(Bp[:], pick[:, n, :], bc[:, par, :], start=True, stop=True).then_inc(S["b_ready"], 1)

            def row_c(u, n, par):
                g = u * DS + n
                after(pe, "hc_done", g)
                pe.matmul(Cp[:], pick[:, DS + n, :], bc[:, par, :], start=True, stop=True).then_inc(S["c_ready"], 1)

            def skips(l, u):
                after(pe, "yzd", u)
                pe.wait_ge(S["xc_ready"], (u + 1) * M)
                for m in range(M):
                    ins = pe.matmul(Y[:, m], skip[:, l, m, :], xc[:, m, :], start=True, stop=False)
                ins.then_inc(S["y_init"], 1)

            def add(u, n):
                pe.wait_ge(S["hc_done"], u * DS + n + 1)
                for m in range(M):
                    ins = pe.matmul(Y[:, m], ident[:], hC[:, n % 2, m], start=False, stop=(n == DS - 1))
                ins.then_inc(S["y_done"], 1)

            def prologue(l, s, v):
                transposes(v)
                for m in range(2 * M):
                    in_proj(l, v, m)
                pe.wait_ge(S["w_in"], WEIGHTS)
                x_proj(l, v)
                for m in range(M):
                    dt_proj(l, v, m)
                pe.wait_ge(S["diag"], LAYERS * M)
                row_b(v, 0, s % 2)
                row_c(v, 0, s % 2)
                row_b(v, 1, s % 2)

            def scan(l, s, u, nxt):
                skips(l, u)
                for n in range(DS):
                    if n + 2 < DS:
                        row_b(u, n + 2, s % 2)
                    elif nxt is not None:
                        row_b(nxt[2], n + 2 - DS, nxt[1] % 2)
                    if n + 1 < DS:
                        row_c(u, n + 1, s % 2)
                    elif nxt is not None:
                        row_c(nxt[2], 0, nxt[1] % 2)
                    add(u, n)
                    late = n in AT["out_proj"] and (not isinstance(u, int) or u > 0)
                    ul = l if not isinstance(s, int) or s > 0 else l - 1
                    if nxt is None:
                        if late:
                            out_proj(ul, u, AT["out_proj"].index(n))
                        continue
                    nl, ns, v = nxt
                    if n == AT["transposes"]:
                        transposes(v)
                    for m in range(2 * M):
                        if n == AT["in_proj"][m]:
                            in_proj(nl, v, m)
                    if n == AT["x_proj"]:
                        x_proj(nl, v)
                    for m in range(M):
                        if n == AT["dt_proj"][m]:
                            dt_proj(nl, v, m)
                    if late:
                        out_proj(ul, u, AT["out_proj"].index(n), v)

            units(pe, prologue, scan, lambda l, s, u: [out_proj(l, u, w) for w in range(2)])


HEADS, KV, HDIM = 16, 4, 16
GRP = HEADS // KV
SLOT = 32
EXP, TOP = 8, 2
CAPACITY = float(max(int(TOK * 1.25 / EXP), 4))


def blend(nc, A, x, name, wb_in, res_in, preload):
    fp32 = mybir.dt.float32
    ALU, ACT = mybir.AluOpType, mybir.ActivationFunctionType
    G = 4
    GROUPS = TILES // G
    from_dram = res_in is None
    with ExitStack() as ctx:
        sb = lambda n, shape: ctx.enter_context(nc.sbuf_tensor(name + n, shape, fp32))
        S = {n: ctx.enter_context(nc.semaphore(name + "_" + n)) for n in """weights residual stats means vare scale normed
            with_bias weighted summed shift""".split()}
        wb = sb("wb", [P, 2, DM])
        r = sb("r", [P, TILES, DM]) if from_dram else x
        v = x if from_dram else res_in
        stats = sb("stats", [P, 2, TILES, 6])
        mv = sb("mv", [P, 2, TILES, 2])
        rstd = sb("rstd", [P, 2, TILES])
        vare = sb("vare", [P, 2, TILES])
        half = sb("half", [P, TILES])
        shift = sb("shift", [P, 2, TILES])
        block = ctx.enter_context(nc.Block())
        tiles = lambda g: slice(g * G, (g + 1) * G)

        @block.sync
        def _(sp):
            sp.dma_start(wb[:].rearrange("p a d -> p (a d)"), wb_in.broadcast_to([P, 2 * DM])).then_inc(S["weights"], 16)
            if from_dram:
                sp.dma_start(r[:], A["x"]).then_inc(S["residual"], 16)
            preload(sp)

        @block.vector
        def _(dve):
            def moments(t, rnd, lo, hi):
                for j in range(lo, hi):
                    dve.bn_stats(stats[:, rnd, j, :], t[:, j, :]).then_inc(S["stats"], 1)
                dve.wait_ge(S["stats"], rnd * TILES + hi)
                for j in range(lo, hi):
                    dve.bn_aggr(mv[:, rnd, j, :], stats[:, rnd, j, :]).then_inc(S["means"], 1)

            def shifts(rnd, at, n):
                dve.wait_ge(S["scale"], n)
                dve.scalar_tensor_tensor(shift[:, rnd, at], mv[:, rnd, at, 0], -1.0, rstd[:, rnd, at],
                                         ALU.mult, ALU.mult).then_inc(S["shift"], 1)
            moments(v, 0, 0, TILES)
            shifts(0, slice(0, TILES), 1)
            dve.wait_ge(S["weights"], 16)
            if from_dram:
                dve.wait_ge(S["residual"], 16)
            bias = wb[:, 1].unsqueeze(1).broadcast_to([P, G, DM])

            def with_bias(g):
                dve.tensor_tensor(r[:, tiles(g)], r[:, tiles(g)], bias, ALU.add).then_inc(S["with_bias"], 1)
            with_bias(0)
            with_bias(1)
            for g in range(GROUPS):
                dve.wait_ge(S["weighted"], g + 1)
                dve.wait_ge(S["with_bias"], g + 1)
                dve.tensor_tensor(x[:, tiles(g)], v[:, tiles(g)], r[:, tiles(g)], ALU.add).then_inc(S["summed"], 1)
                if g + 2 < GROUPS:
                    with_bias(g + 2)
                dve.wait_ge(S["summed"], g + 1)
                moments(x, 1, g * G, (g + 1) * G)
                if g:
                    shifts(1, tiles(g - 1), g + 1)
            shifts(1, tiles(GROUPS - 1), GROUPS + 1)
            for j in range(TILES - G // 2, TILES):
                dve.tensor_scalar(x[:, j, :], x[:, j, :], mv[:, 1, j, 0:1], rstd[:, 1, j:j + 1], ALU.subtract, ALU.mult)

        @block.scalar
        def _(act):
            def norm(t, rnd, lo, hi):
                for j in range(lo, hi):
                    ins = act.activation(t[:, j, :], t[:, j, :], ACT.Identity, scale=rstd[:, rnd, j:j + 1], bias=shift[:, rnd, j:j + 1])
                return ins
            act.wait_ge(S["shift"], 1)
            for g in range(GROUPS):
                norm(v, 0, g * G, (g + 1) * G).then_inc(S["normed"], 1)
            for g in range(GROUPS):
                act.wait_ge(S["shift"], g + 2)
                norm(x, 1, g * G, (g + 1) * G if g < GROUPS - 1 else TILES - G // 2)

        @block.gpsimd
        def _(pool):
            def power(rnd, at, count, means):
                pool.wait_ge(S["means"], means)
                pool.tensor_scalar(vare[:, rnd, at], mv[:, rnd, at, 1], EPS, 0.0, ALU.add, ALU.add).then_inc(S["vare"], 1)
                pool.wait_ge(S["vare"], count + 1)
                pool.tensor_tensor(rstd[:, rnd, at], vare[:, rnd, at], half[:, at], ALU.pow).then_inc(S["scale"], 1)
            pool.memset(half[:], -0.5).then_inc(S["vare"], 1)
            power(0, slice(0, TILES), 1, TILES)
            pool.wait_ge(S["weights"], 16)
            for g in range(GROUPS):
                pool.wait_ge(S["normed"], g + 1)
                pool.tensor_tensor(v[:, tiles(g)], v[:, tiles(g)], wb[:, 0].unsqueeze(1).broadcast_to([P, G, DM]),
                                   ALU.mult).then_inc(S["weighted"], 1)
                if g >= 2:
                    power(1, tiles(g - 2), g, TILES + (g - 1) * G)
            for g in (GROUPS - 2, GROUPS - 1):
                power(1, tiles(g), g + 2, TILES + (g + 1) * G)


AHEAD = dict(q_parts=(0, 1), parts=(1, 2), turns=(2, 2, 3, 3, 4, 4, 5, 5, 6, 6),
             scores=(4, 4, 5, 5, 6, 6, 7, 7, 8, 8, 9, 9, 10, 10, 11, 11), max_parts=12, max_turn=13,
             x_copy=7, x_turn=8, x_taken=8, qkv=9, bias=9, rotate=9, out_take=(8, 15), out_turn=(9, 15),
             norm=(9, 15))


def attention_inputs(nc, ctx, A):
    fp32, bf16 = mybir.dt.float32, mybir.dt.bfloat16
    HW, KW = HEADS * HDIM, KV * HDIM
    w, loads = {}, []
    for name, shape, dt, src in (("identb", [P, P], bf16, A["identb"].bitcast(bf16)),
                                 ("pick", [3 * HEADS, HEADS, P], bf16, A["pickh"].bitcast(bf16)),
                                 ("wq", [P, KD, HW], fp32, A["wq"]),
                                 ("wkv", [P, KD, 2 * KW], fp32, A["wkv"]),
                                 ("bqkv", [P, HW + 2 * KW], fp32, A["bqkv"].broadcast_to([P, HW + 2 * KW])),
                                 ("rope", [P, BATCH * 2 * (HW + KW)], fp32, A["rope"].broadcast_to([P, BATCH * 2 * (HW + KW)]))):
        w[name] = ctx.enter_context(nc.sbuf_tensor("at_" + name, shape, dt))
        loads.append((w[name], src))
    loaded = ctx.enter_context(nc.semaphore("a_weights"))

    def load(sp):
        for dst, src in loads:
            sp.dma_start(dst[:], src).then_inc(loaded, 16)
    return w, loaded, 16 * len(loads), load


def attention(nc, A, x, ident, att, inputs):
    fp32, bf16 = mybir.dt.float32, mybir.dt.bfloat16
    ALU, ACT, AX = mybir.AluOpType, mybir.ActivationFunctionType, mybir.AxisListType
    HW = HEADS * HDIM
    KW = KV * HDIM
    BT = SEQ // P
    NP = 6
    PR = NP * HDIM
    PART = 3
    TURNS = (KV + HEADS) * BT // 4
    HALF = HEADS // 2
    weights, loaded, WEIGHTS, _ = inputs
    with ExitStack() as ctx:
        def sb(name, shape, dt=fp32):
            return ctx.enter_context(nc.sbuf_tensor("at_" + name, shape, dt))

        def pb(name, shape):
            return ctx.enter_context(nc.psum_tensor("ap_" + name, shape, fp32))

        identb, pick, wq, wkv, bqkv = (weights[n] for n in ("identb", "pick", "wq", "wkv", "bqkv"))
        rope = weights["rope"][:].rearrange("p (b k) -> p b k", b=BATCH)
        ctxT = sb("ctxT", [P, KD, SEQ])
        xb = sb("xb", [P, BT, DM])
        xT = sb("xT", [P, KD, SEQ])
        qkv = sb("qkv", [P, BT, HW + 2 * KW])
        rot = sb("rot", [P, BT, HW + KW])
        rest = sb("rest", [P, BT, HW + KW])
        qp = sb("qp", [P, BT, HEADS, NP, HDIM], bf16)
        kp = sb("kp", [P, BT, KV, NP, HDIM], bf16)
        vb = sb("vb", [P, 2, BT, KV, SLOT])
        qT = sb("qT", [PR, 2, HEADS, SEQ], bf16)
        kT = sb("kT", [PR, 2, KV, SEQ], bf16)
        top = sb("top", [P, BT, HEADS])
        topr = sb("topr", [P, BT, HEADS])
        topp = sb("topp", [P, BT, PART, HEADS], bf16)
        topT = sb("topT", [PART * HEADS, 2, SEQ], bf16)
        prob = sb("prob", [P, 2, BT, SEQ])
        outT = sb("outT", [P, 2, SEQ])
        inv = sb("inv", [P, BT, HALF])
        SC = [pb(f"scores{i}", [P, BT, SEQ]) for i in range(2)]
        ST_ = [pb(f"keyed{i}", [P, BT, SEQ]) for i in range(2)]
        OP = [pb(f"out{i}", [P, 2, SEQ]) for i in range(2)]
        W = [pb(f"work{i}", [P, BT * SEQ]) for i in range(2)]
        S = {n: ctx.enter_context(nc.semaphore("a_" + n)) for n in """ctx x_copied x_turned x_taken projected biased
            own spun shifted rotated q_first q_rest q_second parts turned taken scored top max_own max_parts
            max_turned max_taken keyed prob pv out_taken out_turned inv norm gate""".split()}
        block = ctx.enter_context(nc.Block())

        def after(eng, name, value):
            if not isinstance(value, int) or value > 0:
                eng.wait_ge(S[name], value)

        def gate(eng):
            eng.sem_inc(S["gate"], 1)

        def batches(eng, early, late, heads):
            early(0)
            late(0, 0)
            early(1)
            with eng.Fori(0, BATCH // 2 - 1) as r:
                for par in range(2):
                    b = 2 * r + par
                    heads(b, par, b + 1, b + 2)
            heads(BATCH - 2, 0, BATCH - 1, None)
            heads(BATCH - 1, 1, None, None)

        @block.sync
        def _(sp):
            sp.dma_start(ctxT[:], A["ctxT"][0]).then_inc(S["ctx"], 16)
            with sp.Fori(1, BATCH) as e:
                sp.wait_ge(S["projected"], e)
                sp.dma_start(ctxT[:], A["ctxT"][bass.ds(e, 1)].rearrange("a p k t -> p (a k) t")).then_inc(S["ctx"], 16)

        heads_of = lambda t, n: t.rearrange("p b (h d) -> p b h d", h=n)

        @block.vector
        def _(dve):
            K = 2
            dve.sem_inc(S["norm"], 2)
            dve.memset(vb[:], 0.0).then_inc(S["own"], 1)
            dve.wait_ge(S["own"], 1)
            dve.memset(vb[:, :, :, :, HDIM:HDIM + 1], 1.0).then_inc(S["own"], 1)
            dve.wait_ge(S["own"], 2)
            dve.wait_ge(loaded, WEIGHTS)

            def bias(e):
                dve.wait_ge(S["projected"], e + 1)
                after(dve, "rotated", e)
                row = bqkv[:].unsqueeze(1).broadcast_to([P, BT, HW + 2 * KW])
                dve.tensor_tensor(qkv[:, :, 0:HW], W[0][:].rearrange("p (b k) -> p b k", b=BT), row[:, :, 0:HW], ALU.add)
                dve.tensor_tensor(qkv[:, :, HW:], W[1][:, 0:BT * 2 * KW].rearrange("p (b k) -> p b k", b=BT),
                                  row[:, :, HW:], ALU.add).then_inc(S["biased"], 1)

            def k_parts(v, par):
                dve.wait_ge(S["rotated"], v + 1)
                after(dve, "turned", v * TURNS)
                k, r = heads_of(rot[:, :, HW:], KV), heads_of(rest[:, :, HW:], KV)
                for slot in (0, 3, 5):
                    ins = dve.tensor_copy(kp[:, :, :, slot, :], k)
                ins.then_inc(S["own"], 1)
                dve.wait_ge(S["biased"], v + 1)
                dve.tensor_copy(vb[:, par, :, :, 0:HDIM], heads_of(qkv[:, :, HW + KW:], KV))
                dve.wait_ge(S["own"], K * v + 3)
                dve.tensor_tensor(r, k, kp[:, :, :, 0, :], ALU.subtract)
                dve.wait_ge(S["q_first"], v + 1)
                for j in range(BT):
                    ins = dve.tensor_tensor(heads_of(rest[:, j:j + 1, 0:HW], HEADS)[:, 0], heads_of(rot[:, j:j + 1, 0:HW], HEADS)[:, 0],
                                            qp[:, j, :, 0, :], ALU.subtract)
                ins.then_inc(S["q_rest"], 1)

            def last_parts(v):
                r = heads_of(rest[:, :, HW:], KV)
                dve.wait_ge(S["q_rest"], v + 1)
                for slot in (1, 4):
                    ins = dve.tensor_copy(kp[:, :, :, slot, :], r)
                ins.then_inc(S["own"], 1)
                dve.wait_ge(S["own"], K * v + 4)
                dve.tensor_tensor(kp[:, :, :, 2, :], r, kp[:, :, :, 1, :], ALU.subtract)
                dve.wait_ge(S["q_second"], v + 1)
                for j in range(BT):
                    ins = dve.tensor_tensor(qp[:, j, :, 5, :], heads_of(rest[:, j:j + 1, 0:HW], HEADS)[:, 0],
                                            qp[:, j, :, 3, :], ALU.subtract)
                ins.then_inc(S["parts"], 1)

            def maximum(v, h):
                dve.wait_ge(S["scored"], v * HEADS + h + 1)
                dve.tensor_reduce(top[:, :, h], SC[h % 2][:], AX.X, ALU.max, negate=True).then_inc(S["top"], 1)

            def max_parts(v):
                dve.wait_ge(S["top"], (v + 1) * HEADS)
                after(dve, "max_turned", v)
                dve.tensor_copy(topp[:, :, 0, :], top[:]).then_inc(S["max_own"], 1)
                dve.wait_ge(S["max_own"], 3 * v + 1)
                dve.tensor_tensor(topr[:], top[:], topp[:, :, 0, :], ALU.subtract).then_inc(S["max_own"], 1)
                dve.wait_ge(S["max_own"], 3 * v + 2)
                dve.tensor_copy(topp[:, :, 1, :], topr[:]).then_inc(S["max_own"], 1)
                dve.wait_ge(S["max_own"], 3 * v + 3)
                dve.tensor_tensor(topp[:, :, 2, :], topr[:], topp[:, :, 1, :], ALU.subtract).then_inc(S["max_parts"], 1)

            def normalise(b, half):
                dve.wait_ge(S["out_turned"], 2 * b + half + 1)
                got = OP[half][:].rearrange("p b (h d) -> p b h d", d=SLOT)
                dve.wait_ge(S["norm"], 2 * b + half + 2)
                dve.reciprocal(inv[:], got[:, :, :, HDIM]).then_inc(S["inv"], 1)
                dve.wait_ge(S["inv"], 2 * b + half + 1)
                out = att[:, bass.ds(b * BT, BT), half * HALF * HDIM:(half + 1) * HALF * HDIM]
                dve.tensor_tensor(heads_of(out, HALF), got[:, :, :, 0:HDIM],
                                  inv[:].unsqueeze(3).broadcast_to([P, BT, HALF, HDIM]), ALU.mult).then_inc(S["norm"], 1)

            def late(v, par):
                k_parts(v, par)
                last_parts(v)
                for h in range(HEADS):
                    maximum(v, h)
                max_parts(v)

            def heads(b, par, v, e):
                for h in range(HEADS):
                    if v is not None:
                        if h == AHEAD["parts"][0]:
                            k_parts(v, 1 - par)
                        if h == AHEAD["parts"][1]:
                            last_parts(v)
                        for g in range(HEADS):
                            if h == AHEAD["scores"][g]:
                                maximum(v, g)
                        if h == AHEAD["max_parts"]:
                            max_parts(v)
                    if e is not None and h == AHEAD["bias"]:
                        bias(e)
                    for half in range(2):
                        if h == AHEAD["norm"][half]:
                            normalise(b, half)

            batches(dve, bias, late, heads)

        @block.gpsimd
        def _(pool):
            pool.wait_ge(loaded, WEIGHTS)

            def rotate(e):
                pool.wait_ge(S["biased"], e + 1)
                after(pool, "parts", e)
                gate(pool)
                rb = rope[:, bass.ds(e, 1), :] if not isinstance(e, int) else rope[:, e:e + 1, :]
                kinds = ((0, HEADS, HEADS // 2, 0), (HW, KV, KV // 2, 2 * HW))
                for lo, n, cut, c0 in kinds:
                    w = n * HDIM
                    part = lambda t, a, z: heads_of(t, n)[:, :, :, a:z]
                    for j in range(BT):
                        q1 = qkv[:, j:j + 1, lo:lo + w]
                        r1 = rot[:, j:j + 1, lo:lo + w]
                        sn = rb[:, :, c0 + w:c0 + 2 * w]
                        first = HDIM - cut
                        pool.tensor_tensor(part(r1, 0, first), part(q1, cut, HDIM), part(sn, 0, first), ALU.mult)
                        ins = pool.tensor_tensor(part(r1, first, HDIM), part(q1, 0, cut), part(sn, first, HDIM), ALU.mult)
                ins.then_inc(S["spun"], 1)
                pool.wait_ge(S["spun"], e + 1)
                gate(pool)
                for lo, n, cut, c0 in kinds:
                    w = n * HDIM
                    for j in range(BT):
                        ins = pool.tensor_tensor(rot[:, j:j + 1, lo:lo + w], rot[:, j:j + 1, lo:lo + w],
                                                 rb[:, :, c0:c0 + w], ALU.add)
                ins.then_inc(S["shifted"], 1)
                pool.wait_ge(S["shifted"], e + 1)
                pool.tensor_tensor(rot[:], rot[:], qkv[:, :, 0:HW + KW], ALU.mult).then_inc(S["rotated"], 1)

            def heads(b, par, v, e):
                if e is not None:
                    rotate(e)

            batches(pool, rotate, lambda v, par: None, heads)

        @block.scalar
        def _(act):
            act.sem_inc(S["prob"], 2)

            def x_copy(e):
                after(act, "x_turned", e)
                gate(act)
                xs = x[:, bass.ds(e * BT, BT), :] if not isinstance(e, int) else x[:, e * BT:(e + 1) * BT, :]
                act.activation(xb[:], xs, ACT.Copy).then_inc(S["x_copied"], 1)

            def x_taken(e):
                act.wait_ge(S["x_turned"], e + 1)
                act.activation(xT[:], W[0][:].rearrange("p (k t) -> p k t", k=KD), ACT.Copy).then_inc(S["x_taken"], 1)

            def q_part(v, n):
                act.wait_ge(S["rotated" if n == 0 else "q_rest"], v + 1)
                lo, hi = ((0, 3), (3, 5))[n]
                for j in range(BT):
                    q = heads_of((rot, rest)[n][:, j:j + 1, 0:HW], HEADS)[:, 0]
                    ins = act.activation(qp[:, j, :, lo:hi, :], q.unsqueeze(2).broadcast_to([P, HEADS, hi - lo, HDIM]), ACT.Copy)
                ins.then_inc(S["q_second" if n else "q_first"], 1)

            def take(v, par, g):
                act.wait_ge(S["turned"], v * TURNS + g + 1)
                kbanks = KV // 2
                dst = kT[:, par, 2 * g:2 * g + 2, :] if g < kbanks else qT[:, par, 2 * (g - kbanks):2 * (g - kbanks) + 2, :]
                act.activation(dst, W[g % 2][0:PR, :].rearrange("p (h t) -> p h t", h=2), ACT.Copy).then_inc(S["taken"], 1)

            def take_max(v, par):
                act.wait_ge(S["max_turned"], v + 1)
                act.activation(topT[:, par, :], W[0][0:PART * HEADS, 0:SEQ], ACT.Copy).then_inc(S["max_taken"], 1)

            def out_take(b, half):
                act.wait_ge(S["pv"], b * HEADS + (half + 1) * HALF + 2)
                act.activation(outT[:], OP[half][:], ACT.Copy).then_inc(S["out_taken"], 1)

            def early(e):
                x_copy(e)
                x_taken(e)
                if e == 1:
                    take_max(0, 0)

            def late(v, par):
                for n in range(2):
                    q_part(v, n)
                for g in range(TURNS):
                    take(v, par, g)

            def heads(b, par, v, e):
                for h in range(HEADS):
                    act.wait_ge(S["keyed"], b * HEADS + h + 1)
                    act.wait_ge(S["pv"], b * HEADS + h + 1)
                    act.activation(prob[:, h % 2], ST_[h % 2][:], ACT.Exp).then_inc(S["prob"], 1)
                    if v is not None:
                        for n in range(2):
                            if h == AHEAD["q_parts"][n]:
                                q_part(v, n)
                        for g in range(TURNS):
                            if h == AHEAD["turns"][g]:
                                take(v, 1 - par, g)
                    if e is not None:
                        if h == AHEAD["x_copy"]:
                            x_copy(e)
                        if h == AHEAD["x_taken"]:
                            x_taken(e)
                    if v is not None and h == AHEAD["max_turn"]:
                        take_max(v, 1 - par)
                    for half in range(2):
                        if h == AHEAD["out_take"][half]:
                            out_take(b, half)

            batches(act, early, late, heads)

        @block.tensor
        def _(pe):
            pe.sem_inc(S["pv"], 2)
            pe.wait_ge(loaded, WEIGHTS)

            def x_turn(e):
                pe.wait_ge(S["x_copied"], e + 1)
                after(pe, "taken", e * TURNS)
                for k in range(KD):
                    for j in range(BT):
                        ins = pe.transpose(W[0][:, k * SEQ + j * P:k * SEQ + (j + 1) * P], xb[:, j, k * P:(k + 1) * P], ident[:])
                ins.then_inc(S["x_turned"], 1)

            def project(e):
                pe.wait_ge(S["ctx"], 16 * e + 16)
                for j in range(BT):
                    for k in range(KD):
                        pe.matmul(W[1][:, j * 2 * KW:(j + 1) * 2 * KW], ctxT[:, k, j * P:(j + 1) * P], wkv[:, k, :],
                                  start=(k == 0), stop=(k == KD - 1))
                pe.wait_ge(S["x_taken"], e + 1)
                for j in range(BT):
                    for k in range(KD):
                        ins = pe.matmul(W[0][:, j * HW:(j + 1) * HW], xT[:, k, j * P:(j + 1) * P], wq[:, k, :],
                                        start=(k == 0), stop=(k == KD - 1))
                ins.then_inc(S["projected"], 1)

            def turn(v, g):
                if g == 0:
                    pe.wait_ge(S["parts"], v + 1)
                    after(pe, "max_taken", v)
                if g >= 2:
                    pe.wait_ge(S["taken"], v * TURNS + g - 1)
                kbanks = KV // 2
                src, h0 = (kp, 2 * g) if g < kbanks else (qp, 2 * (g - kbanks))
                for i in range(2):
                    for j in range(BT):
                        at = i * SEQ + j * P
                        ins = pe.matmul(W[g % 2][0:PR, at:at + P], src[:, j, h0 + i].rearrange("p n d -> p (n d)"), identb[:],
                                        start=True, stop=True)
                ins.then_inc(S["turned"], 1)

            def score(v, par, h):
                pe.wait_ge(S["taken"], v * TURNS + KV // 2 + h // 2 + 1)
                after(pe, "top", v * HEADS + h - 1)
                for j in range(BT):
                    ins = pe.matmul(SC[h % 2][:, j], qT[:, par, h, j * P:(j + 1) * P], kT[:, par, h // GRP, :],
                                    start=True, stop=True)
                ins.then_inc(S["scored"], 1)

            def max_turn(v, e):
                pe.wait_ge(S["max_parts"], v + 1)
                if e is not None:
                    pe.wait_ge(S["biased"], e + 1)
                for j in range(BT):
                    ins = pe.matmul(W[0][0:PART * HEADS, j * P:(j + 1) * P], topp[:, j].rearrange("p n h -> p (n h)"), identb[:],
                                    start=True, stop=True)
                ins.then_inc(S["max_turned"], 1)

            def keyed(b, par, h):
                if h == 0:
                    pe.wait_ge(S["max_taken"], b + 1)
                pe.wait_ge(S["prob"], b * HEADS + h + 1)
                for j in range(BT):
                    pe.matmul(ST_[h % 2][:, j], kT[:, par, h // GRP, j * P:(j + 1) * P], qT[:, par, h, :], start=True, stop=False)
                    ins = pe.matmul(ST_[h % 2][:, j], pick[:, h, :], topT[:, par, :], start=False, stop=True)
                ins.then_inc(S["keyed"], 1)

            def values(b, par, h):
                half, i = divmod(h, HALF)
                if i == 0:
                    pe.wait_ge(S["norm"], 2 * b + half + 1)
                pe.wait_ge(S["prob"], b * HEADS + h + 3)
                rows = slice(i % 4 * SLOT, (i % 4 + 1) * SLOT)
                for j in range(BT):
                    ins = pe.matmul(OP[half][rows, i // 4, :], vb[:, par, j, h // GRP, :], prob[:, h % 2, j, :],
                                    start=(j == 0), stop=(j == BT - 1))
                ins.then_inc(S["pv"], 1)

            def out_turn(b, half):
                pe.wait_ge(S["out_taken"], 2 * b + half + 1)
                for j in range(BT):
                    for n in range(2):
                        ins = pe.transpose(OP[half][:, j, n * P:(n + 1) * P], outT[:, n, j * P:(j + 1) * P], ident[:])
                ins.then_inc(S["out_turned"], 1)

            def early(e):
                x_turn(e)
                project(e)
                if e == 1:
                    max_turn(0, 1)
                    keyed(0, 0, 0)

            def late(v, par):
                for g in range(TURNS):
                    turn(v, g)
                for h in range(HEADS):
                    score(v, par, h)

            def heads(b, par, v, e):
                for h in range(HEADS):
                    if h + 1 < HEADS:
                        keyed(b, par, h + 1)
                    elif v is not None:
                        keyed(v, 1 - par, 0)
                    if v is not None:
                        for g in range(TURNS):
                            if h == AHEAD["turns"][g]:
                                turn(v, g)
                        for g in range(HEADS):
                            if h == AHEAD["scores"][g]:
                                score(v, 1 - par, g)
                    if e is not None:
                        if h == AHEAD["x_turn"]:
                            x_turn(e)
                        if h == AHEAD["qkv"]:
                            project(e)
                    if v is not None and h == AHEAD["max_turn"]:
                        max_turn(v, e)
                    values(b, par, h)
                    for half in range(2):
                        if h == AHEAD["out_turn"][half]:
                            out_turn(b, half)

            batches(pe, early, late, heads)


def moe_inputs(nc, ctx, A):
    fp32, bf16 = mybir.dt.float32, mybir.dt.bfloat16
    w, loads = {}, []
    for name, shape, dt, src in (("rw", [P, KD, EXP], fp32, A["rw"]),
                                 ("rb", [P, EXP], fp32, A["rb"].broadcast_to([P, EXP])),
                                 ("iota", [P, EXP], fp32, A["iota"].broadcast_to([P, EXP])),
                                 ("identb", [P, P], bf16, A["identb"].bitcast(bf16)),
                                 ("picke", [96, EXP, P], bf16, A["picke"].bitcast(bf16)),
                                 ("b1", [P, KD, EXP], fp32, A["b1"]),
                                 ("b2", [EXP, DM], fp32, A["b2"])):
        w[name] = ctx.enter_context(nc.sbuf_tensor("mo_" + name, shape, dt))
        loads.append((w[name], src))
    for name in ("w1", "w2"):
        w[name] = ctx.enter_context(nc.sbuf_tensor("mo_" + name, [P, 2, KD, DM], fp32))
    loaded = ctx.enter_context(nc.semaphore("m_weights"))
    arrived = [ctx.enter_context(nc.semaphore(f"m_expert{par}")) for par in range(2)]

    def load(sp):
        for dst, src in loads:
            sp.dma_start(dst[:], src).then_inc(loaded, 16)
        for par in range(2):
            sp.dma_start(w["w1"][:, par], A["w1"][par]).then_inc(arrived[par], 16)
            sp.dma_start(w["w2"][:, par], A["w2"][par]).then_inc(arrived[par], 16)
    return w, loaded, 16 * len(loads), arrived, load


def moe(nc, A, x, ident, inputs):
    fp32, bf16 = mybir.dt.float32, mybir.dt.bfloat16
    ALU, ACT, AX = mybir.AluOpType, mybir.ActivationFunctionType, mybir.AxisListType
    CH = 512
    CHUNKS = TOK // CH
    CT = CH // P
    with ExitStack() as ctx:
        sb = lambda n, shape, dt=fp32: ctx.enter_context(nc.sbuf_tensor("mo_" + n, shape, dt))
        sem = lambda n: ctx.enter_context(nc.semaphore("m_" + n))
        weights, loaded, NW, arrived, _ = inputs
        rw, rb, iota, identb, picke, b1, b2, w1, w2 = (weights[n] for n in
                                                       "rw rb iota identb picke b1 b2 w1 w2".split())
        b1e = sb("b1e", [P, 2, KD])
        xT = sb("xT", [P, KD, TOK])
        ones = sb("ones", [P, 1])
        lg = sb("lg", [P, TILES, EXP])
        tmp = sb("tmp", [P, TILES, EXP])
        one = [sb(f"hot{k}", [P, TILES, EXP]) for k in range(TOP)]
        mask = sb("mask", [P, TILES, EXP])
        rmax = sb("rmax", [P, TILES])
        best = sb("best", [P, TILES, 8])
        besti = sb("besti", [P, TILES, 8], mybir.dt.uint32)
        bestf = sb("bestf", [P, TILES, 8])
        norm2 = sb("norm2", [P, TILES])
        mres = sb("mres", [P, TILES, EXP])
        parts = sb("parts", [P, TILES, 96], bf16)
        maskT = sb("maskT", [EXP, TOK])
        partsT = sb("partsT", [96, TOK], bf16)
        mrow = sb("mrow", [P, 2, TOK])
        hid = sb("hid", [P, 2, KD, CH])
        act_ = sb("act", [P, 2, KD, CH])
        stats = sb("stats", [P, TILES, 6])
        mv = sb("mv", [P, TILES, 2])
        rstd = sb("rstd", [P, TILES])
        vare = sb("vare", [P, TILES])
        half = sb("half", [P, CT])
        S = {n: sem(n) for n in """x_turned x_copied logits own router_exp masks masks_turned masks_copied row
            row_copied bias_copied stored hidden scaled gelu product summed done means variance rstd normed""".split()}

        with ExitStack() as ps:
            turned = [ps.enter_context(nc.psum_tensor(f"mo_t{i}", [P, CH], fp32)) for i in range(2)]
            router = ps.enter_context(nc.psum_tensor("mo_router", [P, CH], fp32))
            LG = router[:, 0:TILES * EXP].rearrange("p (t e) -> p t e", e=EXP)
            CS = router[0:EXP, TILES * EXP:TILES * EXP + TOP]
            PT = [ps.enter_context(nc.psum_tensor(f"mo_pt{i}", [96, CH], bf16)) for i in range(2)]
            IN = [ps.enter_context(nc.psum_tensor(f"mo_in{i}", [P, 2, DM], fp32)) for i in range(2)]
            block = ps.enter_context(nc.Block())

            @block.tensor
            def _(pe):
                def turn_x(c):
                    for k in range(KD):
                        n = c * KD + k
                        if n >= 2:
                            pe.wait_ge(S["x_copied"], n - 1)
                        for j in range(CT):
                            last = pe.transpose(turned[n % 2][:, j * P:(j + 1) * P], x[:, c * CT + j, k * P:(k + 1) * P], ident[:])
                        last.then_inc(S["x_turned"], 1)

                def logits(c):
                    pe.wait_ge(S["x_copied"], (c + 1) * KD)
                    for t in range(c * CT, (c + 1) * CT):
                        for k in range(KD):
                            last = pe.matmul(LG[:, t], xT[:, k, t * P:(t + 1) * P], rw[:, k, :], start=(k == 0), stop=(k == KD - 1))
                    return last
                turn_x(0)
                pe.wait_ge(loaded, NW)
                for c in range(CHUNKS):
                    if c + 1 < CHUNKS:
                        turn_x(c + 1)
                    last = logits(c)
                last.then_inc(S["logits"], 1)
                pe.wait_ge(S["masks"], 1)
                for k in range(TOP):
                    for t in range(TILES):
                        last = pe.matmul(CS[:, k:k + 1], one[k][:, t, :], ones[:], start=(t == 0), stop=(t == TILES - 1))
                last.then_inc(S["masks_turned"], 1)
                pe.wait_ge(S["masks"], 2)

                def turn_masks(c):
                    if c >= 2:
                        pe.wait_ge(S["masks_copied"], 2 * (c - 1))
                    for j in range(CT):
                        pe.transpose(turned[c % 2][0:EXP, j * P:(j + 1) * P], mask[:, c * CT + j, :], ident[:])
                        last = pe.transpose(PT[c % 2][:, j * P:(j + 1) * P], parts[:, c * CT + j, :], identb[:])
                    last.then_inc(S["masks_turned"], 1)

                def bias_terms(c):
                    pe.wait_ge(S["masks_copied"], 2 * (c + 1))
                    for t in range(c * CT, (c + 1) * CT):
                        w, half = divmod(t, 2)
                        if half == 0 and w >= 2:
                            pe.wait_ge(S["done"], w - 1)
                        last = pe.matmul(IN[w % 2][:, half], maskT[:, t * P:(t + 1) * P], b2[:], start=True, stop=True)
                        if half:
                            last.then_inc(S["product"], 1)
                turn_masks(0)
                for c in range(CHUNKS):
                    if c + 1 < CHUNKS:
                        turn_masks(c + 1)
                    bias_terms(c)

            @block.scalar
            def _(act):
                n = 0
                for c in range(CHUNKS):
                    for k in range(KD):
                        act.wait_ge(S["x_turned"], n + 1)
                        act.activation(xT[:, k, c * CH:(c + 1) * CH], turned[n % 2][:], ACT.Copy).then_inc(S["x_copied"], 1)
                        n += 1
                act.wait_ge(S["router_exp"], 1)
                act.activation(tmp[:], tmp[:], ACT.Exp).then_inc(S["router_exp"], 1)
                for c in range(CHUNKS):
                    act.wait_ge(S["masks_turned"], c + 2)
                    act.activation(maskT[:, c * CH:(c + 1) * CH], turned[c % 2][0:EXP, :], ACT.Copy).then_inc(S["masks_copied"], 1)
                    act.activation(partsT[:, c * CH:(c + 1) * CH], PT[c % 2][:], ACT.Copy).then_inc(S["masks_copied"], 1)

            @block.vector
            def _(dve):
                n = [0]

                def do(ins):
                    ins.then_inc(S["own"], 1)
                    n[0] += 1
                    dve.wait_ge(S["own"], n[0])
                per = lambda a: a.unsqueeze(2).broadcast_to([P, TILES, EXP])
                do(dve.memset(ones[:], 1.0))
                do(dve.memset(parts[:], 0.0))
                dve.wait_ge(loaded, NW)
                dve.wait_ge(S["logits"], 1)
                do(dve.tensor_tensor(lg[:], LG, rb[:].unsqueeze(1).broadcast_to([P, TILES, EXP]), ALU.add))
                do(dve.tensor_reduce(rmax[:], lg[:], AX.X, ALU.max))
                dve.tensor_tensor(tmp[:], lg[:], per(rmax[:]), ALU.subtract).then_inc(S["router_exp"], 1)
                dve.wait_ge(S["router_exp"], 2)
                do(dve.tensor_reduce(norm2[:], tmp[:], AX.X, ALU.add))
                do(dve.reciprocal(norm2[:], norm2[:]))
                do(dve.tensor_tensor(lg[:], tmp[:], per(norm2[:]), ALU.mult))
                for t in range(TILES):
                    dve.max(best[:, t, :], lg[:, t, :]).then_inc(S["own"], 1)
                n[0] += TILES
                dve.wait_ge(S["own"], n[0])
                for t in range(TILES):
                    dve.max_index(besti[:, t, :], best[:, t, :], lg[:, t, :]).then_inc(S["own"], 1)
                n[0] += TILES
                dve.wait_ge(S["own"], n[0])
                do(dve.tensor_copy(bestf[:], besti[:]))
                do(dve.tensor_tensor(norm2[:], best[:, :, 0], best[:, :, 1], ALU.add))
                do(dve.reciprocal(norm2[:], norm2[:]))
                do(dve.tensor_tensor(best[:], best[:], per(norm2[:]), ALU.mult))
                for k in range(TOP):
                    do(dve.tensor_tensor(one[k][:], iota[:].unsqueeze(1).broadcast_to([P, TILES, EXP]),
                                         per(bestf[:, :, k]), ALU.is_equal))
                    do(dve.tensor_tensor(one[k][:], one[k][:], per(best[:, :, k]), ALU.mult))
                dve.tensor_tensor(mask[:], one[0][:], one[1][:], ALU.add).then_inc(S["masks"], 1)
                dve.wait_ge(S["masks"], 1)
                dve.wait_ge(S["masks_turned"], 1)
                do(dve.tensor_tensor(mask[0:EXP, 0, 0:TOP], mask[0:EXP, 0, 0:TOP], CS, ALU.add))
                do(dve.tensor_scalar(mask[:], mask[:], CAPACITY, None, ALU.min))
                do(dve.tensor_copy(parts[:, :, 0:EXP], mask[:]))
                do(dve.tensor_tensor(mres[:], mask[:], parts[:, :, 0:EXP], ALU.subtract))
                do(dve.tensor_copy(parts[:, :, 32:32 + EXP], mres[:]))
                dve.tensor_tensor(parts[:, :, 64:64 + EXP], mres[:], parts[:, :, 32:32 + EXP], ALU.subtract).then_inc(S["masks"], 1)
                for w in range(TILES // 2):
                    dve.wait_ge(S["product"], w + 1)
                    dve.tensor_tensor(x[:, 2 * w:2 * w + 2, :], x[:, 2 * w:2 * w + 2, :], IN[w % 2][:], ALU.add).then_inc(S["done"], 1)

        with ExitStack() as ps:
            HP = [ps.enter_context(nc.psum_tensor(f"mo_h{i}", [P, CH], fp32)) for i in range(2)]
            MR = [ps.enter_context(nc.psum_tensor(f"mo_mr{i}", [P, CH], fp32)) for i in range(2)]
            OP = [ps.enter_context(nc.psum_tensor(f"mo_o{i}", [P, 2, DM], fp32)) for i in range(4)]
            block = ps.enter_context(nc.Block())
            PAIRS = EXP // 2
            HPE = CHUNKS * KD
            OPE = TILES // 2
            OB = TILES // 2

            def experts(eng, first, expert):
                first()
                with eng.Fori(0, PAIRS - 1) as r:
                    for par in range(2):
                        expert(2 * r + par, par, 2 * r + par + 1)
                expert(EXP - 2, 0, EXP - 1)
                expert(EXP - 1, 1, None)

            @block.sync
            def _(sp):
                with sp.Fori(1, PAIRS) as r:
                    for par in range(2):
                        sp.wait_ge(S["product"], OB + (2 * r - 1 + par) * OPE)
                        for w, name in ((w1, "w1"), (w2, "w2")):
                            src = A[name][bass.ds(2 * r + par, 1)].rearrange("a p k d -> p (a k) d")
                            sp.dma_start(w[:, par], src).then_inc(arrived[par], 16)
                for c in range(CHUNKS):
                    sp.wait_ge(S["normed"], (c + 1) * CT)
                    sp.dma_start(A["out"][:, c * CT:(c + 1) * CT, :], x[:, c * CT:(c + 1) * CT, :]).then_inc(S["stored"], 16)
                sp.wait_ge(S["stored"], 16 * CHUNKS)

            @block.tensor
            def _(pe):
                def weights_row(e, c):
                    if not isinstance(e, int) or e * CHUNKS + c >= 2:
                        pe.wait_ge(S["row_copied"], e * CHUNKS + c - 1)
                    sel = picke[:, e, :] if isinstance(e, int) else picke[:, bass.ds(e, 1), :].rearrange("p a c -> p (a c)")
                    pe.matmul(MR[c % 2][:], sel, partsT[:, c * CH:(c + 1) * CH], start=True, stop=True).then_inc(S["row"], 1)

                def up(e, par, c):
                    if c == 0:
                        pe.wait_ge(arrived[par], (e - par) * 16 + 32)
                    for m in range(KD):
                        i = c * KD + m
                        pe.wait_ge(S["scaled"], e * HPE + i + 1)
                        for k in range(KD):
                            last = pe.matmul(HP[i % 2][:], w1[:, par, k, m * P:(m + 1) * P],
                                             xT[:, k, c * CH:(c + 1) * CH], start=(k == 0), stop=(k == KD - 1))
                        last.then_inc(S["hidden"], 1)

                def down(e, par, c):
                    pe.wait_ge(S["gelu"], e * HPE + (c + 1) * KD + 4)
                    for w in range(2):
                        o = c * 2 + w
                        pe.wait_ge(S["summed"], e * TILES + 2 * o + 2)
                        for j in (2 * w, 2 * w + 1):
                            for k in range(KD):
                                last = pe.matmul(OP[o % 4][:, j % 2], act_[:, c % 2, k, j * P:(j + 1) * P],
                                                 w2[:, par, k, :], start=(k == 0), stop=(k == KD - 1))
                        last.then_inc(S["product"], 1)

                def first():
                    for c in range(CHUNKS):
                        weights_row(0, c)
                    up(0, 0, 0)

                def expert(e, par, nxt):
                    for c in range(CHUNKS):
                        if c + 1 < CHUNKS:
                            up(e, par, c + 1)
                        elif nxt is not None:
                            up(nxt, 1 - par, 0)
                        if nxt is not None:
                            weights_row(nxt, c)
                        down(e, par, c)
                experts(pe, first, expert)

            @block.scalar
            def _(act):
                act.sem_inc(S["gelu"], 4)

                def row(e, par, c):
                    act.wait_ge(S["row"], e * CHUNKS + c + 1)
                    act.activation(mrow[:, par, c * CH:(c + 1) * CH], MR[c % 2][:], ACT.Copy).then_inc(S["row_copied"], 1)

                def first():
                    for c in range(CHUNKS):
                        row(0, 0, c)

                def expert(e, par, nxt):
                    be = b1[:, :, e] if isinstance(e, int) else b1[:, :, bass.ds(e, 1)].rearrange("p k a -> p (k a)")
                    act.activation(b1e[:, par], be, ACT.Copy).then_inc(S["bias_copied"], 1)
                    act.wait_ge(S["bias_copied"], e + 1)
                    for c in range(CHUNKS):
                        for m in range(KD):
                            i = c * KD + m
                            act.wait_ge(S["scaled"], e * HPE + i + 3)
                            act.wait_ge(S["product"], OB + e * OPE + 2 * c - 2)
                            act.activation(act_[:, c % 2, m], hid[:, c % 2, m], ACT.Gelu,
                                           bias=b1e[:, par, m:m + 1]).then_inc(S["gelu"], 1)
                        if nxt is not None:
                            row(nxt, 1 - par, c)
                experts(act, first, expert)

            @block.vector
            def _(dve):
                dve.sem_inc(S["scaled"], 2)
                dve.sem_inc(S["summed"], 8)

                def scale(e, par, c):
                    for m in range(KD):
                        i = c * KD + m
                        dve.wait_ge(S["hidden"], e * HPE + i + 1)
                        dve.wait_ge(S["row_copied"], e * CHUNKS + c + 1)
                        dve.wait_ge(S["gelu"], e * HPE + i + 1)
                        dve.tensor_tensor(hid[:, c % 2, m], HP[i % 2][:], mrow[:, par, c * CH:(c + 1) * CH],
                                          ALU.mult).then_inc(S["scaled"], 1)

                def gather(e, c):
                    for w in range(2):
                        o = c * 2 + w
                        dve.wait_ge(S["product"], OB + e * OPE + o + 1)
                        dve.wait_ge(S["summed"], e * TILES + 8)
                        for j in (2 * w, 2 * w + 1):
                            t = c * CT + j
                            mine = mask[:, t, e:e + 1] if isinstance(e, int) else mask[:, t, bass.ds(e, 1)]
                            dve.scalar_tensor_tensor(x[:, t, :], OP[o % 4][:, j % 2], mine,
                                                     x[:, t, :], ALU.mult, ALU.add).then_inc(S["summed"], 1)

                def moments(c):
                    dve.wait_ge(S["summed"], (EXP - 1) * TILES + (c + 1) * CT + 8)
                    for t in range(c * CT, (c + 1) * CT):
                        dve.bn_stats(stats[:, t, :], x[:, t, :]).then_inc(S["done"], 1)
                    dve.wait_ge(S["done"], TILES // 2 + (c + 1) * CT)
                    for t in range(c * CT, (c + 1) * CT):
                        dve.bn_aggr(mv[:, t, :], stats[:, t, :]).then_inc(S["means"], 1)

                def normalise(c):
                    dve.wait_ge(S["rstd"], c + 1)
                    for t in range(c * CT, (c + 1) * CT):
                        dve.tensor_scalar(x[:, t, :], x[:, t, :], mv[:, t, 0:1], rstd[:, t:t + 1],
                                          ALU.subtract, ALU.mult).then_inc(S["normed"], 1)

                def expert(e, par, nxt):
                    for c in range(CHUNKS):
                        if c + 1 < CHUNKS:
                            scale(e, par, c + 1)
                        elif nxt is not None:
                            scale(nxt, 1 - par, 0)
                        gather(e, c)
                        if nxt is None:
                            moments(c)
                            if c:
                                normalise(c - 1)
                    if nxt is None:
                        normalise(CHUNKS - 1)
                experts(dve, lambda: scale(0, 0, 0), expert)

            @block.gpsimd
            def _(pool):
                pool.memset(half[:], -0.5).then_inc(S["variance"], 1)
                for c in range(CHUNKS):
                    at = slice(c * CT, (c + 1) * CT)
                    pool.wait_ge(S["means"], (c + 1) * CT)
                    pool.tensor_scalar(vare[:, at], mv[:, at, 1], EPS, 0.0, ALU.add, ALU.add).then_inc(S["variance"], 1)
                    pool.wait_ge(S["variance"], c + 2)
                    pool.tensor_tensor(rstd[:, at], vare[:, at], half[:], ALU.pow).then_inc(S["rstd"], 1)


def layout(I, np):
    ONE = 0x3F80
    g = lambda n: np.asarray(I[n])
    parts = lambda a, k: np.ascontiguousarray(a.reshape(k, P, -1).transpose(1, 0, 2))
    out = {}
    out["x"] = g("x").reshape(TILES, P, DM).transpose(1, 0, 2)
    out["ident"] = np.eye(P, dtype=np.float32)
    pick = np.zeros((3, 2 * DS, 2 * DS, P), np.uint16)
    for r in range(2 * DS):
        pick[:, r, r, :] = ONE
    out["pick"] = pick.reshape(96, 2 * DS, P)
    out["lnw"] = np.stack([g("L0_attn_ln_w"), g("L0_attn_ln_b")], 1).reshape(LAYERS, 2, KD, P).transpose(3, 0, 1, 2)
    cw = g("L0_attn_conv_w").transpose(0, 2, 1)
    ch = np.concatenate([g("L0_attn_conv_b")[:, None], g("L0_attn_dt_proj_b")[:, None], g("L0_attn_D_skip")[:, None], cw], 1)
    out["chan"] = ch.reshape(LAYERS, 3 + TAPS, M, P).transpose(3, 0, 1, 2)
    out["alog"] = g("L0_attn_A_log").reshape(LAYERS, M, P, DS).transpose(2, 0, 1, 3)
    out["inw"] = np.stack([parts(g("L0_attn_in_proj_w")[l].T, KD) for l in range(LAYERS)])
    xw = g("L0_attn_x_proj_w")
    xw = np.concatenate([xw[:, RANK:]] * 3 + [xw[:, :RANK]], 1)
    out["xpw"] = np.stack([parts(xw[l].T, M) for l in range(LAYERS)])
    out["dtw"] = g("L0_attn_dt_proj_w").transpose(0, 2, 1)
    out["outw"] = np.stack([parts(g("L0_attn_out_proj_w")[l].T, M) for l in range(LAYERS)])
    QH, KVH, HD = HEADS, KV, HDIM
    out["nf"] = np.concatenate([g("L0_attn_norm_f_w"), g("L0_attn_norm_f_b")])[None]
    out["xn_wb"] = np.concatenate([g("L0_xattn_gamma"), g("L0_xattn_beta")])[None]
    out["ctxT"] = g("ctx_1024").reshape(BATCH, SEQ, KD, P).transpose(0, 3, 2, 1)
    out["wq"] = parts(g("L0_xattn_Wq").T, KD)
    out["wkv"] = parts(np.concatenate([g("L0_xattn_Wk"), g("L0_xattn_Wv")]).T, KD)
    out["bqkv"] = np.concatenate([g("L0_xattn_bq"), g("L0_xattn_bk"), g("L0_xattn_bv")])[None]

    def rope(d, scale):
        theta = (1.0 / 10000.0 ** (np.arange(0, d, 2, dtype=np.float32) / np.float32(d))).astype(np.float32)
        a = np.arange(BATCH, dtype=np.float32)[:, None] * theta[None]
        a = np.concatenate([a, a], -1)[:, :, None]
        sign = np.where(np.arange(HD) < HD - d // 2, -1.0, 1.0).astype(np.float32)
        c = np.broadcast_to(np.cos(a) * np.float32(scale), (BATCH, d, HD))
        return [c.reshape(BATCH, -1), (np.sin(a) * np.float32(scale) * sign).reshape(BATCH, -1)]
    out["rope"] = np.concatenate(rope(QH, HD ** -0.5) + rope(KVH, 1.0), 1).astype(np.float32).reshape(1, -1)
    out["rw"] = parts(g("L0_ffn_router_w"), KD)
    out["rb"] = g("L0_ffn_router_b")[None]
    out["w1"] = g("L0_ffn_w1").reshape(EXP, KD, P, DM).transpose(0, 2, 1, 3)
    out["w2"] = g("L0_ffn_w2").reshape(EXP, KD, P, DM).transpose(0, 2, 1, 3)
    out["b1"] = g("L0_ffn_b1").reshape(EXP, KD, P).transpose(2, 1, 0)
    out["b2"] = g("L0_ffn_b2")
    pe = np.zeros((96, EXP, P), np.uint16)
    for e in range(EXP):
        pe[[e, 32 + e, 64 + e], e, :] = ONE
    out["picke"] = pe
    ph = np.zeros((3 * HEADS, HEADS, P), np.uint16)
    for h in range(HEADS):
        ph[[h, HEADS + h, 2 * HEADS + h], h, :] = ONE
    out["pickh"] = ph
    out["identb"] = np.where(np.eye(P) > 0, ONE, 0).astype(np.uint16)
    out["iota"] = np.arange(EXP, dtype=np.float32)[None]
    return {k: np.ascontiguousarray(v) for k, v in out.items()}


def kernel(**inputs):
    import numpy as np
    import concourse.bacc as bacc
    from concourse.bass_utils import run_bass_kernel_spmd as run

    nc = bacc.Bacc("TRN2", target_bir_lowering=False, num_devices=1)
    arrays, A = {}, {}
    for name, a in layout(inputs, np).items():
        arrays["in_" + name] = a
        A[name] = nc.dram_tensor("in_" + name, a.shape, mybir.dt.from_np(a.dtype), kind="ExternalInput").ap()
    A["out"] = nc.dram_tensor("out", (P, TILES, DM), mybir.dt.float32, kind="ExternalOutput").ap()
    build(nc, A)
    got = run(nc, [arrays], core_ids=[0]).results[0]["out"]
    return np.ascontiguousarray(got.transpose(1, 0, 2)).reshape(BATCH, SEQ, DM)
```
